# Optimizing a Trainium2 kernel written in Bass

```python
import numpy as np
import jax
import jax.numpy as jnp

def _softmax(x, axis=-1):
    return jax.nn.softmax(x, axis=axis)

def _gelu(x):
    return jax.nn.gelu(x, approximate=True)

def _silu(x):
    return jax.nn.silu(x)

def _sigmoid(x):
    return jax.nn.sigmoid(x)

def _layernorm(x, axis=-1, eps=1e-05):
    m = jnp.mean(x, axis=axis, keepdims=True)
    v = jnp.var(x, axis=axis, keepdims=True)
    return (x - m) / jnp.sqrt(v + eps)

def _scatter_add(tgt, idx, src, axis=0):
    return tgt.at[idx].add(src)

def _segment_sum(src, seg, n):
    return jax.ops.segment_sum(src, seg, n)
kernel_name = 'mk_adaln_d4_jaxref_r8_aadb22'

def setup_inputs(seed: int=0):
    np.random.seed(seed)
    _w = jnp.asarray

    def _L0_attn_setup():
        import jax, jax.numpy as jnp
        import numpy as np
        import math
        INPUT_WIDTH = 128
        KEY_WIDTH = 64
        VALUE_WIDTH = 64
        NUM_HEADS = 16
        key = jax.random.key(seed)
        k_x, k_q, k_k, k_v, k_p = jax.random.split(key, 5)
        n, s = (2, 256)
        scale = 1.0 / math.sqrt(INPUT_WIDTH)
        X = jax.random.normal(k_x, (n, s, INPUT_WIDTH), dtype=jnp.float32)
        Wq = jax.random.uniform(k_q, (INPUT_WIDTH, NUM_HEADS * KEY_WIDTH), jnp.float32, -scale, scale)
        Wk = jax.random.uniform(k_k, (INPUT_WIDTH, NUM_HEADS * KEY_WIDTH), jnp.float32, -scale, scale)
        Wv = jax.random.uniform(k_v, (INPUT_WIDTH, NUM_HEADS * VALUE_WIDTH), jnp.float32, -scale, scale)
        p_scale = 1.0 / math.sqrt(NUM_HEADS * VALUE_WIDTH)
        Wpost = jax.random.uniform(k_p, (NUM_HEADS * VALUE_WIDTH, INPUT_WIDTH), jnp.float32, -p_scale, p_scale)
        return {'X': X, 'Wq': Wq, 'Wk': Wk, 'Wv': Wv, 'Wpost': Wpost}
    _L0_attn_in = _L0_attn_setup()

    def _L0_ffn_setup():
        import jax, jax.numpy as jnp
        import numpy as np
        B, T, D, E, H, K = (4, 256, 128, 8, 256, 2)
        key = jax.random.key(seed)
        k0, k1, k2, k3 = jax.random.split(key, 4)
        x = jax.random.normal(k0, (B, T, D), dtype=jnp.float32)
        router_w = jax.random.normal(k1, (E, D), dtype=jnp.float32) * D ** (-0.5)
        w1 = jax.random.normal(k2, (E, D, H), dtype=jnp.float32) * D ** (-0.5)
        w2 = jax.random.normal(k3, (E, H, D), dtype=jnp.float32) * H ** (-0.5)
        return {'x': x, 'router_w': router_w, 'w1': w1, 'w2': w2}
    _L0_ffn_in = _L0_ffn_setup()
    _L0_c = _w((lambda *s: np.random.randn(*s).astype(np.float32) * 0.05)(4, 128))
    _L0_wmod = _w((lambda *s: np.random.randn(*s).astype(np.float32) * 0.05)(128, 6 * 128) * 128 ** (-0.5))

    def _L1_attn_setup():
        import jax, jax.numpy as jnp
        import numpy as np
        D_MODEL = 128
        N_HEADS = 16
        D_K = D_MODEL // N_HEADS
        THETA = 10000.0

        def _rope(x, pos):
            half = D_K // 2
            inv_freq = THETA ** (-jnp.arange(0, half, dtype=jnp.float32) * 2.0 / D_K)
            ang = pos[:, None].astype(jnp.float32) * inv_freq[None, :]
            cos, sin = (jnp.cos(ang), jnp.sin(ang))
            x1, x2 = (x[..., 0::2], x[..., 1::2])
            r1 = x1 * cos - x2 * sin
            r2 = x1 * sin + x2 * cos
            out = jnp.stack([r1, r2], axis=-1).reshape(x.shape)
            return out
        key = jax.random.key(seed)
        ks = jax.random.split(key, 5)
        b, s = (4, 256)
        sc = 1.0 / np.sqrt(D_MODEL)
        return {'x': jax.random.normal(ks[0], (b, s, D_MODEL), dtype=jnp.float32), 'Wq': jax.random.normal(ks[1], (D_MODEL, D_MODEL), dtype=jnp.float32) * sc, 'Wk': jax.random.normal(ks[2], (D_MODEL, D_MODEL), dtype=jnp.float32) * sc, 'Wv': jax.random.normal(ks[3], (D_MODEL, D_MODEL), dtype=jnp.float32) * sc, 'Wo': jax.random.normal(ks[4], (D_MODEL, D_MODEL), dtype=jnp.float32) * sc}
    _L1_attn_in = _L1_attn_setup()

    def _L1_ffn_setup():
        import jax, jax.numpy as jnp
        import numpy as np
        D = 128
        H = 128
        E = 8
        K = 2
        I = 2 * 128
        ROUTE_SCALE = 1.0
        key = jax.random.key(seed)
        ks = jax.random.split(key, 12)
        s = lambda *sh: 1.0 / np.sqrt(sh[-1])
        return {'x': jax.random.normal(ks[0], (1, 256, D), jnp.float32), 'gate_w': jax.random.normal(ks[1], (E, D), jnp.float32) * s(E, D), 'w1': jax.random.normal(ks[2], (E, H, D), jnp.float32) * s(H, D), 'b1': jax.random.normal(ks[3], (E, H), jnp.float32) * 0.01, 'w2': jax.random.normal(ks[4], (E, D, H), jnp.float32) * s(D, H), 'b2': jax.random.normal(ks[5], (E, D), jnp.float32) * 0.01, 'w3': jax.random.normal(ks[6], (E, H, D), jnp.float32) * s(H, D), 'b3': jax.random.normal(ks[7], (E, H), jnp.float32) * 0.01, 'sw1': jax.random.normal(ks[8], (I, D), jnp.float32) * s(I, D), 'sw2': jax.random.normal(ks[9], (I, D), jnp.float32) * s(I, D), 'sw3': jax.random.normal(ks[10], (D, I), jnp.float32) * s(D, I)}
    _L1_ffn_in = _L1_ffn_setup()
    _L1_c = _w((lambda *s: np.random.randn(*s).astype(np.float32) * 0.05)(4, 128))
    _L1_wmod = _w((lambda *s: np.random.randn(*s).astype(np.float32) * 0.05)(128, 6 * 128) * 128 ** (-0.5))

    def _L2_attn_setup():
        import jax, jax.numpy as jnp
        import numpy as np
        import math
        B, S, E = (2, 256, 128)
        H, DC, DR = (16, 32, 128)
        HD = E // H

        def _linear_params(key, din, dout):
            k1, k2 = jax.random.split(key)
            bound = 1.0 / math.sqrt(din)
            w = jax.random.uniform(k1, (din, dout), minval=-bound, maxval=bound, dtype=jnp.float32)
            b = jax.random.uniform(k2, (dout,), minval=-bound, maxval=bound, dtype=jnp.float32)
            return (w, b)

        def _gelu(x):
            return jax.nn.gelu(x, approximate=False)

        def _rope_cos_sin(seq_len, d_rope):
            inv_freq = 1.0 / 10000.0 ** (jnp.arange(0, d_rope, 2, dtype=jnp.float32) / d_rope)
            t = jnp.arange(seq_len, dtype=jnp.float32)
            freqs = t[:, None] * inv_freq[None, :]
            emb = jnp.concatenate([freqs, freqs], axis=-1)
            return (jnp.cos(emb), jnp.sin(emb))

        def _apply_rope(x, cos, sin):
            d = x.shape[-1]
            x1, x2 = (x[..., :d // 2], x[..., d // 2:])
            rot = jnp.concatenate([-x2, x1], axis=-1)
            return x * cos + rot * sin
        key = jax.random.key(seed)
        ks = jax.random.split(key, 10)
        x = jax.random.normal(ks[0], (B, S, E), dtype=jnp.float32)
        wq, bq = _linear_params(ks[1], E, DC)
        wqc, bqc = _linear_params(ks[2], DC, E - DR)
        wqr, bqr = _linear_params(ks[3], E, DR)
        wkv, bkv = _linear_params(ks[4], E, DC)
        wkr, bkr = _linear_params(ks[5], E, DR)
        wkc, bkc = _linear_params(ks[6], DC, E - DR)
        wv, bv = _linear_params(ks[7], DC, E)
        wo, bo = _linear_params(ks[8], E, E)
        return dict(x=x, wq=wq, bq=bq, wqc=wqc, bqc=bqc, wqr=wqr, bqr=bqr, wkv=wkv, bkv=bkv, wkr=wkr, bkr=bkr, wkc=wkc, bkc=bkc, wv=wv, bv=bv, wo=wo, bo=bo)
    _L2_attn_in = _L2_attn_setup()

    def _L2_ffn_setup():
        import jax, jax.numpy as jnp
        import numpy as np
        from jax.scipy.linalg import expm
        B, S, D, E, K, NROT = (2, 256, 128, 8, 2, 3)
        EPS = 1e-05

        def _gelu(x):
            return jax.nn.gelu(x, approximate=False)

        def _forward(x, ln_gamma, ln_beta, abel_w, abel_b, moe_gate_w, moe_gate_b, ew1, eb1, ew2, eb2, gens, gc_w, gc_b):
            residual = x
            mu = jnp.mean(x, axis=-1, keepdims=True)
            var = jnp.mean((x - mu) ** 2, axis=-1, keepdims=True)
            xn = (x - mu) * jax.lax.rsqrt(var + EPS) * ln_gamma + ln_beta
            abel_out = _gelu(xn @ abel_w + abel_b)
            logits = xn @ moe_gate_w + moe_gate_b
            topw, topi = jax.lax.top_k(logits, K)
            topw = jax.nn.softmax(topw, axis=-1)
            w_dense = jnp.sum(jax.nn.one_hot(topi, E, dtype=xn.dtype) * topw[..., None], axis=-2)
            h = _gelu(jnp.einsum('bsd,edh->ebsh', xn, ew1) + eb1[:, None, None, :])
            eo = jnp.einsum('ebsh,ehd->ebsd', h, ew2) + eb2[:, None, None, :]
            moe_out = jnp.einsum('ebsd,bse->bsd', eo, w_dense)
            for i in range(NROT):
                moe_out = moe_out @ expm(gens[i])
            combined = jnp.concatenate([abel_out, moe_out], axis=-1)
            gate = jax.nn.sigmoid(combined @ gc_w + gc_b)
            mixed = abel_out * (1.0 - gate) + moe_out * gate
            return residual + mixed
        key = jax.random.key(seed)
        ks = jax.random.split(key, 16)
        sc = 0.02
        x = jax.random.normal(ks[0], (B, S, D), jnp.float32)
        ln_gamma = 1.0 + sc * jax.random.normal(ks[1], (D,), jnp.float32)
        ln_beta = sc * jax.random.normal(ks[2], (D,), jnp.float32)
        abel_w = sc * jax.random.normal(ks[3], (D, D), jnp.float32)
        abel_b = sc * jax.random.normal(ks[4], (D,), jnp.float32)
        moe_gate_w = sc * jax.random.normal(ks[5], (D, E), jnp.float32)
        moe_gate_b = sc * jax.random.normal(ks[6], (E,), jnp.float32)
        ew1 = sc * jax.random.normal(ks[7], (E, D, 2 * D), jnp.float32)
        eb1 = sc * jax.random.normal(ks[8], (E, 2 * D), jnp.float32)
        ew2 = sc * jax.random.normal(ks[9], (E, 2 * D, D), jnp.float32)
        eb2 = sc * jax.random.normal(ks[10], (E, D), jnp.float32)
        g = sc * jax.random.normal(ks[11], (NROT, D, D), jnp.float32)
        gens = 0.5 * (g - jnp.swapaxes(g, -1, -2))
        gc_w = sc * jax.random.normal(ks[12], (2 * D, 1), jnp.float32)
        gc_b = sc * jax.random.normal(ks[13], (1,), jnp.float32)
        return dict(x=x, ln_gamma=ln_gamma, ln_beta=ln_beta, abel_w=abel_w, abel_b=abel_b, moe_gate_w=moe_gate_w, moe_gate_b=moe_gate_b, ew1=ew1, eb1=eb1, ew2=ew2, eb2=eb2, gens=gens, gc_w=gc_w, gc_b=gc_b)
    _L2_ffn_in = _L2_ffn_setup()
    _L2_c = _w((lambda *s: np.random.randn(*s).astype(np.float32) * 0.05)(4, 128))
    _L2_wmod = _w((lambda *s: np.random.randn(*s).astype(np.float32) * 0.05)(128, 6 * 128) * 128 ** (-0.5))

    def _L3_attn_setup():
        import jax, jax.numpy as jnp
        import numpy as np
        D_MODEL = 128
        NHEAD = 16

        def unitnorm(v):
            n = jnp.sqrt(jnp.sum(v * v, axis=-1, keepdims=True))
            return v / jnp.maximum(n, 1e-12)

        def _reference_tuple_inner(inp, Wq_w, Wq_b, Wk_w, Wk_b, Wv_w, Wv_b, Wo_w, Wo_b, Ww_w, Ww_b, Wr_w, Wr_b):
            src = inp
            S, B, d = inp.shape
            n = NHEAD
            k = (src @ Wk_w.T + Wk_b).reshape(S, B, n, -1)
            v = (src @ Wv_w.T + Wv_b).reshape(S, B, n, -1)
            q = (inp @ Wq_w.T + Wq_b).reshape(S, B, n, -1)
            k = unitnorm(k)
            q = unitnorm(q)
            w = jax.nn.sigmoid(src @ Ww_w.T + Ww_b)
            A = jnp.einsum('sbnq,sbnv->bnvq', k, v * w[:, :, :, None])
            r = jax.nn.sigmoid(inp @ Wr_w.T + Wr_b)
            out = jnp.einsum('sbnq,bnvq->sbnv', q, A) * r[:, :, :, None]
            out = out.reshape(S, B, d)
            out = out @ Wo_w.T + Wo_b
            return (out, A)
        key = jax.random.key(seed)
        ks = jax.random.split(key, 14)
        d = D_MODEL
        sc = 1.0 / np.sqrt(d)
        inp = jax.random.normal(ks[0], (256, 8, d), dtype=jnp.float32)

        def lin(kw, kb, out_dim):
            W = jax.random.uniform(kw, (out_dim, d), minval=-sc, maxval=sc, dtype=jnp.float32)
            b = jax.random.uniform(kb, (out_dim,), minval=-sc, maxval=sc, dtype=jnp.float32)
            return (W, b)
        Wq_w, Wq_b = lin(ks[1], ks[2], d)
        Wk_w, Wk_b = lin(ks[3], ks[4], d)
        Wv_w, Wv_b = lin(ks[5], ks[6], d)
        Wo_w, Wo_b = lin(ks[7], ks[8], d)
        Ww_w, Ww_b = lin(ks[9], ks[10], NHEAD)
        Wr_w, Wr_b = lin(ks[11], ks[12], NHEAD)
        return {'inp': inp, 'Wq_w': Wq_w, 'Wq_b': Wq_b, 'Wk_w': Wk_w, 'Wk_b': Wk_b, 'Wv_w': Wv_w, 'Wv_b': Wv_b, 'Wo_w': Wo_w, 'Wo_b': Wo_b, 'Ww_w': Ww_w, 'Ww_b': Ww_b, 'Wr_w': Wr_w, 'Wr_b': Wr_b}
    _L3_attn_in = _L3_attn_setup()

    def _L3_ffn_setup():
        import jax, jax.numpy as jnp
        import numpy as np
        B, S, D, H, E = (4, 256, 128, 512, 8)
        key = jax.random.key(seed)
        ks = jax.random.split(key, 8)
        s_d = 1.0 / np.sqrt(D)
        s_h = 1.0 / np.sqrt(H)
        return {'x': jax.random.normal(ks[0], (B, S, D), dtype=jnp.float32), 'gate_w': jax.random.uniform(ks[1], (E, D), jnp.float32, -s_d, s_d), 'gate_b': jax.random.uniform(ks[2], (E,), jnp.float32, -s_d, s_d), 'w1': jax.random.uniform(ks[3], (E, H, D), jnp.float32, -s_d, s_d), 'b1': jax.random.uniform(ks[4], (E, H), jnp.float32, -s_d, s_d), 'w2': jax.random.uniform(ks[5], (E, D, H), jnp.float32, -s_h, s_h), 'b2': jax.random.uniform(ks[6], (E, D), jnp.float32, -s_h, s_h)}
    _L3_ffn_in = _L3_ffn_setup()
    _L3_c = _w((lambda *s: np.random.randn(*s).astype(np.float32) * 0.05)(4, 128))
    _L3_wmod = _w((lambda *s: np.random.randn(*s).astype(np.float32) * 0.05)(128, 6 * 128) * 128 ** (-0.5))
    _d = {'L0_attn_X': _L0_attn_in['X'], 'L0_attn_Wq': _L0_attn_in['Wq'], 'L0_attn_Wk': _L0_attn_in['Wk'], 'L0_attn_Wv': _L0_attn_in['Wv'], 'L0_attn_Wpost': _L0_attn_in['Wpost'], 'L0_ffn_router_w': _L0_ffn_in['router_w'], 'L0_ffn_w1': _L0_ffn_in['w1'], 'L0_ffn_w2': _L0_ffn_in['w2'], 'L0_c': _L0_c, 'L0_wmod': _L0_wmod, 'L1_attn_Wq': _L1_attn_in['Wq'], 'L1_attn_Wk': _L1_attn_in['Wk'], 'L1_attn_Wv': _L1_attn_in['Wv'], 'L1_attn_Wo': _L1_attn_in['Wo'], 'L1_ffn_gate_w': _L1_ffn_in['gate_w'], 'L1_ffn_w1': _L1_ffn_in['w1'], 'L1_ffn_b1': _L1_ffn_in['b1'], 'L1_ffn_w2': _L1_ffn_in['w2'], 'L1_ffn_b2': _L1_ffn_in['b2'], 'L1_ffn_w3': _L1_ffn_in['w3'], 'L1_ffn_b3': _L1_ffn_in['b3'], 'L1_ffn_sw1': _L1_ffn_in['sw1'], 'L1_ffn_sw2': _L1_ffn_in['sw2'], 'L1_ffn_sw3': _L1_ffn_in['sw3'], 'L1_c': _L1_c, 'L1_wmod': _L1_wmod, 'L2_attn_wq': _L2_attn_in['wq'], 'L2_attn_bq': _L2_attn_in['bq'], 'L2_attn_wqc': _L2_attn_in['wqc'], 'L2_attn_bqc': _L2_attn_in['bqc'], 'L2_attn_wqr': _L2_attn_in['wqr'], 'L2_attn_bqr': _L2_attn_in['bqr'], 'L2_attn_wkv': _L2_attn_in['wkv'], 'L2_attn_bkv': _L2_attn_in['bkv'], 'L2_attn_wkr': _L2_attn_in['wkr'], 'L2_attn_bkr': _L2_attn_in['bkr'], 'L2_attn_wkc': _L2_attn_in['wkc'], 'L2_attn_bkc': _L2_attn_in['bkc'], 'L2_attn_wv': _L2_attn_in['wv'], 'L2_attn_bv': _L2_attn_in['bv'], 'L2_attn_wo': _L2_attn_in['wo'], 'L2_attn_bo': _L2_attn_in['bo'], 'L2_ffn_ln_gamma': _L2_ffn_in['ln_gamma'], 'L2_ffn_ln_beta': _L2_ffn_in['ln_beta'], 'L2_ffn_abel_w': _L2_ffn_in['abel_w'], 'L2_ffn_abel_b': _L2_ffn_in['abel_b'], 'L2_ffn_moe_gate_w': _L2_ffn_in['moe_gate_w'], 'L2_ffn_moe_gate_b': _L2_ffn_in['moe_gate_b'], 'L2_ffn_ew1': _L2_ffn_in['ew1'], 'L2_ffn_eb1': _L2_ffn_in['eb1'], 'L2_ffn_ew2': _L2_ffn_in['ew2'], 'L2_ffn_eb2': _L2_ffn_in['eb2'], 'L2_ffn_gens': _L2_ffn_in['gens'], 'L2_ffn_gc_w': _L2_ffn_in['gc_w'], 'L2_ffn_gc_b': _L2_ffn_in['gc_b'], 'L2_c': _L2_c, 'L2_wmod': _L2_wmod, 'L3_attn_Wq_w': _L3_attn_in['Wq_w'], 'L3_attn_Wq_b': _L3_attn_in['Wq_b'], 'L3_attn_Wk_w': _L3_attn_in['Wk_w'], 'L3_attn_Wk_b': _L3_attn_in['Wk_b'], 'L3_attn_Wv_w': _L3_attn_in['Wv_w'], 'L3_attn_Wv_b': _L3_attn_in['Wv_b'], 'L3_attn_Wo_w': _L3_attn_in['Wo_w'], 'L3_attn_Wo_b': _L3_attn_in['Wo_b'], 'L3_attn_Ww_w': _L3_attn_in['Ww_w'], 'L3_attn_Ww_b': _L3_attn_in['Ww_b'], 'L3_attn_Wr_w': _L3_attn_in['Wr_w'], 'L3_attn_Wr_b': _L3_attn_in['Wr_b'], 'L3_ffn_gate_w': _L3_ffn_in['gate_w'], 'L3_ffn_gate_b': _L3_ffn_in['gate_b'], 'L3_ffn_w1': _L3_ffn_in['w1'], 'L3_ffn_b1': _L3_ffn_in['b1'], 'L3_ffn_w2': _L3_ffn_in['w2'], 'L3_ffn_b2': _L3_ffn_in['b2'], 'L3_c': _L3_c, 'L3_wmod': _L3_wmod}
    _x0 = _d['L0_attn_X']
    _d['L0_attn_X'] = jax.random.normal(jax.random.fold_in(jax.random.key(seed), 1), (4, 1024, 128), dtype=_x0.dtype)
    del _x0
    return _d

def reference(L0_attn_X, L0_attn_Wq, L0_attn_Wk, L0_attn_Wv, L0_attn_Wpost, L0_ffn_router_w, L0_ffn_w1, L0_ffn_w2, L0_c, L0_wmod, L1_attn_Wq, L1_attn_Wk, L1_attn_Wv, L1_attn_Wo, L1_ffn_gate_w, L1_ffn_w1, L1_ffn_b1, L1_ffn_w2, L1_ffn_b2, L1_ffn_w3, L1_ffn_b3, L1_ffn_sw1, L1_ffn_sw2, L1_ffn_sw3, L1_c, L1_wmod, L2_attn_wq, L2_attn_bq, L2_attn_wqc, L2_attn_bqc, L2_attn_wqr, L2_attn_bqr, L2_attn_wkv, L2_attn_bkv, L2_attn_wkr, L2_attn_bkr, L2_attn_wkc, L2_attn_bkc, L2_attn_wv, L2_attn_bv, L2_attn_wo, L2_attn_bo, L2_ffn_ln_gamma, L2_ffn_ln_beta, L2_ffn_abel_w, L2_ffn_abel_b, L2_ffn_moe_gate_w, L2_ffn_moe_gate_b, L2_ffn_ew1, L2_ffn_eb1, L2_ffn_ew2, L2_ffn_eb2, L2_ffn_gens, L2_ffn_gc_w, L2_ffn_gc_b, L2_c, L2_wmod, L3_attn_Wq_w, L3_attn_Wq_b, L3_attn_Wk_w, L3_attn_Wk_b, L3_attn_Wv_w, L3_attn_Wv_b, L3_attn_Wo_w, L3_attn_Wo_b, L3_attn_Ww_w, L3_attn_Ww_b, L3_attn_Wr_w, L3_attn_Wr_b, L3_ffn_gate_w, L3_ffn_gate_b, L3_ffn_w1, L3_ffn_b1, L3_ffn_w2, L3_ffn_b2, L3_c, L3_wmod):

    def _L0_attn_ref(X, Wq, Wk, Wv, Wpost):
        import jax, jax.numpy as jnp
        import numpy as np
        import math
        INPUT_WIDTH = 128
        KEY_WIDTH = 64
        VALUE_WIDTH = 64
        NUM_HEADS = 16
        n, s, _ = X.shape
        Q = (X @ Wq).reshape(n, s, NUM_HEADS, KEY_WIDTH)
        K = (X @ Wk).reshape(n, s, NUM_HEADS, KEY_WIDTH)
        V = (X @ Wv).reshape(n, s, NUM_HEADS, VALUE_WIDTH)
        inv_sqrt_d = 1.0 / math.sqrt(KEY_WIDTH)
        raw_attn = jnp.einsum('bshe,bthe->bsth', Q, K * inv_sqrt_d)
        attn = jax.nn.softmax(raw_attn, axis=2)
        A = jnp.einsum('bsth,bthe->bshe', attn, V).reshape(n, s, NUM_HEADS * VALUE_WIDTH)
        A = jax.nn.gelu(A, approximate=False)
        P = A @ Wpost
        return X + P

    def _L0_ffn_ref(x, router_w, w1, w2):
        import jax, jax.numpy as jnp
        import numpy as np
        B, T, D, E, H, K = (4, 256, 128, 8, 256, 2)
        Bb, Tt, Dd = x.shape
        N = Bb * Tt
        logits = jnp.einsum('btd,ed->bte', x, router_w)
        top_vals, top_idx = jax.lax.top_k(logits, K)
        top_w = jax.nn.softmax(top_vals, axis=-1)
        xf = x.reshape(N, Dd)
        h = jnp.einsum('nd,edh->enh', xf, w1)
        h = jnp.square(jax.nn.relu(h))
        y = jnp.einsum('enh,ehd->end', h, w2)
        idx_f = top_idx.reshape(N, K)
        w_f = top_w.reshape(N, K)
        y_sel = y[idx_f, jnp.arange(N)[:, None]]
        out = jnp.einsum('nk,nkd->nd', w_f, y_sel)
        return out.reshape(Bb, Tt, Dd)

    def _L1_attn_ref(x, Wq, Wk, Wv, Wo):
        import jax, jax.numpy as jnp
        import numpy as np
        D_MODEL = 128
        N_HEADS = 16
        D_K = D_MODEL // N_HEADS
        THETA = 10000.0

        def _rope(x, pos):
            half = D_K // 2
            inv_freq = THETA ** (-jnp.arange(0, half, dtype=jnp.float32) * 2.0 / D_K)
            ang = pos[:, None].astype(jnp.float32) * inv_freq[None, :]
            cos, sin = (jnp.cos(ang), jnp.sin(ang))
            x1, x2 = (x[..., 0::2], x[..., 1::2])
            r1 = x1 * cos - x2 * sin
            r2 = x1 * sin + x2 * cos
            out = jnp.stack([r1, r2], axis=-1).reshape(x.shape)
            return out
        b, s, _ = x.shape
        pos = jnp.arange(s)

        def split_heads(t):
            return t.reshape(b, s, N_HEADS, D_K).transpose(0, 2, 1, 3).reshape(b * N_HEADS, s, D_K)
        q = split_heads(x @ Wq.T)
        k = split_heads(x @ Wk.T)
        v = split_heads(x @ Wv.T)
        q = _rope(q, pos)
        k = _rope(k, pos)
        score = jnp.einsum('bqd,bkd->bqk', q, k)
        causal = jnp.tril(jnp.ones((s, s), dtype=bool))
        score = jnp.where(causal[None], score, -jnp.inf)
        attn = jax.nn.softmax(score / jnp.sqrt(jnp.float32(D_K)), axis=-1)
        out = jnp.einsum('bqk,bkd->bqd', attn, v)
        out = out.reshape(b, N_HEADS, s, D_K).transpose(0, 2, 1, 3).reshape(b, s, D_MODEL)
        return out @ Wo.T

    def _L1_ffn_ref(x, gate_w, w1, b1, w2, b2, w3, b3, sw1, sw2, sw3):
        import jax, jax.numpy as jnp
        import numpy as np
        D = 128
        H = 128
        E = 8
        K = 2
        I = 2 * 128
        ROUTE_SCALE = 1.0
        B, S, _ = x.shape
        xt = x.reshape(-1, D)
        logits = xt @ gate_w.T
        scores = jax.nn.softmax(logits.astype(jnp.float32), axis=-1)
        top_vals, idx = jax.lax.top_k(scores, K)
        weights = jnp.take_along_axis(scores, idx, axis=1).astype(x.dtype) * ROUTE_SCALE
        xs = xt[:, None, :] * weights[:, :, None]
        y = jnp.zeros_like(xt)
        for e in range(E):
            mask = (idx == e).astype(x.dtype)
            h = jax.nn.silu(jnp.einsum('tkd,hd->tkh', xs, w1[e]) + b1[e])
            x2 = jnp.einsum('tkh,dh->tkd', h, w2[e]) + b2[e]
            x3 = jnp.einsum('tkd,hd->tkh', xs, w3[e]) + b3[e]
            y = y + jnp.sum(x2 * x3 * mask[:, :, None], axis=1)
        z = jax.nn.silu(xt @ sw1.T) * (xt @ sw2.T) @ sw3.T
        return (y + z).reshape(B, S, D)

    def _L2_attn_ref(x, wq, bq, wqc, bqc, wqr, bqr, wkv, bkv, wkr, bkr, wkc, bkc, wv, bv, wo, bo):
        import jax, jax.numpy as jnp
        import numpy as np
        import math
        B, S, E = (2, 256, 128)
        H, DC, DR = (16, 32, 128)
        HD = E // H

        def _linear_params(key, din, dout):
            k1, k2 = jax.random.split(key)
            bound = 1.0 / math.sqrt(din)
            w = jax.random.uniform(k1, (din, dout), minval=-bound, maxval=bound, dtype=jnp.float32)
            b = jax.random.uniform(k2, (dout,), minval=-bound, maxval=bound, dtype=jnp.float32)
            return (w, b)

        def _gelu(x):
            return jax.nn.gelu(x, approximate=False)

        def _rope_cos_sin(seq_len, d_rope):
            inv_freq = 1.0 / 10000.0 ** (jnp.arange(0, d_rope, 2, dtype=jnp.float32) / d_rope)
            t = jnp.arange(seq_len, dtype=jnp.float32)
            freqs = t[:, None] * inv_freq[None, :]
            emb = jnp.concatenate([freqs, freqs], axis=-1)
            return (jnp.cos(emb), jnp.sin(emb))

        def _apply_rope(x, cos, sin):
            d = x.shape[-1]
            x1, x2 = (x[..., :d // 2], x[..., d // 2:])
            rot = jnp.concatenate([-x2, x1], axis=-1)
            return x * cos + rot * sin
        b, s, _ = x.shape
        cq = _gelu(x @ wq + bq)
        q_c = cq @ wqc + bqc
        q_r = x @ wqr + bqr
        ckv = _gelu(x @ wkv + bkv)
        k_r = x @ wkr + bkr
        k_c = ckv @ wkc + bkc
        v = (ckv @ wv + bv).reshape(b, s, H, HD).transpose(0, 2, 1, 3)
        cos, sin = _rope_cos_sin(s, DR)
        q_r = _apply_rope(q_r, cos, sin)
        k_r = _apply_rope(k_r, cos, sin)
        q = _gelu(jnp.concatenate([q_c, q_r], axis=-1)).reshape(b, s, H, HD).transpose(0, 2, 1, 3)
        k = _gelu(jnp.concatenate([k_c, k_r], axis=-1)).reshape(b, s, H, HD).transpose(0, 2, 1, 3)
        scale = 1.0 / math.sqrt(HD)
        scores = jnp.einsum('bhqd,bhkd->bhqk', q, k) * scale
        causal = jnp.triu(jnp.ones((s, s), dtype=bool), k=1)
        scores = jnp.where(causal[None, None], -jnp.inf, scores)
        attn = jax.nn.softmax(scores, axis=-1)
        out = jnp.einsum('bhqk,bhkd->bhqd', attn, v)
        out = out.transpose(0, 2, 1, 3).reshape(b, s, E)
        return out @ wo + bo

    def _L2_ffn_ref(x, ln_gamma, ln_beta, abel_w, abel_b, moe_gate_w, moe_gate_b, ew1, eb1, ew2, eb2, gens, gc_w, gc_b):
        import jax, jax.numpy as jnp
        import numpy as np
        from jax.scipy.linalg import expm
        B, S, D, E, K, NROT = (2, 256, 128, 8, 2, 3)
        EPS = 1e-05

        def _gelu(x):
            return jax.nn.gelu(x, approximate=False)

        def _forward(x, ln_gamma, ln_beta, abel_w, abel_b, moe_gate_w, moe_gate_b, ew1, eb1, ew2, eb2, gens, gc_w, gc_b):
            residual = x
            mu = jnp.mean(x, axis=-1, keepdims=True)
            var = jnp.mean((x - mu) ** 2, axis=-1, keepdims=True)
            xn = (x - mu) * jax.lax.rsqrt(var + EPS) * ln_gamma + ln_beta
            abel_out = _gelu(xn @ abel_w + abel_b)
            logits = xn @ moe_gate_w + moe_gate_b
            topw, topi = jax.lax.top_k(logits, K)
            topw = jax.nn.softmax(topw, axis=-1)
            w_dense = jnp.sum(jax.nn.one_hot(topi, E, dtype=xn.dtype) * topw[..., None], axis=-2)
            h = _gelu(jnp.einsum('bsd,edh->ebsh', xn, ew1) + eb1[:, None, None, :])
            eo = jnp.einsum('ebsh,ehd->ebsd', h, ew2) + eb2[:, None, None, :]
            moe_out = jnp.einsum('ebsd,bse->bsd', eo, w_dense)
            for i in range(NROT):
                moe_out = moe_out @ expm(gens[i])
            combined = jnp.concatenate([abel_out, moe_out], axis=-1)
            gate = jax.nn.sigmoid(combined @ gc_w + gc_b)
            mixed = abel_out * (1.0 - gate) + moe_out * gate
            return residual + mixed
        return _forward(x, ln_gamma, ln_beta, abel_w, abel_b, moe_gate_w, moe_gate_b, ew1, eb1, ew2, eb2, gens, gc_w, gc_b)

    def _L3_attn_ref(inp, Wq_w, Wq_b, Wk_w, Wk_b, Wv_w, Wv_b, Wo_w, Wo_b, Ww_w, Ww_b, Wr_w, Wr_b):
        import jax, jax.numpy as jnp
        import numpy as np
        D_MODEL = 128
        NHEAD = 16

        def unitnorm(v):
            n = jnp.sqrt(jnp.sum(v * v, axis=-1, keepdims=True))
            return v / jnp.maximum(n, 1e-12)

        def _reference_tuple_inner(inp, Wq_w, Wq_b, Wk_w, Wk_b, Wv_w, Wv_b, Wo_w, Wo_b, Ww_w, Ww_b, Wr_w, Wr_b):
            src = inp
            S, B, d = inp.shape
            n = NHEAD
            k = (src @ Wk_w.T + Wk_b).reshape(S, B, n, -1)
            v = (src @ Wv_w.T + Wv_b).reshape(S, B, n, -1)
            q = (inp @ Wq_w.T + Wq_b).reshape(S, B, n, -1)
            k = unitnorm(k)
            q = unitnorm(q)
            w = jax.nn.sigmoid(src @ Ww_w.T + Ww_b)
            A = jnp.einsum('sbnq,sbnv->bnvq', k, v * w[:, :, :, None])
            r = jax.nn.sigmoid(inp @ Wr_w.T + Wr_b)
            out = jnp.einsum('sbnq,bnvq->sbnv', q, A) * r[:, :, :, None]
            out = out.reshape(S, B, d)
            out = out @ Wo_w.T + Wo_b
            return (out, A)
        return _reference_tuple_inner(inp, Wq_w, Wq_b, Wk_w, Wk_b, Wv_w, Wv_b, Wo_w, Wo_b, Ww_w, Ww_b, Wr_w, Wr_b)[0]

    def _L3_ffn_ref(x, gate_w, gate_b, w1, b1, w2, b2):
        import jax, jax.numpy as jnp
        import numpy as np
        B, S, D, H, E = (4, 256, 128, 512, 8)
        b, s, d = x.shape
        xf = x.reshape(-1, d)
        logits = xf @ gate_w.T + gate_b
        top1 = jnp.argmax(logits, axis=-1)
        out = jnp.zeros_like(xf)
        n_experts = w1.shape[0]
        for e in range(n_experts):
            h = jax.nn.relu(xf @ w1[e].T + b1[e])
            y = h @ w2[e].T + b2[e]
            out = out + jnp.where((top1 == e)[:, None], y, jnp.zeros((), y.dtype))
        return out.reshape(b, s, d)
    x = L0_attn_X
    mod = (_silu(L0_c) @ L0_wmod).reshape(L0_c.shape[0], 6, 1, -1)
    sa, ca, ga, sb, cb, gb = (mod[:, 0], mod[:, 1], mod[:, 2], mod[:, 3], mod[:, 4], mod[:, 5])
    ga = (2 * (ga >= 0) - 1) * jnp.maximum(jnp.abs(ga), 0.25)
    gb = (2 * (gb >= 0) - 1) * jnp.maximum(jnp.abs(gb), 0.25)
    h = _layernorm(x, axis=-1) * (1 + ca) + sa
    x = x + ga * _L0_attn_ref(h, L0_attn_Wq, L0_attn_Wk, L0_attn_Wv, L0_attn_Wpost)
    h = _layernorm(x, axis=-1) * (1 + cb) + sb
    x = x + gb * _L0_ffn_ref(h, L0_ffn_router_w, L0_ffn_w1, L0_ffn_w2)
    mod = (_silu(L1_c) @ L1_wmod).reshape(L1_c.shape[0], 6, 1, -1)
    sa, ca, ga, sb, cb, gb = (mod[:, 0], mod[:, 1], mod[:, 2], mod[:, 3], mod[:, 4], mod[:, 5])
    ga = (2 * (ga >= 0) - 1) * jnp.maximum(jnp.abs(ga), 0.25)
    gb = (2 * (gb >= 0) - 1) * jnp.maximum(jnp.abs(gb), 0.25)
    h = _layernorm(x, axis=-1) * (1 + ca) + sa
    x = x + ga * _L1_attn_ref(h, L1_attn_Wq, L1_attn_Wk, L1_attn_Wv, L1_attn_Wo)
    h = _layernorm(x, axis=-1) * (1 + cb) + sb
    x = x + gb * _L1_ffn_ref(h, L1_ffn_gate_w, L1_ffn_w1, L1_ffn_b1, L1_ffn_w2, L1_ffn_b2, L1_ffn_w3, L1_ffn_b3, L1_ffn_sw1, L1_ffn_sw2, L1_ffn_sw3)
    mod = (_silu(L2_c) @ L2_wmod).reshape(L2_c.shape[0], 6, 1, -1)
    sa, ca, ga, sb, cb, gb = (mod[:, 0], mod[:, 1], mod[:, 2], mod[:, 3], mod[:, 4], mod[:, 5])
    ga = (2 * (ga >= 0) - 1) * jnp.maximum(jnp.abs(ga), 0.25)
    gb = (2 * (gb >= 0) - 1) * jnp.maximum(jnp.abs(gb), 0.25)
    h = _layernorm(x, axis=-1) * (1 + ca) + sa
    x = x + ga * _L2_attn_ref(h, L2_attn_wq, L2_attn_bq, L2_attn_wqc, L2_attn_bqc, L2_attn_wqr, L2_attn_bqr, L2_attn_wkv, L2_attn_bkv, L2_attn_wkr, L2_attn_bkr, L2_attn_wkc, L2_attn_bkc, L2_attn_wv, L2_attn_bv, L2_attn_wo, L2_attn_bo)
    h = _layernorm(x, axis=-1) * (1 + cb) + sb
    x = x + gb * _L2_ffn_ref(h, L2_ffn_ln_gamma, L2_ffn_ln_beta, L2_ffn_abel_w, L2_ffn_abel_b, L2_ffn_moe_gate_w, L2_ffn_moe_gate_b, L2_ffn_ew1, L2_ffn_eb1, L2_ffn_ew2, L2_ffn_eb2, L2_ffn_gens, L2_ffn_gc_w, L2_ffn_gc_b)
    mod = (_silu(L3_c) @ L3_wmod).reshape(L3_c.shape[0], 6, 1, -1)
    sa, ca, ga, sb, cb, gb = (mod[:, 0], mod[:, 1], mod[:, 2], mod[:, 3], mod[:, 4], mod[:, 5])
    ga = (2 * (ga >= 0) - 1) * jnp.maximum(jnp.abs(ga), 0.25)
    gb = (2 * (gb >= 0) - 1) * jnp.maximum(jnp.abs(gb), 0.25)
    h = _layernorm(x, axis=-1) * (1 + ca) + sa
    x = x + ga * _L3_attn_ref(h, L3_attn_Wq_w, L3_attn_Wq_b, L3_attn_Wk_w, L3_attn_Wk_b, L3_attn_Wv_w, L3_attn_Wv_b, L3_attn_Wo_w, L3_attn_Wo_b, L3_attn_Ww_w, L3_attn_Ww_b, L3_attn_Wr_w, L3_attn_Wr_b)
    h = _layernorm(x, axis=-1) * (1 + cb) + sb
    x = x + gb * _L3_ffn_ref(h, L3_ffn_gate_w, L3_ffn_gate_b, L3_ffn_w1, L3_ffn_b1, L3_ffn_w2, L3_ffn_b2)
    return x

_drawn_inputs = setup_inputs


def setup_inputs(seed=0):
    import zlib

    import numpy as np

    out = dict(_drawn_inputs(seed))
    spreads = {}
    factors = {'L0_attn_Wq': 8.0,
     'L0_attn_Wk': 8.0,
     'L0_attn_Wv': 8.0,
     'L0_attn_Wpost': 8.0,
     'L1_ffn_b1': 56.16,
     'L1_ffn_b2': 24.432,
     'L1_ffn_b3': 38.785,
     'L2_attn_wqr': 8.0,
     'L2_attn_bqr': 8.0,
     'L2_attn_wkv': 8.0,
     'L2_attn_bkv': 8.0,
     'L2_attn_wkr': 8.0,
     'L2_attn_bkr': 8.0,
     'L2_attn_wv': 5.197,
     'L2_attn_bv': 3.144,
     'L2_attn_bo': 4.184,
     'L2_ffn_ln_gamma': 8.0,
     'L2_ffn_ln_beta': 8.0,
     'L2_ffn_abel_w': 3.748,
     'L2_ffn_abel_b': 46.411,
     'L2_ffn_moe_gate_w': 8.0,
     'L2_ffn_moe_gate_b': 8.0,
     'L2_ffn_ew1': 8.0,
     'L2_ffn_eb1': 8.0,
     'L2_ffn_ew2': 8.0,
     'L2_ffn_eb2': 64.0,
     'L2_ffn_gens': 8.0,
     'L2_ffn_gc_w': 8.0,
     'L3_attn_Wq_w': 3.405,
     'L3_attn_Wq_b': 40.487,
     'L3_attn_Wk_w': 3.502,
     'L3_attn_Wk_b': 40.942,
     'L3_attn_Wv_w': 3.512,
     'L3_attn_Wv_b': 43.347,
     'L3_attn_Wo_w': 3.428,
     'L3_attn_Wo_b': 24.177,
     'L3_attn_Ww_w': 8.0,
     'L3_attn_Ww_b': 64.0,
     'L3_attn_Wr_w': 8.0,
     'L3_attn_Wr_b': 64.0,
     'L3_ffn_gate_b': 20.837,
     'L3_ffn_b1': 64.0,
     'L3_ffn_b2': 50.543,
     'L3_ffn_gate_w': 3.945,
     'L3_ffn_w1': 6.448,
     'L3_ffn_w2': 4.484}
    for name, (base, spread) in spreads.items():
        noise = np.random.default_rng([zlib.crc32(name.encode()), seed]).standard_normal(out[name].shape)
        drawn = base * np.exp(spread * noise) if base else spread * noise
        out[name] = jnp.asarray(drawn.astype(out[name].dtype))
    for name, factor in factors.items():
        out[name] = (out[name] * factor).astype(out[name].dtype)
    return out
```

```python
from contextlib import ExitStack

import concourse.bass as bass
from concourse import mybir

F32 = mybir.dt.float32
F32R = mybir.dt.float32r
BF16 = mybir.dt.bfloat16
I32 = mybir.dt.int32
U32 = mybir.dt.uint32
ALU = mybir.AluOpType
ACT = mybir.ActivationFunctionType
AX = mybir.AxisListType.X

P = 128
BATCH = 4
SEQ = 1024
TILES = SEQ // P
NT = BATCH * TILES
TOK = BATCH * SEQ
LAYERS = 4
CH = 512
NCH = TOK // CH
EXPERTS = 8
EPS = 1e-5
SHIFT_A, SCALE_A, GATE_A, SHIFT_B, SCALE_B, GATE_B = range(6)


class Memory:
    pass


def bcast(ap, n):
    return ap.unsqueeze(2).broadcast_to((*ap.shape, n))


def load_and_modulation(nc, t, sem, d):
    s_c = sem("mod_inputs_loaded")
    s_silu = sem("mod_silu_ready")
    s_mm = sem("mod_products_ready")
    s_v = sem("mod_vector_steps")
    s_once = sem("resident_loaded")
    with ExitStack() as ctx:
        cT = ctx.enter_context(nc.sbuf_tensor("cT", [P, LAYERS * BATCH], F32))
        cs = ctx.enter_context(nc.sbuf_tensor("c_silu", [P, LAYERS * BATCH], F32))
        wmod = ctx.enter_context(nc.sbuf_tensor("wmod_all", [P, LAYERS, 6 * P], F32))
        sign = ctx.enter_context(nc.sbuf_tensor("gate_sign", [P, LAYERS, 2, BATCH], F32))
        size = ctx.enter_context(nc.sbuf_tensor("gate_size", [P, LAYERS, 2, BATCH], F32))
        mod_ps = t.PS[:, 0, 0:LAYERS * 6 * BATCH]
        gates = t.MOD[:, :, GATE_A:GATE_B + 1:3, :]
        scales = t.MOD[:, :, SCALE_A:SCALE_B + 1:3, :]
        with nc.Block() as block:
            @block.sync
            def _(sp):
                sp.dma_start(cT[:], d["c_T"]).then_inc(s_c, 16)
                for l in range(LAYERS):
                    sp.dma_start(wmod[:, l, :], d[f"L{l}_wmod"]).then_inc(s_c, 16)
                for b in range(BATCH):
                    sp.dma_start(t.X[:, b * TILES:(b + 1) * TILES, :],
                                 d["L0_attn_X"][b].rearrange("(i p) f -> p i f", p=P)).then_inc(s_once, 16)
                sp.dma_start(t.ident[:], d["ident"]).then_inc(s_once, 16)
                sp.wait_ge(s_once, 16 * (BATCH + 1))

            @block.scalar
            def _(act):
                act.wait_ge(s_c, 16 * (1 + LAYERS))
                act.activation(cs[:], cT[:], ACT.Silu).then_inc(s_silu, 1)

            @block.tensor
            def _(pe):
                pe.wait_ge(s_c, 16 * (1 + LAYERS))
                pe.wait_ge(s_silu, 1)
                for l in range(LAYERS):
                    for j in range(6):
                        mm = pe.matmul(mod_ps[:, (l * 6 + j) * BATCH:(l * 6 + j + 1) * BATCH],
                                       wmod[:, l, j * P:(j + 1) * P], cs[:, l * BATCH:(l + 1) * BATCH],
                                       start=True, stop=True)
                mm.then_inc(s_mm, 1)

            @block.vector
            def _(dve):
                dve.wait_ge(s_mm, 1)
                dve.tensor_copy(t.MOD[:], mod_ps.rearrange("p (l j b) -> p l j b", l=LAYERS, j=6)).then_inc(s_v, 1)
                dve.wait_ge(s_v, 1)
                dve.tensor_scalar(scales, scales, 1.0, None, ALU.add).then_inc(s_v, 1)
                dve.tensor_scalar(sign[:], gates, 0.0, 2.0, ALU.is_ge, ALU.mult).then_inc(s_v, 1)
                dve.scalar_tensor_tensor(size[:], gates, -1.0, gates, ALU.mult, ALU.max).then_inc(s_v, 1)
                dve.wait_ge(s_v, 4)
                dve.tensor_scalar(sign[:], sign[:], -1.0, None, ALU.add).then_inc(s_v, 1)
                dve.wait_ge(s_v, 5)
                dve.scalar_tensor_tensor(gates, size[:], 0.25, sign[:], ALU.max, ALU.mult).then_inc(s_v, 1)
                dve.wait_ge(s_v, 6)


def residual(nc, t, sem, name, store=None):
    s_tr = sem(f"{name}_res_transposed")
    s_add = sem(f"{name}_res_added")
    s_out = sem(f"{name}_res_stored") if store is not None else None
    half = TILES // 2
    with nc.Block() as block:
        @block.tensor
        def _(pe):
            for c in range(NCH):
                if c >= 4:
                    pe.wait_ge(s_add, c - 3)
                for i in range(half):
                    mm = pe.transpose(t.PS[:, c % 4, i * P:(i + 1) * P],
                                      t.YT[:, (c * half + i) * P:(c * half + i + 1) * P], t.ident[:])
                mm.then_inc(s_tr, 1)

        @block.vector
        def _(dve):
            for c in range(NCH):
                dve.wait_ge(s_tr, c + 1)
                x = t.X[:, c * half:(c + 1) * half, :]
                dve.tensor_tensor(x, t.PS[:, c % 4, :].rearrange("p (i f) -> p i f", f=P), x,
                                  ALU.add).then_inc(s_add, 1)

        if store is not None:
            @block.sync
            def _(sp):
                for b in range(BATCH):
                    sp.wait_ge(s_add, 2 * b + 2)
                    sp.dma_start(store[b].rearrange("(i p) f -> p i f", p=P),
                                 t.X[:, b * TILES:(b + 1) * TILES, :]).then_inc(s_out, 16)
                sp.wait_ge(s_out, 16 * BATCH)


def norm_transpose(nc, t, sem, name, layer, shift, scale):
    s_cen = sem(f"{name}_ln_centred")
    s_sq = sem(f"{name}_ln_squares")
    s_v = sem(f"{name}_ln_vector_steps")
    s_sd = sem(f"{name}_ln_deviation")
    s_xn = sem(f"{name}_ln_normalised")
    s_tr = sem(f"{name}_ln_transposed")
    s_ht = sem(f"{name}_ln_modulated")
    half = TILES // 2
    with ExitStack() as ctx:
        xc = ctx.enter_context(nc.sbuf_tensor(f"{name}_xc", [P, NT, P], F32))
        sq = ctx.enter_context(nc.sbuf_tensor(f"{name}_sq", [P, 2, TILES, P], F32))
        st = ctx.enter_context(nc.sbuf_tensor(f"{name}_st", [P, 6, NT], F32))
        SUM, VAR, SD, RS, SQR, TMP = range(6)
        with nc.Block() as block:
            @block.vector
            def _(dve):
                v = 0
                for b in range(BATCH):
                    tl = slice(b * TILES, (b + 1) * TILES)
                    dve.tensor_reduce(st[:, SUM, tl], t.X[:, tl, :], AX, ALU.add).then_inc(s_v, 1)
                    v += 1
                    dve.wait_ge(s_v, v)
                    dve.tensor_scalar(st[:, SUM, tl], st[:, SUM, tl], 1.0 / P, None, ALU.mult).then_inc(s_v, 1)
                    v += 1
                    dve.wait_ge(s_v, v)
                    dve.tensor_tensor(xc[:, tl, :], t.X[:, tl, :], bcast(st[:, SUM, tl], P),
                                      ALU.subtract).then_inc(s_cen, 1)
                for b in range(BATCH):
                    tl = slice(b * TILES, (b + 1) * TILES)
                    dve.wait_ge(s_sq, b + 1)
                    dve.tensor_reduce(st[:, VAR, tl], sq[:, b % 2], AX, ALU.add).then_inc(s_v, 1)
                    v += 1
                dve.wait_ge(s_v, v)
                dve.tensor_scalar(st[:, VAR], st[:, VAR], 1.0 / P, EPS, ALU.mult, ALU.add).then_inc(s_v, 1)
                v += 1
                dve.wait_ge(s_sd, 1)
                dve.reciprocal(st[:, RS], st[:, SD]).then_inc(s_v, 1)
                v += 1
                dve.wait_ge(s_v, v)
                dve.tensor_tensor(st[:, SQR], st[:, RS], st[:, RS], ALU.mult).then_inc(s_v, 1)
                v += 1
                dve.wait_ge(s_v, v)
                dve.tensor_tensor(st[:, SQR], st[:, SQR], st[:, VAR], ALU.mult).then_inc(s_v, 1)
                v += 1
                dve.wait_ge(s_v, v)
                dve.tensor_scalar(st[:, TMP], st[:, SQR], -0.5, 1.5, ALU.mult, ALU.add).then_inc(s_v, 1)
                v += 1
                dve.wait_ge(s_v, v)
                dve.tensor_tensor(st[:, RS], st[:, RS], st[:, TMP], ALU.mult).then_inc(s_v, 1)
                v += 1
                dve.wait_ge(s_v, v)
                dve.wait_ge(s_cen, BATCH)
                for b in range(BATCH):
                    tl = slice(b * TILES, (b + 1) * TILES)
                    dve.tensor_tensor(xc[:, tl, :], xc[:, tl, :], bcast(st[:, RS, tl], P),
                                      ALU.mult).then_inc(s_xn, 1)

            @block.scalar
            def _(act):
                for b in range(BATCH):
                    act.wait_ge(s_cen, b + 1)
                    if b >= 2:
                        act.wait_ge(s_v, 2 * BATCH + b - 1)
                    act.activation(sq[:, b % 2], xc[:, b * TILES:(b + 1) * TILES, :], ACT.Square).then_inc(s_sq, 1)
                act.wait_ge(s_v, 3 * BATCH + 1)
                act.activation(st[:, SD], st[:, VAR], ACT.Sqrt).then_inc(s_sd, 1)
                for c in range(NCH):
                    act.wait_ge(s_tr, c + 1)
                    b = c // 2
                    act.activation(t.HT[:, c * CH:(c + 1) * CH], t.PS[:, c % 4, :], ACT.Identity,
                                   bias=t.MOD[:, layer, shift, b:b + 1],
                                   scale=t.MOD[:, layer, scale, b:b + 1]).then_inc(s_ht, 1)

            @block.tensor
            def _(pe):
                for c in range(NCH):
                    pe.wait_ge(s_xn, c // 2 + 1)
                    if c >= 4:
                        pe.wait_ge(s_ht, c - 3)
                    for i in range(half):
                        mm = pe.transpose(t.PS[:, c % 4, i * P:(i + 1) * P], xc[:, c * half + i, :], t.ident[:])
                    mm.then_inc(s_tr, 1)



GATE_ROWS = 4 * EXPERTS
TOP2_SOFTMAX, SOFTMAX_TOP2, TOP1 = range(3)


def route(nc, t, sem, name, src, router, bias, kind):
    s_lg = sem(f"{name}_logits")
    s_v = sem(f"{name}_route_vector_steps")
    s_e = sem(f"{name}_route_exponentials")
    s_tr = sem(f"{name}_route_transposed")
    s_gt = sem(f"{name}_route_copied")
    s_parts = sem(f"{name}_route_parts_ready")
    shape = [P, NT, EXPERTS]
    with ExitStack() as ctx:
        def sb(n, s, dt=F32):
            return ctx.enter_context(nc.sbuf_tensor(f"{name}_{n}", s, dt))
        lg, rest = sb("lg", shape), sb("rest", shape)
        top, first, second = sb("top", shape), sb("first", shape), sb("second", shape)
        where, wheref = sb("where", shape, U32), sb("wheref", [P, NT, 2])
        w = sb("w", shape)
        ratio, total, share = sb("ratio", [P, NT]), sb("total", [P, NT]), sb("share", [P, NT])
        g = sb("g", [P, NT, 4, EXPERTS], BF16)
        logits_ps = t.PS[:, 0, 0:NT * EXPERTS].rearrange("p (i e) -> p i e", e=EXPERTS)
        gt_ps = [t.PS[:, 1 + b, :].bitcast(BF16) for b in range(BATCH)]
        with nc.Block() as block:
            @block.tensor
            def _(pe):
                for i in range(NT):
                    mm = pe.matmul(logits_ps[:, i, :], src[:, i * P:(i + 1) * P], router, start=True, stop=True)
                mm.then_inc(s_lg, 1)
                pe.wait_ge(s_parts, 1)
                for b in range(BATCH):
                    for i in range(TILES):
                        mm = pe.transpose(gt_ps[b][0:GATE_ROWS, i * P:(i + 1) * P],
                                          g[:, b * TILES + i].rearrange("p k e -> p (k e)"), t.ident_bf[:])
                    mm.then_inc(s_tr, 1)

            @block.scalar
            def _(act):
                if kind == SOFTMAX_TOP2:
                    act.wait_ge(s_v, 3)
                    act.activation(lg[:], lg[:], ACT.Exp).then_inc(s_e, 1)
                if kind == TOP2_SOFTMAX:
                    act.wait_ge(s_v, 3)
                    act.activation(ratio[:], ratio[:], ACT.Exp).then_inc(s_e, 1)
                for b in range(BATCH):
                    act.wait_ge(s_tr, b + 1)
                    act.activation(t.GT[0:GATE_ROWS, b * SEQ:(b + 1) * SEQ], gt_ps[b][0:GATE_ROWS, 0:SEQ],
                                   ACT.Copy).then_inc(s_gt, 1)

            @block.vector
            def _(dve):
                v = 0

                def done(instruction):
                    nonlocal v
                    v += 1
                    instruction.then_inc(s_v, 1)
                    dve.wait_ge(s_v, v)

                dve.wait_ge(s_lg, 1)
                if bias is None:
                    done(dve.tensor_copy(lg[:], logits_ps))
                else:
                    done(dve.tensor_tensor(lg[:], logits_ps, bias.unsqueeze(1).broadcast_to(shape), ALU.add))
                if kind == SOFTMAX_TOP2:
                    done(dve.tensor_reduce(total[:], lg[:], AX, ALU.max))
                    done(dve.tensor_tensor(lg[:], lg[:], bcast(total[:], EXPERTS), ALU.subtract))
                    dve.wait_ge(s_e, 1)
                    done(dve.tensor_reduce(total[:], lg[:], AX, ALU.add))
                    done(dve.reciprocal(share[:], total[:]))
                    done(dve.tensor_tensor(lg[:], lg[:], bcast(share[:], EXPERTS), ALU.mult))
                last = None
                for i in range(NT):
                    last = dve.max(top[:, i], lg[:, i])
                if kind == TOP2_SOFTMAX:
                    done(last)
                    done(dve.tensor_tensor(ratio[:], top[:, :, 1], top[:, :, 0], ALU.subtract))
                else:
                    done(last)
                for i in range(NT):
                    last = dve.max_index(where[:, i], top[:, i], lg[:, i])
                done(last)
                done(dve.tensor_copy(wheref[:], where[:, :, 0:2]))
                places = t.iota8[:].unsqueeze(1).broadcast_to(shape)
                dve.tensor_tensor(first[:], places, bcast(wheref[:, :, 0], EXPERTS), ALU.is_equal)
                done(dve.tensor_tensor(second[:], places, bcast(wheref[:, :, 1], EXPERTS), ALU.is_equal))
                if kind == TOP1:
                    dve.memset(g[:, :, 0:3], 0.0)
                    dve.tensor_copy(g[:, :, 3], first[:]).then_inc(s_parts, 1)
                else:
                    if kind == TOP2_SOFTMAX:
                        dve.wait_ge(s_e, 1)
                        done(dve.tensor_scalar(total[:], ratio[:], 1.0, None, ALU.add))
                        done(dve.reciprocal(share[:], total[:]))
                        done(dve.tensor_tensor(total[:], ratio[:], share[:], ALU.mult))
                        done(dve.tensor_tensor(w[:], first[:], bcast(share[:], EXPERTS), ALU.mult))
                        done(dve.tensor_tensor(rest[:], second[:], bcast(total[:], EXPERTS), ALU.mult))
                        done(dve.tensor_tensor(w[:], w[:], rest[:], ALU.add))
                    done(dve.tensor_tensor(first[:], first[:], second[:], ALU.add))
                    if kind == SOFTMAX_TOP2:
                        done(dve.tensor_tensor(w[:], first[:], lg[:], ALU.mult))
                    dve.tensor_copy(g[:, :, 3], first[:])
                    done(dve.tensor_copy(g[:, :, 0], w[:]))
                    done(dve.tensor_tensor(rest[:], w[:], g[:, :, 0], ALU.subtract))
                    done(dve.tensor_copy(g[:, :, 1], rest[:]))
                    done(dve.tensor_tensor(w[:], rest[:], g[:, :, 1], ALU.subtract))
                    dve.tensor_copy(g[:, :, 2], w[:]).then_inc(s_parts, 1)


def experts(nc, t, sem, name, src, acc, hid, w1_d, w2_d, b1_d, b2_d, act_fn, gate_at):
    parts = hid // (2 * P)
    units = 2 * NCH
    n_w = 2 if b1_d is None else 4
    s_w = [sem(f"{name}_weights_loaded_{k}") for k in range(2)]
    s_free = sem(f"{name}_slots_reloaded")
    s_up = sem(f"{name}_first_products")
    s_relu = sem(f"{name}_relu")
    s_h = sem(f"{name}_hidden_ready")
    s_y = sem(f"{name}_second_products")
    s_gp = sem(f"{name}_gate_rows")
    s_g = sem(f"{name}_gates_ready")
    s_t = sem(f"{name}_gated")
    s_a = sem(f"{name}_added")
    with ExitStack() as ctx:
        def sb(n, s, dt=F32):
            return ctx.enter_context(nc.sbuf_tensor(f"{name}_{n}", s, dt))
        w1 = [sb(f"w1_{k}", [P, hid]) for k in range(2)]
        w2 = [sb(f"w2_{k}", [P, hid // P, P]) for k in range(2)]
        b1 = [sb(f"b1_{k}", [P, hid // P]) for k in range(2)]
        b2 = [sb(f"b2_{k}", [P, 1]) for k in range(2)]
        relu = sb("relu", [P, 2, 2, CH])
        h = sb("h", [P, 2, 2, CH])
        gate = sb("gate", [P, 2, CH])
        gated = sb("gated", [P, 2, CH])
        up_ps = [t.PS[:, 2 * k:2 * k + 2, :] for k in range(2)]
        g_ps = [t.PS[:, 4 + k, :] for k in range(2)]
        y_ps = [t.PS[:, 6 + k, :] for k in range(2)]
        with nc.Block() as block:
            @block.sync
            def _(sp):
                def load(e, k):
                    sp.dma_start(w1[k][:], w1_d[bass.ds(e, 1)].rearrange("a p f -> p (a f)")).then_inc(s_w[k], 16)
                    sp.dma_start(w2[k][:], w2_d[bass.ds(e, 1)].rearrange("a (j p) f -> p (a j) f", p=P)).then_inc(s_w[k], 16)
                    if b1_d is not None:
                        sp.dma_start(b1[k][:], b1_d[bass.ds(e, 1)].rearrange("a p j -> p (a j)")).then_inc(s_w[k], 16)
                        sp.dma_start(b2[k][:], b2_d[bass.ds(e, 1)].rearrange("a p o -> p (a o)")).then_inc(s_w[k], 16)
                for k in range(2):
                    load(k, k)
                with sp.Fori(0, EXPERTS // 2 - 1) as i:
                    for k in range(2):
                        sp.wait_ge(s_y, (2 * i + k + 1) * NCH * parts + 2)
                        sp.sem_inc(s_free, 1)
                        sp.wait_ge(s_t, (2 * i + k + 1) * NCH + 2)
                        load(2 * i + 2 + k, k)

            @block.tensor
            def _(pe):
                def up(i, u, part):
                    k, c, n = u // NCH, u % NCH, u * parts + part
                    if c == 0 and part == 0:
                        pe.wait_ge(s_w[k], 16 * n_w * (i + 1))
                    pe.wait_ge(s_h, i * units * parts + n + 1)
                    for j in range(2):
                        m = 2 * part + j
                        mm = pe.matmul(up_ps[n % 2][:, j, :], w1[k][:, m * P:(m + 1) * P],
                                       src[:, c * CH:(c + 1) * CH], start=True, stop=True)
                    mm.then_inc(s_up, 1)

                def spread(i, u):
                    k, c = u // NCH, u % NCH
                    pe.wait_ge(s_g, i * units + u + 1)
                    pe.matmul(g_ps[u % 2], t.Sel[:, bass.ds(i * 2 + k + gate_at, 1), :].rearrange("p a f -> p (a f)"),
                              t.GT[:, c * CH:(c + 1) * CH], start=True, stop=True).then_inc(s_gp, 1)

                def down(i, u, part):
                    k, n = u // NCH, u * parts + part
                    pe.wait_ge(s_h, i * units * parts + n + 3)
                    if part == 0:
                        pe.wait_ge(s_t, i * units + u + 1)
                    for j in range(2):
                        m = 2 * part + j
                        mm = pe.matmul(y_ps[u % 2], w2[k][:, m, :], h[:, n % 2, j, :],
                                       start=(m == 0), stop=(m == hid // P - 1))
                    mm.then_inc(s_y, 1)

                with pe.Fori(0, EXPERTS // 2) as i:
                    steps = [(u, part) for u in range(units) for part in range(parts)]
                    for n, (u, part) in enumerate(steps):
                        up(i, u, part)
                        if part == 0:
                            spread(i, u)
                        if n:
                            down(i, *steps[n - 1])
                    down(i, *steps[-1])

            @block.scalar
            def _(act):
                act.sem_inc(s_g, 2)
                with act.Fori(0, EXPERTS // 2) as i:
                    for u in range(units):
                        k = u // NCH
                        for part in range(parts):
                            n = u * parts + part
                            act.wait_ge(s_up, i * units * parts + n + 1)
                            if act_fn is None:
                                act.wait_ge(s_h, i * units * parts + n + 1)
                                act.activation(relu[:, n % 2], up_ps[n % 2], ACT.Relu).then_inc(s_relu, 1)
                            else:
                                act.wait_ge(s_y, i * units * parts + n + 1)
                                for j in range(2):
                                    m = 2 * part + j
                                    a = act.activation(h[:, n % 2, j, :], up_ps[n % 2][:, j, :], act_fn,
                                                       bias=b1[k][:, m:m + 1])
                                a.then_inc(s_h, 1)
                            if part == 0:
                                act.wait_ge(s_gp, i * units + u + 1)
                                act.wait_ge(s_t, i * units + u + 1)
                                act.activation(gate[:, u % 2], g_ps[u % 2], ACT.Copy).then_inc(s_g, 1)

            @block.vector
            def _(dve):
                dve.sem_inc(s_t, 2)
                dve.sem_inc(s_y, 2)
                dve.sem_inc(s_h, 2)

                def square(i, u, part):
                    n = u * parts + part
                    dve.wait_ge(s_relu, i * units * parts + n + 1)
                    dve.wait_ge(s_y, i * units * parts + n + 1)
                    dve.scalar_tensor_tensor(h[:, n % 2], up_ps[n % 2], 0.0, relu[:, n % 2], ALU.max,
                                             ALU.mult).then_inc(s_h, 1)

                def weigh(i, u):
                    dve.wait_ge(s_y, i * units * parts + (u + 1) * parts + 2)
                    dve.wait_ge(s_g, i * units + u + 3)
                    dve.wait_ge(s_a, i * units + u + 1)
                    if b2_d is None:
                        dve.tensor_tensor(gated[:, u % 2], y_ps[u % 2], gate[:, u % 2], ALU.mult).then_inc(s_t, 1)
                    else:
                        dve.scalar_tensor_tensor(gated[:, u % 2], y_ps[u % 2], b2[u // NCH][:, 0:1],
                                                 gate[:, u % 2], ALU.add, ALU.mult).then_inc(s_t, 1)

                with dve.Fori(0, EXPERTS // 2) as i:
                    for u in range(units):
                        for part in range(parts):
                            if act_fn is None:
                                square(i, u, part)
                        if u:
                            weigh(i, u - 1)
                    weigh(i, units - 1)

            @block.gpsimd
            def _(pool):
                pool.memset(acc[:], 0.0).then_inc(s_a, 2)
                with pool.Fori(0, EXPERTS // 2) as i:
                    for u in range(units):
                        c = u % NCH
                        pool.wait_ge(s_t, i * units + u + 3)
                        pool.wait_ge(s_a, i * units + u + 2)
                        part = acc[:, c * CH:(c + 1) * CH]
                        pool.tensor_tensor(part, part, gated[:, u % 2], ALU.add).then_inc(s_a, 1)


def gate_in_place(nc, t, sem, name, layer, gate):
    s = sem(f"{name}_gate_applied")
    with nc.Block() as block:
        @block.vector
        def _(dve):
            for b in range(BATCH):
                y = t.YT[:, b * SEQ:(b + 1) * SEQ]
                dve.tensor_scalar(y, y, t.MOD[:, layer, gate, b:b + 1], None, ALU.mult).then_inc(s, 1)
            dve.wait_ge(s, BATCH)


def open_gates(nc, t, sem, name, d, ctx, router, bias=None):
    t.GT = ctx.enter_context(nc.sbuf_tensor(f"{name}_GT", [P, TOK], BF16))
    t.Sel = ctx.enter_context(nc.sbuf_tensor(f"{name}_Sel", [P, 2 * EXPERTS, P], BF16))
    router_sb = ctx.enter_context(nc.sbuf_tensor(f"{name}_router", [P, EXPERTS], F32))
    bias_sb = ctx.enter_context(nc.sbuf_tensor(f"{name}_router_b", [P, EXPERTS], F32))
    s = sem(f"{name}_gate_inputs_loaded")
    s_c = sem(f"{name}_gate_constants_ready")
    with nc.sbuf_tensor(f"{name}_sel_f32", [P, 2 * EXPERTS, P], F32) as sel, nc.Block() as block:
        @block.sync
        def _(sp):
            sp.dma_start(router_sb[:], router).then_inc(s, 16)
            sp.dma_start(sel[:], d["gate_rows"]).then_inc(s, 16)
            sp.dma_start(t.iota8[:], d["iota8"]).then_inc(s, 16)
            if bias is not None:
                sp.dma_start(bias_sb[:], bias.broadcast_to((P, EXPERTS))).then_inc(s, 16)

        @block.vector
        def _(dve):
            dve.memset(t.GT[:], 0.0).then_inc(s_c, 1)
            dve.wait_ge(s, 48 if bias is None else 64)
            dve.tensor_copy(t.ident_bf[:], t.ident[:]).then_inc(s_c, 1)
            dve.tensor_copy(t.Sel[:], sel[:]).then_inc(s_c, 1)
            dve.wait_ge(s_c, 3)
    return router_sb[:], None if bias is None else bias_sb[:]


def ffn0(nc, t, sem, d):
    with ExitStack() as ctx:
        router, _ = open_gates(nc, t, sem, "f0", d, ctx, d["L0_router"])
        route(nc, t, sem, "f0", t.HT, router, None, TOP2_SOFTMAX)
        experts(nc, t, sem, "f0", t.HT, t.YT, 2 * P, d["L0_w1"], d["L0_w2"], None, None, None, 0)
        gate_in_place(nc, t, sem, "f0", 0, GATE_B)


def ffn3(nc, t, sem, d):
    with ExitStack() as ctx:
        router, bias = open_gates(nc, t, sem, "f3", d, ctx, d["L3_router"], d["L3_router_b"])
        route(nc, t, sem, "f3", t.HT, router, bias, TOP1)
        experts(nc, t, sem, "f3", t.HT, t.YT, 4 * P, d["L3_w1"], d["L3_w2"], d["L3_b1"], d["L3_b2"],
                ACT.Relu, EXPERTS)
        gate_in_place(nc, t, sem, "f3", 3, GATE_B)


def glu_experts(nc, t, sem, name, src, acc, w_d, b_d):
    units = 2 * NCH
    s_w = [sem(f"{name}_weights_loaded_{k}") for k in range(2)]
    s_gp = sem(f"{name}_gate_rows")
    s_g = sem(f"{name}_gates_ready")
    s_xs = sem(f"{name}_scaled_inputs")
    s_up = sem(f"{name}_first_products")
    s_h = sem(f"{name}_hidden_ready")
    s_x3 = sem(f"{name}_third_ready")
    s_y = sem(f"{name}_second_products")
    s_t = sem(f"{name}_products_taken")
    s_a = sem(f"{name}_added")
    with ExitStack() as ctx:
        def sb(n, s, dt=F32):
            return ctx.enter_context(nc.sbuf_tensor(f"{name}_{n}", s, dt))
        w = [sb(f"w_{k}", [P, 3, P]) for k in range(2)]
        bias = [sb(f"b_{k}", [P, 3]) for k in range(2)]
        gate = sb("gate", [P, 2, 2, CH])
        xs, h, x3, prod = sb("xs", [P, 2, CH]), sb("h", [P, 2, CH]), sb("x3", [P, 2, CH]), sb("prod", [P, 2, CH])
        up_ps = [t.PS[:, 2 * k:2 * k + 2, :] for k in range(2)]
        g_ps = t.PS[:, 4:6, :]
        y_ps = [t.PS[:, 6 + k, :] for k in range(2)]
        with nc.Block() as block:
            @block.sync
            def _(sp):
                def load(e, k):
                    sp.dma_start(w[k][:], w_d[bass.ds(e, 1)].rearrange("a p j f -> p (a j) f")).then_inc(s_w[k], 16)
                    sp.dma_start(bias[k][:], b_d[bass.ds(e, 1)].rearrange("a p j -> p (a j)")).then_inc(s_w[k], 16)
                for k in range(2):
                    load(k, k)
                with sp.Fori(0, EXPERTS // 2 - 1) as i:
                    for k in range(2):
                        sp.wait_ge(s_y, (2 * i + k + 1) * NCH + 2)
                        sp.wait_ge(s_t, (2 * i + k + 1) * NCH + 2)
                        load(2 * i + 2 + k, k)

            @block.tensor
            def _(pe):
                def spread(i, u, k, c):
                    pe.wait_ge(s_g, i * units + u + 1)
                    for m in range(2):
                        mm = pe.matmul(g_ps[:, m, :],
                                       t.Sel[:, bass.ds(i * 2 + k + m * EXPERTS, 1), :].rearrange("p a f -> p (a f)"),
                                       t.GT[:, c * CH:(c + 1) * CH], start=True, stop=True)
                    mm.then_inc(s_gp, 1)

                def up(i, u):
                    k = u // NCH
                    if u % NCH == 0:
                        pe.wait_ge(s_w[k], 32 * (i + 1))
                    pe.wait_ge(s_xs, i * units + u + 1)
                    pe.wait_ge(s_h, i * units + u + 1)
                    pe.wait_ge(s_x3, i * units + u + 1)
                    for m in range(2):
                        mm = pe.matmul(up_ps[u % 2][:, m, :], w[k][:, m, :], xs[:, u % 2, :], start=True, stop=True)
                    mm.then_inc(s_up, 1)

                def down(i, u):
                    pe.wait_ge(s_h, i * units + u + 3)
                    pe.wait_ge(s_t, i * units + u + 1)
                    pe.matmul(y_ps[u % 2], w[u // NCH][:, 2, :], h[:, u % 2, :], start=True, stop=True).then_inc(s_y, 1)

                with pe.Fori(0, EXPERTS // 2) as i:
                    spread(i, 0, 0, 0)
                    for u in range(units):
                        if u + 1 < units:
                            spread(i, u + 1, (u + 1) // NCH, (u + 1) % NCH)
                        up(i, u)
                        if u:
                            down(i, u - 1)
                    down(i, units - 1)

            @block.scalar
            def _(act):
                act.sem_inc(s_g, 1)
                act.sem_inc(s_h, 2)
                with act.Fori(0, EXPERTS // 2) as i:
                    def gates(u):
                        act.wait_ge(s_gp, i * units + u + 1)
                        act.wait_ge(s_x3, i * units + u + 1)
                        act.activation(gate[:, u % 2], g_ps, ACT.Copy).then_inc(s_g, 1)
                    gates(0)
                    for u in range(units):
                        if u + 1 < units:
                            gates(u + 1)
                        act.wait_ge(s_up, i * units + u + 1)
                        act.wait_ge(s_y, i * units + u + 1)
                        act.activation(h[:, u % 2], up_ps[u % 2][:, 0, :], ACT.Silu,
                                       bias=bias[u // NCH][:, 0:1]).then_inc(s_h, 1)

            @block.vector
            def _(dve):
                dve.sem_inc(s_x3, 2)
                dve.sem_inc(s_y, 2)
                dve.sem_inc(s_t, 2)
                with dve.Fori(0, EXPERTS // 2) as i:
                    def scaled(u):
                        c = u % NCH
                        dve.wait_ge(s_g, i * units + u + 2)
                        if u >= 2:
                            dve.wait_ge(s_up, i * units + u - 1)
                        dve.tensor_tensor(xs[:, u % 2], src[:, c * CH:(c + 1) * CH], gate[:, u % 2, 0],
                                          ALU.mult).then_inc(s_xs, 1)

                    def third(u):
                        dve.wait_ge(s_up, i * units + u + 1)
                        dve.wait_ge(s_t, i * units + u + 1)
                        dve.scalar_tensor_tensor(x3[:, u % 2], up_ps[u % 2][:, 1, :], bias[u // NCH][:, 1:2],
                                                 gate[:, u % 2, 1], ALU.add, ALU.mult).then_inc(s_x3, 1)

                    def combine(u):
                        dve.wait_ge(s_y, i * units + u + 3)
                        dve.wait_ge(s_x3, i * units + u + 3)
                        dve.wait_ge(s_a, i * units + u + 1)
                        dve.scalar_tensor_tensor(prod[:, u % 2], y_ps[u % 2], bias[u // NCH][:, 2:3],
                                                 x3[:, u % 2], ALU.add, ALU.mult).then_inc(s_t, 1)

                    scaled(0)
                    for u in range(units):
                        if u + 1 < units:
                            scaled(u + 1)
                        third(u)
                        if u:
                            combine(u - 1)
                    combine(units - 1)

            @block.gpsimd
            def _(pool):
                pool.memset(acc[:], 0.0).then_inc(s_a, 2)
                with pool.Fori(0, EXPERTS // 2) as i:
                    for u in range(units):
                        c = u % NCH
                        pool.wait_ge(s_t, i * units + u + 3)
                        pool.wait_ge(s_a, i * units + u + 2)
                        part = acc[:, c * CH:(c + 1) * CH]
                        pool.tensor_tensor(part, part, prod[:, u % 2], ALU.add).then_inc(s_a, 1)


def shared_expert(nc, t, sem, name, src, acc, d):
    s_w = sem(f"{name}_shared_weights_loaded")
    s_u1, s_u2 = sem(f"{name}_shared_up1"), sem(f"{name}_shared_up2")
    s_si, s_m = sem(f"{name}_shared_silu"), sem(f"{name}_shared_product")
    s_y, s_a = sem(f"{name}_shared_down"), sem(f"{name}_shared_added")
    with ExitStack() as ctx:
        def sb(n, s, dt=F32):
            return ctx.enter_context(nc.sbuf_tensor(f"{name}_{n}", s, dt))
        w = sb("shared_w", [P, 6, P])
        silu, m = sb("shared_silu", [P, 2, 2, CH]), sb("shared_m", [P, 2, 2, CH])
        u1 = [t.PS[:, 2 * k:2 * k + 2, :] for k in range(2)]
        u2 = t.PS[:, 4:6, :]
        y = [t.PS[:, 6 + k, :] for k in range(2)]
        with nc.Block() as block:
            @block.sync
            def _(sp):
                sp.dma_start(w[:], d["L1_shared"]).then_inc(s_w, 16)

            @block.tensor
            def _(pe):
                def down(c):
                    pe.wait_ge(s_m, c + 1)
                    if c >= 2:
                        pe.wait_ge(s_a, c - 1)
                    for j in range(2):
                        mm = pe.matmul(y[c % 2], w[:, 4 + j, :], m[:, c % 2, j, :], start=(j == 0), stop=(j == 1))
                    mm.then_inc(s_y, 1)

                pe.wait_ge(s_w, 16)
                for c in range(NCH):
                    x = src[:, c * CH:(c + 1) * CH]
                    if c >= 2:
                        pe.wait_ge(s_si, c - 1)
                    for j in range(2):
                        mm = pe.matmul(u1[c % 2][:, j, :], w[:, j, :], x, start=True, stop=True)
                    mm.then_inc(s_u1, 1)
                    if c >= 1:
                        down(c - 1)
                    for j in range(2):
                        mm = pe.matmul(u2[:, j, :], w[:, 2 + j, :], x, start=True, stop=True)
                    mm.then_inc(s_u2, 1)
                down(NCH - 1)

            @block.scalar
            def _(act):
                for c in range(NCH):
                    act.wait_ge(s_u1, c + 1)
                    if c >= 2:
                        act.wait_ge(s_m, c - 1)
                    act.activation(silu[:, c % 2], u1[c % 2], ACT.Silu).then_inc(s_si, 1)

            @block.vector
            def _(dve):
                def add(c):
                    dve.wait_ge(s_y, c + 1)
                    part = acc[:, c * CH:(c + 1) * CH]
                    dve.tensor_tensor(part, y[c % 2], part, ALU.add).then_inc(s_a, 1)
                for c in range(NCH):
                    dve.wait_ge(s_u2, c + 1)
                    dve.wait_ge(s_si, c + 1)
                    if c >= 2:
                        dve.wait_ge(s_y, c - 1)
                    dve.tensor_tensor(m[:, c % 2], u2, silu[:, c % 2], ALU.mult).then_inc(s_m, 1)
                    if c:
                        add(c - 1)
                add(NCH - 1)


def ffn1(nc, t, sem, d):
    with ExitStack() as ctx:
        router, _ = open_gates(nc, t, sem, "f1", d, ctx, d["L1_router"])
        route(nc, t, sem, "f1", t.HT, router, None, SOFTMAX_TOP2)
        glu_experts(nc, t, sem, "f1", t.HT, t.YT, d["L1_w"], d["L1_b"])
        shared_expert(nc, t, sem, "f1", t.HT, t.YT, d)
        gate_in_place(nc, t, sem, "f1", 1, GATE_B)


ROTATIONS = 3
SQUARINGS = 16
TAYLOR = [1.0, 1.0, 1 / 2, 1 / 6, 1 / 24, 1 / 120, 1 / 720, 1 / 5040, 1 / 40320, 1 / 362880]
THETA = 0.5


def matrix_exponentials(nc, t, sem, d):
    s_in, s_v, s_mm = sem("expm_loaded"), sem("expm_vector_steps"), sem("expm_products")
    s_sq = sem("expm_squarings")
    FIRST = 22
    shape = [P, 2 * ROTATIONS, P]
    with ExitStack() as ctx:
        def sb(n, s, dt=F32):
            return ctx.enter_context(nc.sbuf_tensor(f"expm_{n}", s, dt))
        b1, b2, b3, r = sb("b1", shape), sb("b2", shape), sb("b3", shape), sb("r", shape)
        a, q = sb("a", shape), sb("q", shape)
        diag = sb("diag", [P, 3, P])
        ones = sb("ones", [P, P])
        norm, thr, flag = sb("norm", [P, ROTATIONS]), sb("thr", [P, 1]), sb("flag", [P, ROTATIONS])
        inv = sb("inv", [P, ROTATIONS])
        table = sb("table", [P, 2, SQUARINGS + 1])
        cand = sb("cand", [P, ROTATIONS, SQUARINGS + 1])
        ps = t.PS[:, 0:2, :].rearrange("p b f -> p (b f)")[:, 0:2 * ROTATIONS * P].rearrange("p (m f) -> p m f", f=P)
        with nc.Block() as block:
            @block.sync
            def _(sp):
                sp.dma_start(b1[:], d["L2_gens"]).then_inc(s_in, 16)
                sp.dma_start(table[:], d["expm_table"]).then_inc(s_in, 16)

            @block.tensor
            def _(pe):
                def products(left, right):
                    for m in range(ROTATIONS):
                        pe.matmul(ps[:, 2 * m, :], left[:, 2 * m + 1, :], right[:, 2 * m, :], start=True, stop=True)
                        last = pe.matmul(ps[:, 2 * m + 1, :], left[:, 2 * m, :], right[:, 2 * m + 1, :],
                                         start=True, stop=True)
                    last.then_inc(s_mm, 1)

                pe.wait_ge(s_v, 2)
                for m in range(ROTATIONS):
                    last = pe.matmul(ps[:, m, :], ones[:], a[:, 2 * m, :], start=True, stop=True)
                last.then_inc(s_mm, 1)
                pe.wait_ge(s_v, 7)
                products(b1, b1)
                pe.wait_ge(s_v, 8)
                products(b2, b1)
                pe.wait_ge(s_v, 15)
                products(b3, r)
                pe.wait_ge(s_v, 18)
                products(b3, r)
                with pe.Fori(0, SQUARINGS) as k:
                    pe.wait_ge(s_v, 3 * k + FIRST)
                    products(r, r)
                pe.wait_ge(s_v, 3 * SQUARINGS + FIRST)
                pe.matmul(ps[:, 0, :], r[:, 3, :], r[:, 4, :], start=True, stop=True).then_inc(s_mm, 1)
                pe.wait_ge(s_v, 3 * SQUARINGS + FIRST + 1)
                pe.matmul(ps[:, 1, :], r[:, 1, :], a[:, 0, :], start=True, stop=True).then_inc(s_mm, 1)

            @block.vector
            def _(dve):
                v = 0

                def done(instruction):
                    nonlocal v
                    v += 1
                    instruction.then_inc(s_v, 1)
                    dve.wait_ge(s_v, v)

                dve.wait_ge(s_in, 32)
                done(dve.memset(ones[:], 1.0))
                done(dve.scalar_tensor_tensor(a[:], b1[:], -1.0, b1[:], ALU.mult, ALU.max))
                dve.wait_ge(s_mm, 1)
                done(dve.tensor_reduce(norm[:], ps[:, 0:ROTATIONS, :], AX, ALU.max))
                done(dve.tensor_tensor(cand[:], table[:, 0:1, :].broadcast_to(cand.shape),
                                       bcast(norm[:], SQUARINGS + 1), ALU.is_ge))
                done(dve.tensor_tensor(cand[:], cand[:], table[:, 1:2, :].broadcast_to(cand.shape), ALU.mult))
                done(dve.tensor_reduce(inv[:], cand[:], AX, ALU.max))
                done(dve.tensor_tensor(b1[:].rearrange("p (m k) f -> p m (k f)", k=2),
                                       b1[:].rearrange("p (m k) f -> p m (k f)", k=2), bcast(inv[:], 2 * P), ALU.mult))
                dve.wait_ge(s_mm, 2)
                done(dve.tensor_copy(b2[:], ps))
                dve.wait_ge(s_mm, 3)
                done(dve.tensor_copy(b3[:], ps))
                for j in range(3):
                    done(dve.tensor_scalar(diag[:, j], t.ident[:], TAYLOR[3 * j], None, ALU.mult))

                def bracket(j, out):
                    done(dve.scalar_tensor_tensor(out[:], b1[:], TAYLOR[3 * j + 1],
                                                  diag[:, j:j + 1].broadcast_to(shape), ALU.mult, ALU.add))
                    done(dve.scalar_tensor_tensor(out[:], b2[:], TAYLOR[3 * j + 2], out[:], ALU.mult, ALU.add))

                bracket(2, a)
                done(dve.scalar_tensor_tensor(r[:], b3[:], TAYLOR[9], a[:], ALU.mult, ALU.add))
                bracket(1, q)
                dve.wait_ge(s_mm, 4)
                done(dve.tensor_tensor(r[:], ps, q[:], ALU.add))
                bracket(0, q)
                dve.wait_ge(s_mm, 5)
                done(dve.tensor_tensor(r[:], ps, q[:], ALU.add))
                done(dve.memset(thr[:], THETA))
                assert v == FIRST
                with dve.Fori(0, SQUARINGS) as k:
                    dve.tensor_scalar(flag[:], norm[:], thr[:, 0:1], None, ALU.is_gt).then_inc(s_v, 1)
                    dve.wait_ge(s_v, 3 * k + FIRST + 1)
                    dve.tensor_scalar(thr[:], thr[:], 2.0, None, ALU.mult).then_inc(s_v, 1)
                    dve.wait_ge(s_mm, k + 6)
                    dve.wait_ge(s_v, 3 * k + FIRST + 2)
                    dve.sem_inc(s_sq, 1)
                    dve.copy_predicated(r[:].rearrange("p (m k) f -> p m (k f)", k=2),
                                        bcast(flag[:].bitcast(I32), 2 * P),
                                        ps.rearrange("p (m k) f -> p m (k f)", k=2)).then_inc(s_v, 1)
                    dve.wait_ge(s_v, 3 * k + FIRST + 3)
                v += 3 * SQUARINGS
                dve.wait_ge(s_mm, SQUARINGS + 6)
                done(dve.tensor_copy(a[:, 0], ps[:, 0, :]))
                dve.wait_ge(s_mm, SQUARINGS + 7)
                done(dve.tensor_copy(t.C[:], ps[:, 1, :]))


def norm_features(nc, t, sem, xn, d):
    s_in, s_one = sem("n2_loaded"), sem("n2_ones_ready")
    s_mean, s_c, s_sq = sem("n2_means"), sem("n2_centred"), sem("n2_squares")
    s_var, s_v, s_sd, s_xn = sem("n2_variances"), sem("n2_vector_steps"), sem("n2_deviation"), sem("n2_normalised")
    with ExitStack() as ctx:
        def sb(n, s, dt=F32):
            return ctx.enter_context(nc.sbuf_tensor(f"n2_{n}", s, dt))
        affine, ones = sb("affine", [P, 2]), sb("ones", [P, P])
        sq, var, sd, r, tmp = (sb(n, [P, 2, CH]) for n in ("sq", "var", "sd", "r", "tmp"))
        mean_ps = [t.PS[:, k, :] for k in range(2)]
        var_ps = [t.PS[:, 2 + k, :] for k in range(2)]
        with nc.Block() as block:
            @block.sync
            def _(sp):
                sp.dma_start(affine[:], d["L2_norm"]).then_inc(s_in, 16)

            @block.tensor
            def _(pe):
                def variances(c):
                    pe.wait_ge(s_sq, c + 1)
                    if c >= 2:
                        pe.wait_ge(s_v, 6 * (c - 2) + 1)
                    pe.matmul(var_ps[c % 2], ones[:], sq[:, c % 2], start=True, stop=True).then_inc(s_var, 1)
                pe.wait_ge(s_one, 1)
                for c in range(NCH):
                    if c >= 2:
                        pe.wait_ge(s_c, c - 1)
                    pe.matmul(mean_ps[c % 2], ones[:], t.HT[:, c * CH:(c + 1) * CH],
                              start=True, stop=True).then_inc(s_mean, 1)
                    if c:
                        variances(c - 1)
                variances(NCH - 1)

            @block.scalar
            def _(act):
                def roots(c):
                    act.wait_ge(s_v, 6 * c + 1)
                    act.activation(sd[:, c % 2], var[:, c % 2], ACT.Sqrt).then_inc(s_sd, 1)
                for c in range(NCH):
                    act.wait_ge(s_c, c + 1)
                    if c >= 2:
                        act.wait_ge(s_var, c - 1)
                    act.activation(sq[:, c % 2], xn[:, c * CH:(c + 1) * CH], ACT.Square).then_inc(s_sq, 1)
                    if c:
                        roots(c - 1)
                roots(NCH - 1)

            @block.vector
            def _(dve):
                v = 0

                def done(instruction):
                    nonlocal v
                    v += 1
                    instruction.then_inc(s_v, 1)
                    dve.wait_ge(s_v, v)

                def centre(c):
                    dve.wait_ge(s_mean, c + 1)
                    part = slice(c * CH, (c + 1) * CH)
                    dve.tensor_tensor(xn[:, part], t.HT[:, part], mean_ps[c % 2], ALU.subtract).then_inc(s_c, 1)

                dve.memset(ones[:], 1.0 / P).then_inc(s_one, 1)
                dve.wait_ge(s_in, 16)
                centre(0)
                for c in range(NCH):
                    if c + 1 < NCH:
                        centre(c + 1)
                    k = c % 2
                    part = xn[:, c * CH:(c + 1) * CH]
                    dve.wait_ge(s_var, c + 1)
                    done(dve.tensor_scalar(var[:, k], var_ps[k], EPS, None, ALU.add))
                    dve.wait_ge(s_sd, c + 1)
                    done(dve.reciprocal(r[:, k], sd[:, k]))
                    done(dve.tensor_tensor(tmp[:, k], r[:, k], r[:, k], ALU.mult))
                    done(dve.tensor_tensor(tmp[:, k], tmp[:, k], var[:, k], ALU.mult))
                    done(dve.tensor_scalar(tmp[:, k], tmp[:, k], -0.5, 1.5, ALU.mult, ALU.add))
                    done(dve.tensor_tensor(r[:, k], r[:, k], tmp[:, k], ALU.mult))
                    dve.tensor_tensor(part, part, r[:, k], ALU.mult).then_inc(s_xn, 1)
                    dve.wait_ge(s_xn, 2 * c + 1)
                    dve.tensor_scalar(part, part, affine[:, 0:1], affine[:, 1:2], ALU.mult, ALU.add).then_inc(s_xn, 1)
                    dve.wait_ge(s_xn, 2 * c + 2)


def mix(nc, t, sem, xn, d):
    s_in, s_w = sem("m2_loaded"), sem("m2_mix_weights_ready")
    s_p, s_a, s_m = sem("m2_products"), sem("m2_abel_ready"), sem("m2_moe_ready")
    s_z, s_g, s_v = sem("m2_mix_logits"), sem("m2_mix_gates"), sem("m2_vector_steps")
    with ExitStack() as ctx:
        def sb(n, s, dt=F32):
            return ctx.enter_context(nc.sbuf_tensor(f"m2_{n}", s, dt))
        wa, ba, mw, mb = sb("abel_w", [P, P]), sb("abel_b", [P, 1]), sb("mix_w", [P, 2]), sb("mix_b", [P, 1])
        mwb = sb("mix_wb", [P, 2, P])
        abel, moe, g = sb("abel", [P, 2, CH]), sb("moe", [P, 2, CH]), sb("g", [P, 2, CH])
        with nc.Block() as block:
            @block.sync
            def _(sp):
                sp.dma_start(wa[:], d["L2_abel_w"]).then_inc(s_in, 16)
                sp.dma_start(ba[:], d["L2_abel_b"]).then_inc(s_in, 16)
                sp.dma_start(mw[:], d["L2_mix_w"]).then_inc(s_in, 16)
                sp.dma_start(mb[:], d["L2_mix_b"].broadcast_to((P, 1))).then_inc(s_in, 16)

            @block.tensor
            def _(pe):
                def logits(c):
                    pe.wait_ge(s_a, c + 1)
                    pe.wait_ge(s_m, c + 1)
                    if c >= 2:
                        pe.wait_ge(s_g, c - 1)
                    pe.matmul(t.PS[:, 4 + c % 2, :], mwb[:, 0], abel[:, c % 2], start=True, stop=False)
                    pe.matmul(t.PS[:, 4 + c % 2, :], mwb[:, 1], moe[:, c % 2], start=False, stop=True).then_inc(s_z, 1)
                pe.wait_ge(s_in, 64)
                pe.wait_ge(s_w, 1)
                for c in range(NCH):
                    part = slice(c * CH, (c + 1) * CH)
                    if c >= 2:
                        pe.wait_ge(s_a, c - 1)
                        pe.wait_ge(s_m, c - 1)
                    pe.matmul(t.PS[:, c % 2, :], wa[:], xn[:, part], start=True, stop=True)
                    pe.matmul(t.PS[:, 2 + c % 2, :], t.C[:], t.YT[:, part], start=True, stop=True).then_inc(s_p, 1)
                    if c:
                        logits(c - 1)
                logits(NCH - 1)

            @block.scalar
            def _(act):
                def gates(c):
                    act.wait_ge(s_z, c + 1)
                    if c >= 2:
                        act.wait_ge(s_v, 3 * (c - 1))
                    act.activation(g[:, c % 2], t.PS[:, 4 + c % 2, :], ACT.Sigmoid, bias=mb[:, 0:1]).then_inc(s_g, 1)
                act.wait_ge(s_in, 64)
                for c in range(NCH):
                    act.wait_ge(s_p, c + 1)
                    if c >= 2:
                        act.wait_ge(s_v, 3 * (c - 1))
                    act.activation(abel[:, c % 2], t.PS[:, c % 2, :], ACT.Gelu, bias=ba[:, 0:1]).then_inc(s_a, 1)
                    if c:
                        gates(c - 1)
                gates(NCH - 1)

            @block.vector
            def _(dve):
                dve.wait_ge(s_in, 64)
                dve.tensor_copy(mwb[:], bcast(mw[:], P)).then_inc(s_w, 1)

                def moes(c):
                    dve.wait_ge(s_p, c + 1)
                    dve.tensor_copy(moe[:, c % 2], t.PS[:, 2 + c % 2, :]).then_inc(s_m, 1)
                moes(0)
                for c in range(NCH):
                    k = c % 2
                    part = slice(c * CH, (c + 1) * CH)
                    dve.wait_ge(s_z, c + 1)
                    dve.wait_ge(s_m, c + 1)
                    dve.wait_ge(s_a, c + 1)
                    dve.tensor_tensor(moe[:, k], moe[:, k], abel[:, k], ALU.subtract).then_inc(s_v, 1)
                    if c + 1 < NCH:
                        if c:
                            dve.wait_ge(s_v, 3 * c)
                        moes(c + 1)
                    dve.wait_ge(s_g, c + 1)
                    dve.wait_ge(s_v, 3 * c + 1)
                    dve.tensor_tensor(moe[:, k], moe[:, k], g[:, k], ALU.mult)
                    dve.tensor_tensor(abel[:, k], abel[:, k], t.HT[:, part], ALU.add).then_inc(s_v, 1)
                    dve.wait_ge(s_v, 3 * c + 2)
                    dve.tensor_tensor(t.YT[:, part], moe[:, k], abel[:, k], ALU.add).then_inc(s_v, 1)


def ffn2(nc, t, sem, d):
    with ExitStack() as ctx:
        xn = ctx.enter_context(nc.sbuf_tensor("f2_xn", [P, TOK], F32))
        t.C = ctx.enter_context(nc.sbuf_tensor("expm_C", [P, P], F32))
        matrix_exponentials(nc, t, sem, d)
        norm_features(nc, t, sem, xn, d)
        router, bias = open_gates(nc, t, sem, "f2", d, ctx, d["L2_router"], d["L2_router_b"])
        route(nc, t, sem, "f2", xn, router, bias, TOP2_SOFTMAX)
        experts(nc, t, sem, "f2", xn, t.YT, 2 * P, d["L2_w1"], d["L2_w2"], d["L2_b1"], d["L2_b2"], ACT.Gelu, 0)
        mix(nc, t, sem, xn, d)
        gate_in_place(nc, t, sem, "f2", 2, GATE_B)


HEADS = 16
HD = P // HEADS


def attention3(nc, t, sem, d):
    Q, K, V, W, R = 0, P, 2 * P, 3 * P, 3 * P + HEADS
    COLS = 3 * P + 2 * HEADS
    s_in, s_p, s_qkv = sem("a3_loaded"), sem("a3_projected"), sem("a3_biased")
    s_v, s_act, s_s = sem("a3_vector_steps"), sem("a3_scalar_steps"), sem("a3_scores")
    s_sv, s_o = sem("a3_weighted_values"), sem("a3_heads_out")
    s_tr, s_ot, s_y, s_yt = sem("a3_transposed"), sem("a3_transposes_copied"), sem("a3_output"), sem("a3_gated")
    with ExitStack() as ctx:
        def sb(n, s, dt=F32):
            return ctx.enter_context(nc.sbuf_tensor(f"a3_{n}", s, dt))
        w, bias = sb("w", [P, COLS]), sb("bias", [P, COLS])
        wo, bo = sb("wo", [P, P]), sb("bo", [P, 1])
        qkv = sb("qkv", [P, NT, COLS])
        prod = sb("prod", [P, BATCH, TILES * P])
        sv = sb("sv", [P, BATCH, TILES * P])
        score = sb("score", [P, NT * HEADS])
        o = sb("o", [P, 2, TILES * P])
        n2, nrm, rec = (sb(n, [P, NT, 2 * HEADS]) for n in ("n2", "nrm", "rec"))
        ot = t.HT
        with nc.Block() as block:
            @block.sync
            def _(sp):
                sp.dma_start(w[:], d["L3_qkvwr"]).then_inc(s_in, 16)
                sp.dma_start(bias[:], d["L3_qkvwr_b"].broadcast_to((P, COLS))).then_inc(s_in, 16)
                sp.dma_start(wo[:], d["L3_wo"]).then_inc(s_in, 16)
                sp.dma_start(bo[:], d["L3_bo"]).then_inc(s_in, 16)

            @block.tensor
            def _(pe):
                pe.wait_ge(s_in, 64)
                for i in range(NT):
                    if i >= 4:
                        pe.wait_ge(s_qkv, i - 3)
                    pe.matmul(t.PS[:, i % 4, 0:COLS], t.HT[:, i * P:(i + 1) * P], w[:], start=True,
                              stop=True).then_inc(s_p, 1)
                for s in range(BATCH):
                    pe.wait_ge(s_o, s + 1)
                    for half in range(2):
                        c = 2 * s + half
                        if c >= 2:
                            pe.wait_ge(s_ot, c - 1)
                        for i in range(4):
                            j = 4 * half + i
                            mm = pe.transpose(t.PS[:, 4 + half, i * P:(i + 1) * P],
                                              o[:, s % 2, j * P:(j + 1) * P], t.ident[:])
                        mm.then_inc(s_tr, 1)
                    for half in range(2):
                        c = 2 * s + half
                        pe.wait_ge(s_ot, c + 1)
                        if c >= 2:
                            pe.wait_ge(s_yt, c - 1)
                        pe.matmul(t.PS[:, 6 + half, :], wo[:], ot[:, c * CH:(c + 1) * CH], start=True,
                                  stop=True).then_inc(s_y, 1)

            @block.scalar
            def _(act):
                act.wait_ge(s_v, 1)
                act.activation(nrm[:], n2[:], ACT.Sqrt).then_inc(s_act, 1)
                act.activation(qkv[:, :, W:COLS], qkv[:, :, W:COLS], ACT.Sigmoid).then_inc(s_act, 1)
                for c in range(NCH):
                    act.wait_ge(s_tr, c + 1)
                    act.activation(ot[:, c * CH:(c + 1) * CH], t.PS[:, 4 + c % 2, :], ACT.Copy).then_inc(s_ot, 1)

            @block.vector
            def _(dve):
                v = 0

                def done(instruction):
                    nonlocal v
                    v += 1
                    instruction.then_inc(s_v, 1)
                    dve.wait_ge(s_v, v)

                def by_head(ap):
                    return ap.rearrange("p i (h e) -> p i h e", e=HD)

                dve.wait_ge(s_in, 64)
                for i in range(NT):
                    dve.wait_ge(s_p, i + 1)
                    dve.tensor_tensor(qkv[:, i], t.PS[:, i % 4, 0:COLS], bias[:], ALU.add).then_inc(s_qkv, 1)
                dve.wait_ge(s_qkv, NT)
                for half, buf in ((0, prod), (1, sv)):
                    tl = slice(half * NT // 2, (half + 1) * NT // 2)
                    sq = buf[:].rearrange("p a b -> p (a b)").rearrange("p (i f) -> p i f", f=2 * P)
                    dve.tensor_tensor(sq, qkv[:, tl, Q:V], qkv[:, tl, Q:V], ALU.mult).then_inc(s_s, 1)
                for half, buf in ((0, prod), (1, sv)):
                    tl = slice(half * NT // 2, (half + 1) * NT // 2)
                    sq = buf[:].rearrange("p a b -> p (a b)").rearrange("p (i f) -> p i f", f=2 * P)
                    dve.wait_ge(s_s, half + 1)
                    last = dve.tensor_reduce(n2[:, tl], by_head(sq), AX, ALU.add)
                done(last)
                dve.wait_ge(s_act, 2)
                done(dve.tensor_scalar(nrm[:], nrm[:], 1e-18, None, ALU.max))
                done(dve.reciprocal(rec[:], nrm[:]))
                done(dve.tensor_tensor(rec[:], rec[:], n2[:], ALU.mult))
                done(dve.tensor_tensor(nrm[:], nrm[:], rec[:], ALU.add))
                done(dve.tensor_scalar(nrm[:], nrm[:], 0.5, 1e-12, ALU.mult, ALU.max))
                done(dve.reciprocal(rec[:], nrm[:]))
                done(dve.tensor_tensor(by_head(qkv[:, :, Q:V]), by_head(qkv[:, :, Q:V]),
                                       rec[:].unsqueeze(3).broadcast_to((P, NT, 2 * HEADS, HD)), ALU.mult))
                done(dve.tensor_tensor(by_head(qkv[:, :, V:W]), by_head(qkv[:, :, V:W]),
                                       qkv[:, :, W:R].unsqueeze(3).broadcast_to((P, NT, HEADS, HD)), ALU.mult))

                def finish(s):
                    dve.wait_ge(s_sv, s + 1)
                    if s >= 2:
                        dve.wait_ge(s_tr, 2 * (s - 1))
                    out = o[:, s % 2]
                    done(dve.tensor_reduce(out, sv[:].rearrange("p s f -> p f s"), AX, ALU.add))
                    tl = slice(s * TILES, (s + 1) * TILES)
                    out4 = out.rearrange("p (i h e) -> p i h e", h=HEADS, e=HD)
                    dve.tensor_tensor(out4, out4, qkv[:, tl, R:COLS].unsqueeze(3).broadcast_to((P, TILES, HEADS, HD)),
                                      ALU.mult).then_inc(s_o, 1)

                def gated(c):
                    dve.wait_ge(s_y, c + 1)
                    dve.tensor_scalar(t.YT[:, c * CH:(c + 1) * CH], t.PS[:, 6 + c % 2, :], bo[:, 0:1],
                                      t.MOD[:, 3, GATE_A, c // 2:c // 2 + 1], ALU.add, ALU.mult).then_inc(s_yt, 1)

                for s in range(BATCH):
                    q = qkv[:, s * TILES:(s + 1) * TILES, Q:K]
                    for s2 in range(BATCH):
                        last = dve.tensor_tensor(prod[:, s2].rearrange("p (i f) -> p i f", f=P), q,
                                                 qkv[:, s2 * TILES:(s2 + 1) * TILES, K:V], ALU.mult)
                    done(last)
                    if s:
                        dve.wait_ge(s_sv, s)
                    dve.tensor_reduce(score[:], prod[:].rearrange("p s (h e) -> p (s h) e", e=HD), AX,
                                      ALU.add).then_inc(s_s, 1)
                    dve.wait_ge(s_s, s + 3)
                    if s:
                        finish(s - 1)
                    dve.sem_inc(s_v, 1)
                    v += 1
                    if s >= 2:
                        gated(2 * (s - 2))
                        gated(2 * (s - 2) + 1)
                finish(BATCH - 1)
                for c in range(2 * (BATCH - 2), NCH):
                    gated(c)

            @block.gpsimd
            def _(pool):
                FIRST, EACH = 9, 3
                for s in range(BATCH):
                    pool.wait_ge(s_s, s + 3)
                    pool.wait_ge(s_v, FIRST + 2 + EACH * s)
                    pool.tensor_tensor(sv[:].rearrange("p s (h e) -> p (s h) e", e=HD),
                                       qkv[:, :, V:W].rearrange("p i (h e) -> p i h e", e=HD),
                                       bcast(score[:], HD), ALU.mult).then_inc(s_sv, 1)


def causal_attention(nc, t, sem, name, layer, w_d, rows, rope_d, bias_d, down_d, scale):
    J, GROUPS = 4, HEADS // 4
    NS = 8 * J
    KEYS = [4, 8]
    NV0, NV = KEYS[0] * J, sum(KEYS) * J
    s_in, s_cst, s_cv = sem(f"{name}_loaded"), sem(f"{name}_values_cleared"), sem(f"{name}_constants")
    s_pj, s_pv0 = sem(f"{name}_projected"), sem(f"{name}_values_projected")
    s_a, s_d = sem(f"{name}_batch_scalar_steps"), sem(f"{name}_batch_vector_steps")
    s_vt = sem(f"{name}_values_transposed")
    s_pool = sem(f"{name}_group_staged")
    s_st = sem(f"{name}_stacked")
    s_qa, s_qd = sem(f"{name}_stacks_by_scalar"), sem(f"{name}_stacks_by_vector")
    s_S = sem(f"{name}_scores")
    s_mx = sem(f"{name}_maxima")
    s_P = sem(f"{name}_probabilities")
    s_T = sem(f"{name}_blocks_transposed")
    s_ed, s_ea = sem(f"{name}_blocks_by_vector"), sem(f"{name}_blocks_by_scalar")
    s_pv = sem(f"{name}_values_weighted")
    s_at = sem(f"{name}_heads_copied")
    s_att = sem(f"{name}_heads_transposed")
    s_rc, s_o = sem(f"{name}_sums_inverted"), sem(f"{name}_heads_normalised")
    s_ot, s_oc, s_y = sem(f"{name}_rows_transposed"), sem(f"{name}_rows_copied"), sem(f"{name}_output")
    s_yt = sem(f"{name}_gated")
    s_bt = sem(f"{name}_batch_stages")
    s_r, s_g = sem(f"{name}_rotary_products"), sem(f"{name}_gelu")
    biased = bias_d is not None
    with ExitStack() as ctx:
        def sb(n, s, dt=F32):
            return ctx.enter_context(nc.sbuf_tensor(f"{name}_{n}", s, dt))
        w, rope = sb("w", [P, 6, P]), sb("rope", [P, 2, SEQ])
        bias, wd, bd = sb("bias", [P, 6]), sb("wd", [P, 32]), sb("bd", [32, 1])
        high, low = sb("high", [P, 2, SEQ], F32R), sb("low", [P, 2, SEQ], F32R)
        rot = t.YT[:, 3 * SEQ:4 * SEQ].rearrange("p (r f) -> p r f", r=2)
        pick_f, picks = t.YT[:, SEQ:SEQ + 4 * GROUPS * P], sb("picks", [P, GROUPS, 4, P], BF16)
        vT, vb = sb("vT", [P, SEQ]), sb("vb", [P, TILES, P])
        pick, head = sb("pick", [P, 4, P], F32R), sb("head", [P, J])
        mask_f, mask = sb("mask_f", [P, P]), sb("mask", [P, P], BF16)
        ident_bf = sb("identb", [P, P], BF16)
        vst = sb("vst", [P, TILES, J, 32])
        qs, ks = sb("qs", [P, J, SEQ], F32R), sb("ks", [P, SEQ], F32R)
        probs = [[sb(f"p{c}_{i}", [P, J, (4 * c + i + 1) * P]) for i in range(4)] for c in range(2)]
        nmax = sb("nmax", [P, NS])
        blk = sb("blk", [P, 4, CH])
        latent = blk[0:32, 2:4, :].rearrange("p a f -> p (a f)")
        at, rec = sb("at", [P, CH]), sb("rec", [P, 4, J])
        o = sb("o", [P, TILES, P])
        score_ps = [t.PS[:, 2 * k:2 * k + 2, :].rearrange("p b f -> p (b f)") for k in range(2)]
        blk_ps = [t.PS[:, 4 + k, :] for k in range(2)]
        at_ps, tr_ps = t.PS[:, 6, :], t.PS[:, 7, :]

        def tile_of(n):
            return n // J, n % J

        order = [("S", 0, n) for n in range(4 * J)]
        for n in range(4 * J):
            order += [("S", 1, n), ("T", 0, n)]
        order += [("T", 1, m) for m in range(KEYS[1] * J)]

        def block_of(c, m):
            kt, j = m // J, m % J
            return kt, j, max(0, kt - 4 * c), (NV0 if c else 0) + m

        NA = 8 if biased else 6
        with nc.Block() as block:
            @block.sync
            def _(sp):
                sp.dma_start(w[:], w_d).then_inc(s_in, 16)
                sp.dma_start(rope[:], rope_d).then_inc(s_in, 16)
                sp.dma_start(pick_f, rows["picks"]).then_inc(s_in, 16)
                sp.dma_start(head[:], rows["head_rows"]).then_inc(s_in, 16)
                sp.dma_start(mask_f[:], rows["causal"]).then_inc(s_in, 16)
                if biased:
                    sp.dma_start(bias[:], bias_d[0]).then_inc(s_in, 16)
                    sp.dma_start(wd[:], down_d).then_inc(s_in, 16)
                    sp.dma_start(bd[:], bias_d[1]).then_inc(s_in, 16)
            LOADED = 16 * (8 if biased else 5)

            @block.gpsimd
            def _(pool):
                pool.memset(vst[:], 0.0).then_inc(s_cst, 1)
                pool.wait_ge(s_cst, 1)
                pool.memset(vst[:, :, :, HD:HD + 1], 1.0).then_inc(s_cst, 1)
                pool.wait_ge(s_cst, 2)
                pool.wait_ge(s_cv, 3)
                with pool.Fori(0, BATCH) as b:
                    with pool.Fori(0, GROUPS) as g:
                        it = b * GROUPS + g
                        pool.wait_ge(s_st, it + 1)
                        pool.tensor_copy(pick[:], picks[:, bass.ds(g, 1)].rearrange("p a k f -> p (a k) f")).then_inc(s_pool, 1)
                        pool.wait_ge(s_vt, b + 1)
                        pool.wait_ge(s_pv, it * NV + 4)
                        pool.tensor_copy(vst[:, :, :, 0:HD],
                                         vb[:, :, bass.ds(g * J * HD, J * HD)].rearrange("p i (j e) -> p i j e", e=HD)).then_inc(s_pool, 1)

            @block.tensor
            def _(pe):
                pe.wait_ge(s_in, LOADED)
                pe.wait_ge(s_cst, 2)
                pe.wait_ge(s_cv, 3)
                with pe.Fori(0, BATCH) as b:
                    for c in range(2):
                        x = t.HT[:, bass.ds(b * SEQ + c * CH, CH)]
                        pe.wait_ge(s_P, b * GROUPS * NS + 2)
                        for r in range(2):
                            if c:
                                pe.wait_ge(s_d, b * 8 + 2 * r + 2)
                            for k in range(2):
                                mm = pe.matmul(t.PS[:, 2 * r + k, :], w[:, 2 * r + k, :], x, start=True, stop=True)
                            mm.then_inc(s_pj, 1)
                    for c in range(2):
                        x = t.HT[:, bass.ds(b * SEQ + c * CH, CH)]
                        pe.wait_ge(s_o, b * GROUPS * 2 + 1)
                        if biased:
                            pe.sem_inc(s_bt, 1)
                            pe.matmul(t.PS[0:32, 6 + c, :], wd[:], x, start=True, stop=True).then_inc(s_pv0, 1)
                        else:
                            pe.matmul(t.PS[:, 6 + c, :], w[:, 4, :], x, start=True, stop=True).then_inc(s_pv0, 1)
                    if biased:
                        for c in range(2):
                            pe.wait_ge(s_a, b * NA + 5 + c)
                            pe.matmul(t.PS[:, 6 + c, :], w[0:32, 4, :], latent[:, c * CH:(c + 1) * CH],
                                      start=True, stop=True).then_inc(s_pv0, 1)
                    for c in range(2):
                        pe.wait_ge(s_a, b * NA + NA - 1 + c)
                        for i in range(4):
                            mm = pe.transpose(t.PS[:, 6 + c, i * P:(i + 1) * P],
                                              vT[:, (4 * c + i) * P:(4 * c + i + 1) * P], t.ident[:])
                        mm.then_inc(s_ot, 1)
                    pe.wait_ge(s_d, b * 8 + 8)
                    pe.sem_inc(s_bt, 1)
                    with pe.Fori(0, GROUPS) as g:
                        it = b * GROUPS + g
                        pe.wait_ge(s_pool, it * 2 + 1)
                        pe.wait_ge(s_P, it * NS + 2)
                        for r in range(2):
                            for c in range(2):
                                pe.matmul(t.PS[:, 2 * r + c, :], pick[:, 2 * r, :], high[:, r, c * CH:(c + 1) * CH],
                                          start=True, stop=False)
                                mm = pe.matmul(t.PS[:, 2 * r + c, :], pick[:, 2 * r + 1, :],
                                               low[:, r, c * CH:(c + 1) * CH], start=False, stop=True)
                        mm.then_inc(s_st, 1)
                        pe.wait_ge(s_qa, it * 3 + 3)
                        pe.wait_ge(s_qd, it * 2 + 2)
                        pe.wait_ge(s_pool, it * 2 + 2)
                        pending = []

                        def weigh(c, m):
                            kt, j, i0, n = block_of(c, m)
                            if m == 0:
                                pe.wait_ge(s_at, it * 2 + c + 1)
                            ready = s_ea if n % 2 else s_ed
                            pe.wait_ge(ready, it * (NV // 2) + n // 2 + 2)
                            pe.matmul(at_ps[32 * j:32 * j + 32, i0 * P:], vst[:, kt, j, :], blk[:, n % 4, i0 * P:],
                                      start=(kt == 0), stop=(kt == KEYS[c] - 1), skip_group_check=True).then_inc(s_pv, 1)

                        def heads_back(c):
                            pe.wait_ge(s_at, it * 2 + c + 2)
                            pe.wait_ge(s_o, it * 2 + c + 1)
                            for i in range(4):
                                mm = pe.transpose(tr_ps[:, i * P:(i + 1) * P], at[:, i * P:(i + 1) * P], t.ident[:])
                            mm.then_inc(s_att, 1)

                        for what, c, n in order:
                            if what == "S":
                                i, j = tile_of(n)
                                q = 4 * c + i
                                N = 4 * J * c + n
                                width = (q + 1) * P
                                pe.wait_ge(s_P, it * NS + N + 1)
                                for k0 in range(0, width, CH):
                                    k1 = min(width, k0 + CH)
                                    pe.matmul(score_ps[N % 2][:, k0:k1], qs[:, j, q * P:(q + 1) * P], ks[:, k0:k1],
                                              start=True, stop=(k1 < width))
                                pe.matmul(score_ps[N % 2][:, q * P:width], ident_bf[:], mask[:], start=False,
                                          stop=True).then_inc(s_S, 1)
                                continue
                            kt, j, i0, m = block_of(c, n)
                            if n == 0:
                                pe.wait_ge(s_P, it * NS + 4 * J * (c + 1) + 2)
                            free = s_ea if m % 2 else s_ed
                            pe.wait_ge(free, it * (NV // 2) + m // 2 + 1)
                            for i in range(i0, 4):
                                mm = pe.transpose(blk_ps[m % 2][:, i * P:(i + 1) * P],
                                                  probs[c][i][:, j, kt * P:(kt + 1) * P], t.ident[:])
                            mm.then_inc(s_T, 1)
                            pending.append((c, n))
                            if len(pending) > 2:
                                done = pending.pop(0)
                                weigh(*done)
                                if done == (1, 0):
                                    heads_back(0)
                        while pending:
                            weigh(*pending.pop(0))
                        heads_back(1)
                    for c in range(2):
                        pe.wait_ge(s_o, (b + 1) * GROUPS * 2 + 1)
                        for i in range(4):
                            mm = pe.transpose(t.PS[:, 6 + c, i * P:(i + 1) * P], o[:, 4 * c + i, :], t.ident[:])
                        mm.then_inc(s_ot, 1)
                    for c in range(2):
                        pe.wait_ge(s_oc, b * 2 + c + 1)
                        pe.matmul(t.PS[:, 6 + c, :], w[:, 5, :], vT[:, c * CH:(c + 1) * CH], start=True,
                                  stop=True).then_inc(s_y, 1)
                    pe.wait_ge(s_yt, b * 2 + 2)

            @block.scalar
            def _(act):
                act.sem_inc(s_ea, 1)
                act.wait_ge(s_in, LOADED)
                with act.Fori(0, BATCH) as b:
                    for c in range(2):
                        part = slice(c * CH, (c + 1) * CH)
                        for r in range(2):
                            if biased:
                                act.wait_ge(s_d, b * 8 + 4 * c + 2 * r + 1)
                                act.activation(rot[:, r], rot[:, r], ACT.Gelu).then_inc(s_g, 1)
                                act.wait_ge(s_g, b * 4 + 2 * c + r + 1)
                            else:
                                act.wait_ge(s_d, b * 8 + 4 * c + 2 * r + 1)
                            act.activation(high[:, r, part], rot[:, r], ACT.Copy, scale=scale if r == 0 else 1.0).then_inc(s_a, 1)
                    if biased:
                        for c in range(2):
                            act.wait_ge(s_pv0, b * 4 + c + 1)
                            act.activation(latent[:, c * CH:(c + 1) * CH], t.PS[0:32, 6 + c, :], ACT.Gelu,
                                           bias=bd[:, 0:1]).then_inc(s_a, 1)
                    for c in range(2):
                        act.wait_ge(s_pv0, b * (4 if biased else 2) + (2 if biased else 0) + c + 1)
                        a = act.activation(vT[:, c * CH:(c + 1) * CH], t.PS[:, 6 + c, :],
                                           ACT.Identity if biased else ACT.Copy,
                                           **({"bias": bias[:, 4:5]} if biased else {}))
                        a.then_inc(s_a, 1)
                    with act.Fori(0, GROUPS) as g:
                        it = b * GROUPS + g
                        act.wait_ge(s_st, it + 2)
                        act.wait_ge(s_S, it * NS + 1)
                        act.activation(ks[:], score_ps[1], ACT.Copy).then_inc(s_qa, 1)
                        act.wait_ge(s_qd, it * 2 + 2)
                        for j in (2, 3):
                            act.activation(qs[:, j], score_ps[0], ACT.Copy, scale=head[:, j:j + 1]).then_inc(s_qa, 1)
                        for what, c, n in order:
                            if what == "S":
                                i, j = tile_of(n)
                                N = 4 * J * c + n
                                if n == 0:
                                    act.wait_ge(s_T, it * NV + (NV if c else NV0))
                                act.wait_ge(s_mx, it * NS + N + 1)
                                width = (4 * c + i + 1) * P
                                act.activation(probs[c][i][:, j, :], score_ps[N % 2][:, 0:width], ACT.Exp,
                                               bias=nmax[:, N:N + 1]).then_inc(s_P, 1)
                                continue
                            kt, j, i0, m = block_of(c, n)
                            if m % 2:
                                act.wait_ge(s_T, NV + it * NV + m + 1)
                                act.wait_ge(s_pv, it * NV + m + 1)
                                act.activation(blk[:, m % 4, i0 * P:], blk_ps[1][:, i0 * P:], ACT.Copy).then_inc(s_ea, 1)
                    for c in range(2):
                        act.wait_ge(s_ot, b * 4 + 2 + c + 1)
                        act.activation(vT[:, c * CH:(c + 1) * CH], t.PS[:, 6 + c, :], ACT.Copy).then_inc(s_oc, 1)

            @block.vector
            def _(dve):
                dve.sem_inc(s_st, 1)
                dve.sem_inc(s_S, 1)
                dve.sem_inc(s_P, 2)
                dve.sem_inc(s_T, NV)
                dve.sem_inc(s_ed, 1)
                dve.sem_inc(s_pv, 4)
                dve.sem_inc(s_at, 1)
                dve.sem_inc(s_o, 1)
                dve.wait_ge(s_in, LOADED)
                dve.tensor_copy(picks[:].rearrange("p g k f -> p (g k f)"), pick_f).then_inc(s_cv, 1)
                dve.tensor_copy(mask[:], mask_f[:]).then_inc(s_cv, 1)
                dve.tensor_copy(ident_bf[:], t.ident[:]).then_inc(s_cv, 1)
                dve.wait_ge(s_cv, 3)
                with dve.Fori(0, BATCH) as b:
                    for c in range(2):
                        part = slice(c * CH, (c + 1) * CH)
                        for r in range(2):
                            x_ps, r_ps = t.PS[:, 2 * r, :], t.PS[:, 2 * r + 1, :]
                            dve.wait_ge(s_pj, b * 4 + 2 * c + r + 1)
                            if c:
                                dve.wait_ge(s_a, b * NA + r + 1)
                            if biased:
                                dve.scalar_tensor_tensor(rot[:, r], x_ps, bias[:, 2 * r:2 * r + 1], rope[:, 0, part],
                                                         ALU.add, ALU.mult).then_inc(s_r, 1)
                                dve.scalar_tensor_tensor(blk[:, r], r_ps, bias[:, 2 * r + 1:2 * r + 2], rope[:, 1, part],
                                                         ALU.add, ALU.mult).then_inc(s_r, 1)
                            else:
                                dve.tensor_tensor(rot[:, r], x_ps, rope[:, 0, part], ALU.mult).then_inc(s_r, 1)
                                dve.tensor_tensor(blk[:, r], r_ps, rope[:, 1, part], ALU.mult).then_inc(s_r, 1)
                            dve.wait_ge(s_r, b * 8 + 4 * c + 2 * r + 2)
                            dve.tensor_tensor(rot[:, r], rot[:, r], blk[:, r], ALU.add).then_inc(s_d, 1)
                            dve.wait_ge(s_d, b * 8 + 4 * c + 2 * r + 1)
                            dve.wait_ge(s_a, b * NA + 2 * c + r + 1)
                            dve.scalar_tensor_tensor(low[:, r, part], rot[:, r], scale if r == 0 else 1.0,
                                                     high[:, r, part].bitcast(F32), ALU.mult, ALU.subtract).then_inc(s_d, 1)
                    for c in range(2):
                        dve.wait_ge(s_ot, b * 4 + c + 1)
                        last = dve.tensor_copy(vb[:, 4 * c:4 * c + 4, :], t.PS[:, 6 + c, :].rearrange("p (i f) -> p i f", f=P))
                    last.then_inc(s_vt, 1)
                    with dve.Fori(0, GROUPS) as g:
                        it = b * GROUPS + g
                        dve.wait_ge(s_st, it + 2)
                        dve.wait_ge(s_S, it * NS + 1)
                        for j in (0, 1):
                            dve.tensor_scalar(qs[:, j], score_ps[0], head[:, j:j + 1], None, ALU.mult).then_inc(s_qd, 1)

                        def heads_out(c):
                            dve.wait_ge(s_pv, 4 + it * NV + (NV if c else NV0))
                            dve.tensor_copy(at[:], at_ps).then_inc(s_at, 1)

                        def normalise(c):
                            dve.wait_ge(s_att, it * 2 + c + 1)
                            got = tr_ps.rearrange("p (i j e) -> p i j e", j=J, e=32)
                            dve.reciprocal(rec[:], got[:, :, :, HD]).then_inc(s_rc, 1)
                            dve.wait_ge(s_rc, it * 2 + c + 1)
                            dst = o[:, 4 * c:4 * c + 4, bass.ds(g * J * HD, J * HD)].rearrange("p i (j e) -> p i j e", e=HD)
                            dve.tensor_tensor(dst, got[:, :, :, 0:HD], rec[:].unsqueeze(3).broadcast_to((P, 4, J, HD)),
                                              ALU.mult).then_inc(s_o, 1)

                        for what, c, n in order:
                            if what == "S":
                                i, j = tile_of(n)
                                N = 4 * J * c + n
                                width = (4 * c + i + 1) * P
                                dve.wait_ge(s_S, 1 + it * NS + N + 1)
                                dve.tensor_reduce(nmax[:, N:N + 1], score_ps[N % 2][:, 0:width], AX, ALU.max,
                                                  negate=True).then_inc(s_mx, 1)
                                continue
                            kt, j, i0, m = block_of(c, n)
                            if m % 2 == 0:
                                dve.wait_ge(s_T, NV + it * NV + m + 1)
                                dve.wait_ge(s_pv, it * NV + m + 1)
                                dve.tensor_copy(blk[:, m % 4, i0 * P:], blk_ps[0][:, i0 * P:]).then_inc(s_ed, 1)
                            if c == 1 and n == 0:
                                heads_out(0)
                            if c == 1 and n == 6:
                                normalise(0)
                        heads_out(1)
                        normalise(1)
                    for c in range(2):
                        dve.wait_ge(s_y, b * 2 + c + 1)
                        y = t.YT[:, bass.ds(b * SEQ + c * CH, CH)]
                        dve.tensor_scalar(y, t.PS[:, 6 + c, :], bias[:, 5:6] if biased else 0.0,
                                          t.MOD[:, layer, GATE_A, bass.ds(b, 1)], ALU.add, ALU.mult).then_inc(s_yt, 1)


def attention1(nc, t, sem, d):
    causal_attention(nc, t, sem, "a1", 1, d["L1_attn_w"], d, d["L1_rope"], None, None, HD ** -0.5)


def attention2(nc, t, sem, d):
    causal_attention(nc, t, sem, "a2", 2, d["L2_attn_w"], d, d["L2_rope"], (d["L2_attn_b"], d["L2_latent_b"]),
                     d["L2_down"], HD ** -0.5)


def attention0(nc, t, sem, d):
    WIDE = 64
    PAIRS = HEADS // 2
    NS, NB = 8, 16
    scale = WIDE ** -0.5
    s_wq, s_wv, s_wo = sem("a0_qk_weights_loaded"), sem("a0_v_weights_loaded"), sem("a0_output_weights_loaded")
    s_one = sem("a0_ones_ready")
    s_hb = sem("a0_batch_inputs_copied")
    s_pj, s_hi, s_lo = sem("a0_projected"), sem("a0_high_parts"), sem("a0_low_parts")
    s_vp, s_vd, s_va = sem("a0_values"), sem("a0_values_by_vector"), sem("a0_values_by_scalar")
    s_S, s_mx = sem("a0_scores"), sem("a0_maxima")
    s_P = sem("a0_probabilities")
    s_T = sem("a0_blocks_transposed")
    s_ed, s_ea = sem("a0_blocks_by_vector"), sem("a0_blocks_by_scalar")
    s_pv = sem("a0_values_weighted")
    s_rc = sem("a0_sums_inverted")
    s_dg = sem("a0_diagonals")
    s_rb = sem("a0_inverse_sums_spread")
    s_sp = sem("a0_inverse_sums_copied")
    s_at = sem("a0_heads_normalised")
    s_ge, s_y, s_yt, s_z = sem("a0_gelu"), sem("a0_output"), sem("a0_gated"), sem("a0_input_added")
    with ExitStack() as ctx:
        def sb(n, s, dt=F32):
            return ctx.enter_context(nc.sbuf_tensor(f"a0_{n}", s, dt))
        wqk, wv, wo = sb("wqk", [P, 2, 2, P]), sb("wv", [P, P]), sb("wo", [P, PAIRS, P])
        ones = sb("ones", [P, WIDE])
        hb = sb("hb", [P, SEQ])
        qs, kh, kl = (sb(n, [P, 2, SEQ], F32R) for n in ("qs", "kh", "kl"))
        vst = sb("vst", [P, TILES, P])
        probs = [sb(f"p{c}", [P, 2, 4, SEQ]) for c in range(2)]
        nmax, sums, rec = sb("nmax", [P, 2 * NS]), sb("sums", [P, 2, NS]), sb("rec", [P, 2, NS])
        diag = sb("diag", [P, NS, P])
        spread = sb("spread", [P, CH])
        blk = sb("blk", [P, 4, CH])
        at = sb("at", [P, PAIRS, SEQ])
        score_ps = [t.PS[:, 2 * k:2 * k + 2, :].rearrange("p b f -> p (b f)") for k in range(2)]
        blk_ps = [t.PS[:, 4 + k, :] for k in range(2)]
        at_ps, rec_ps = t.PS[:, 6, :], t.PS[:, 7, :]

        first, second = [], []
        for kt in range(TILES):
            first += [("B", kt), ("S", kt)]
            second += [("B", kt)] + ([("P", kt)] if kt < 4 else [("S", 2 * kt - 8), ("S", 2 * kt - 7)])
        orders = [first, second]

        with nc.Block() as block:
            @block.sync
            def _(sp):
                sp.dma_start(wqk[:], d["L0_qk"][0]).then_inc(s_wq, 16)
                sp.dma_start(wv[:], d["L0_v"][0]).then_inc(s_wv, 16)
                sp.dma_start(wo[:], d["L0_post"]).then_inc(s_wo, 16)
                with sp.Fori(0, BATCH) as b:
                    with sp.Fori(0, PAIRS) as p:
                        it = b * PAIRS + p
                        sp.wait_ge(s_pj, it * 4 + 4)
                        sp.dma_start(wqk[:].rearrange("p h r f -> p (h r f)"),
                                     d["L0_qk"][bass.ds(p + 1, 1)].rearrange("a p h r f -> p (a h r f)")).then_inc(s_wq, 16)
                        sp.wait_ge(s_vp, it * 2 + 3)
                        sp.dma_start(wv[:], d["L0_v"][bass.ds(p + 1, 1)].rearrange("a p f -> p (a f)")).then_inc(s_wv, 16)
                sp.wait_ge(s_wv, 16 * (BATCH * PAIRS + 1))

            @block.gpsimd
            def _(pool):
                pool.sem_inc(s_rb, 1)
                pool.sem_inc(s_dg, 2)
                pool.memset(ones[:], 1.0).then_inc(s_one, 1)
                with pool.Fori(0, BATCH * PAIRS) as it:
                    for c in range(2):
                        pool.wait_ge(s_rc, it * 2 + c + 2)
                        pool.wait_ge(s_rb, it * 2 + c + 1)
                        pool.tensor_tensor(diag[:], t.ident[:].unsqueeze(1).broadcast_to((P, NS, P)),
                                           bcast(rec[:, c], P), ALU.mult).then_inc(s_dg, 1)

            @block.tensor
            def _(pe):
                def project(J, k, offset):
                    if k == 0:
                        pe.wait_ge(s_wq, 16 * (J + 1))
                    h, r = k // 2, k % 2
                    if k < 2:
                        pe.wait_ge(s_P, J * 2 * NS + 2)
                    else:
                        pe.wait_ge(s_lo, J * 4 + k - 1)
                    for c in range(2):
                        mm = pe.matmul(score_ps[r][:, c * CH:(c + 1) * CH], wqk[:, h, r, :],
                                       t.HT[:, bass.ds(offset + c * CH, CH)], start=True, stop=True)
                    mm.then_inc(s_pj, 1)

                def score(J, c, n):
                    j, i = n // 4, n % 4
                    if c == 0 and n < 2:
                        pe.wait_ge(s_lo, J * 4 + n + 3)
                    pe.wait_ge(s_P, J * 2 * NS + NS * c + n + 1)
                    q = qs[:, j, (4 * c + i) * P:(4 * c + i + 1) * P]
                    for part in (kh, kl):
                        for g in range(2):
                            mm = pe.matmul(score_ps[n % 2][:, g * CH:(g + 1) * CH], q, part[:, j, g * CH:(g + 1) * CH],
                                           start=(part is kh), stop=(part is kl))
                    mm.then_inc(s_S, 1)

                def weigh(it, c, kt):
                    U = 2 * it + c
                    if kt == 0:
                        pe.wait_ge(s_at, U + 1)
                        pe.wait_ge(s_vd, it + 1)
                        pe.wait_ge(s_va, it + 1)
                    pe.wait_ge(s_ed, U * TILES + kt + 2)
                    pe.wait_ge(s_ea, U * TILES + kt + 2)
                    for j in range(2):
                        pe.matmul(at_ps[WIDE * j:WIDE * (j + 1), :], vst[:, kt, WIDE * j:WIDE * (j + 1)],
                                  blk[:, 2 * (kt % 2) + j, :], start=(kt == 0), stop=(kt == TILES - 1),
                                  skip_group_check=True).then_inc(s_pv, 1)

                def blocks(it, c, kt):
                    U = 2 * it + c
                    if kt == 0:
                        pe.wait_ge(s_P, U * NS + NS + 2)
                    for j in range(2):
                        if kt == 0 and c == 0:
                            pe.wait_ge((s_vd, s_va)[j], it + 1)
                        pe.wait_ge((s_ed, s_ea)[j], U * TILES + kt + 1)
                        for i in range(4):
                            mm = pe.transpose(blk_ps[j][:, i * P:(i + 1) * P],
                                              probs[c][:, j, i, kt * P:(kt + 1) * P], t.ident[:])
                        mm.then_inc(s_T, 1)
                    if kt:
                        weigh(it, c, kt - 1)

                pe.wait_ge(s_one, 1)
                for k in range(4):
                    project(0, k, 0)
                for n in range(NS):
                    score(0, 0, n)
                with pe.Fori(0, BATCH) as b:
                    with pe.Fori(0, PAIRS) as p:
                        it = b * PAIRS + p
                        after = ((it + 1) // PAIRS) % BATCH * SEQ
                        pe.wait_ge(s_hb, b + 1)
                        pe.wait_ge(s_wv, 16 * (it + 1))
                        for g in range(2):
                            pe.wait_ge((s_ed, s_ea)[g], it * 2 * TILES + 1)
                            for i in range(4):
                                mm = pe.matmul(blk_ps[g][:, i * P:(i + 1) * P], hb[:, (4 * g + i) * P:(4 * g + i + 1) * P],
                                               wv[:], start=True, stop=True)
                            mm.then_inc(s_vp, 1)
                        for c in range(2):
                            for what, n in orders[c]:
                                if what == "B":
                                    blocks(it, c, n)
                                elif what == "P":
                                    project(it + 1, n, after)
                                elif c == 0:
                                    score(it, 1, n)
                                else:
                                    score(it + 1, 0, n)
                            weigh(it, c, TILES - 1)
                            pe.wait_ge(s_dg, it * 2 + c + 3)
                            for j in range(2):
                                mm = pe.matmul(rec_ps[WIDE * j:WIDE * (j + 1), :], ones[:],
                                               diag[:, 4 * j:4 * j + 4, :].rearrange("p i f -> p (i f)"),
                                               start=True, stop=True, skip_group_check=True)
                            mm.then_inc(s_rb, 1)
                    pe.wait_ge(s_wo, 16)
                    for k in range(PAIRS):
                        pe.wait_ge(s_ge, b * PAIRS + k + 1)
                        for c in range(2):
                            mm = pe.matmul(t.PS[:, 6 + c, :], wo[:, k, :], at[:, k, c * CH:(c + 1) * CH],
                                           start=(k == 0), stop=(k == PAIRS - 1))
                    mm.then_inc(s_y, 1)
                    pe.wait_ge(s_z, b * 2 + 2)

            @block.scalar
            def _(act):
                def split_high(J, k):
                    h, r = k // 2, k % 2
                    act.wait_ge(s_pj, J * 4 + k + 1)
                    dst = (qs, kh)[r][:, h, :]
                    act.activation(dst, score_ps[r], ACT.Copy, scale=scale if r == 0 else 1.0).then_inc(s_hi, 1)

                def exponentiate(J, c, n):
                    j, i = n // 4, n % 4
                    act.wait_ge(s_mx, J * 2 * NS + NS * c + n + 1)
                    act.activation(probs[c][:, j, i, :], score_ps[n % 2], ACT.Exp,
                                   bias=nmax[:, NS * c + n:NS * c + n + 1],
                                   accum_out=sums[:, c, n:n + 1]).then_inc(s_P, 1)

                act.sem_inc(s_P, 2)
                act.sem_inc(s_ea, 1)
                for k in range(4):
                    split_high(0, k)
                for n in range(NS):
                    exponentiate(0, 0, n)
                with act.Fori(0, BATCH) as b:
                    act.wait_ge(s_vp, b * PAIRS * 2 + 1)
                    act.activation(hb[:], t.HT[:, bass.ds(b * SEQ, SEQ)], ACT.Copy).then_inc(s_hb, 1)
                    with act.Fori(0, PAIRS) as p:
                        it = b * PAIRS + p
                        act.wait_ge(s_vp, it * 2 + 3)
                        act.wait_ge(s_pv, it * 2 * NB + 4)
                        act.activation(vst[:, 4:8, :].rearrange("p i f -> p (i f)"), blk_ps[1], ACT.Copy).then_inc(s_va, 1)
                        for c in range(2):
                            U = 2 * it + c
                            for what, n in orders[c]:
                                if what == "B":
                                    m = U * NB + 2 * n + 1
                                    act.wait_ge(s_T, m + 1 + 2 * NB)
                                    act.wait_ge(s_pv, m + 1)
                                    act.activation(blk[:, 2 * (n % 2) + 1, :], blk_ps[1], ACT.Copy).then_inc(s_ea, 1)
                                elif what == "P":
                                    split_high(it + 1, n)
                                elif c == 0:
                                    if n == 0:
                                        act.wait_ge(s_T, it * 2 * NB + 2 * NB)
                                        act.wait_ge(s_rc, it * 2 + 1)
                                    exponentiate(it, 1, n)
                                else:
                                    if n == 0:
                                        act.wait_ge(s_T, it * 2 * NB + 3 * NB)
                                        act.wait_ge(s_rc, it * 2 + 2)
                                    exponentiate(it + 1, 0, n)
                    act.wait_ge(s_at, (b + 1) * PAIRS * 2 + 1)
                    for k in range(PAIRS):
                        act.activation(at[:, k, :], at[:, k, :], ACT.Gelu).then_inc(s_ge, 1)

            @block.vector
            def _(dve):
                def split_low(J, k):
                    h, r = k // 2, k % 2
                    dve.wait_ge(s_hi, J * 4 + k + 1)
                    if r == 0:
                        rows = qs[WIDE:, h, :]
                        dve.scalar_tensor_tensor(rows, score_ps[0][WIDE:], scale, rows.bitcast(F32), ALU.mult,
                                                 ALU.subtract).then_inc(s_lo, 1)
                    else:
                        dve.tensor_tensor(kl[:, h, :], score_ps[1], kh[:, h, :].bitcast(F32),
                                          ALU.subtract).then_inc(s_lo, 1)

                def maximum(J, c, n):
                    dve.wait_ge(s_S, J * 2 * NS + NS * c + n + 1)
                    dve.tensor_reduce(nmax[:, NS * c + n:NS * c + n + 1], score_ps[n % 2], AX, ALU.max,
                                      negate=True).then_inc(s_mx, 1)

                def invert_sums(it, c):
                    U = 2 * it + c
                    dve.wait_ge(s_P, U * NS + NS + 2)
                    dve.wait_ge(s_dg, U + 1)
                    dve.reciprocal(rec[:, c], sums[:, c]).then_inc(s_rc, 1)

                def normalise(it, p, c):
                    dve.wait_ge(s_rb, it * 2 + c + 2)
                    dve.wait_ge(s_at, it * 2 + c + 1)
                    dve.tensor_copy(spread[:], rec_ps).then_inc(s_sp, 1)
                    dve.wait_ge(s_sp, it * 2 + c + 1)
                    dve.tensor_tensor(at[:, bass.ds(p, 1), c * CH:(c + 1) * CH].rearrange("p a f -> p (a f)"),
                                      at_ps, spread[:], ALU.mult).then_inc(s_at, 1)

                dve.sem_inc(s_vp, 1)
                dve.sem_inc(s_T, 2 * NB)
                dve.sem_inc(s_ed, 1)
                dve.sem_inc(s_pv, 4)
                dve.sem_inc(s_rc, 1)
                dve.sem_inc(s_at, 1)
                for k in range(4):
                    split_low(0, k)
                for n in range(NS):
                    maximum(0, 0, n)
                with dve.Fori(0, BATCH) as b:
                    with dve.Fori(0, PAIRS) as p:
                        it = b * PAIRS + p
                        dve.wait_ge(s_vp, it * 2 + 2)
                        dve.wait_ge(s_pv, it * 2 * NB + 4)
                        dve.tensor_copy(vst[:, 0:4, :].rearrange("p i f -> p (i f)"), blk_ps[0]).then_inc(s_vd, 1)
                        for c in range(2):
                            U = 2 * it + c
                            for what, n in orders[c]:
                                if what == "B":
                                    m = U * NB + 2 * n
                                    dve.wait_ge(s_T, m + 1 + 2 * NB)
                                    dve.wait_ge(s_pv, m + 1)
                                    dve.tensor_copy(blk[:, 2 * (n % 2), :], blk_ps[0]).then_inc(s_ed, 1)
                                    if n == 0:
                                        if c == 1:
                                            normalise(it, p, 0)
                                        invert_sums(it, c)
                                elif what == "P":
                                    split_low(it + 1, n)
                                elif c == 0:
                                    maximum(it, 1, n)
                                else:
                                    maximum(it + 1, 0, n)
                        normalise(it, p, 1)
                    dve.wait_ge(s_y, b + 1)
                    for c in range(2):
                        y = t.YT[:, bass.ds(b * SEQ + c * CH, CH)]
                        dve.tensor_tensor(y, t.PS[:, 6 + c, :], t.HT[:, bass.ds(b * SEQ + c * CH, CH)],
                                          ALU.add).then_inc(s_z, 1)
                    for c in range(2):
                        dve.wait_ge(s_z, b * 2 + c + 1)
                        y = t.YT[:, bass.ds(b * SEQ + c * CH, CH)]
                        dve.tensor_scalar(y, y, t.MOD[:, 0, GATE_A, bass.ds(b, 1)], None, ALU.mult).then_inc(s_yt, 1)


def program(nc, d, out):
    with ExitStack() as ctx:
        def sb(name, shape, dt=F32):
            return ctx.enter_context(nc.sbuf_tensor(name, shape, dt))

        in_use = []

        def sem(name):
            in_use.append(nc.alloc_semaphore(name))
            return in_use[-1]

        def clear_semaphores():
            nc.clear_and_free_semaphores(in_use)
            nc.all_engine_barrier()
            in_use.clear()

        t = Memory()
        t.X, t.HT, t.YT = sb("X", [P, NT, P]), sb("HT", [P, TOK]), sb("YT", [P, TOK])
        t.MOD, t.iota8 = sb("MOD", [P, LAYERS, 6, BATCH]), sb("iota8", [P, EXPERTS])
        t.ident, t.ident_bf = sb("ident", [P, P]), sb("ident_bf", [P, P], BF16)
        t.PS = ctx.enter_context(nc.psum_tensor("PS", [P, 8, CH], F32))

        def L0_attn():
            norm_transpose(nc, t, sem, "a0", 0, SHIFT_A, SCALE_A)
            attention0(nc, t, sem, d)
            residual(nc, t, sem, "a0")

        def L0_ffn():
            norm_transpose(nc, t, sem, "f0", 0, SHIFT_B, SCALE_B)
            ffn0(nc, t, sem, d)
            residual(nc, t, sem, "f0")

        def L1_attn():
            norm_transpose(nc, t, sem, "a1", 1, SHIFT_A, SCALE_A)
            attention1(nc, t, sem, d)
            residual(nc, t, sem, "a1")

        def L1_ffn():
            norm_transpose(nc, t, sem, "f1", 1, SHIFT_B, SCALE_B)
            ffn1(nc, t, sem, d)
            residual(nc, t, sem, "f1")

        def L2_attn():
            norm_transpose(nc, t, sem, "a2", 2, SHIFT_A, SCALE_A)
            attention2(nc, t, sem, d)
            residual(nc, t, sem, "a2")

        def L2_ffn():
            norm_transpose(nc, t, sem, "f2", 2, SHIFT_B, SCALE_B)
            ffn2(nc, t, sem, d)
            residual(nc, t, sem, "f2")

        def L3_attn():
            norm_transpose(nc, t, sem, "a3", 3, SHIFT_A, SCALE_A)
            attention3(nc, t, sem, d)
            residual(nc, t, sem, "a3")

        def L3_ffn():
            norm_transpose(nc, t, sem, "f3", 3, SHIFT_B, SCALE_B)
            ffn3(nc, t, sem, d)
            residual(nc, t, sem, "f3", store=out)

        load_and_modulation(nc, t, sem, d)
        every = [L0_attn, L0_ffn, L1_attn, L1_ffn, L2_attn, L2_ffn, L3_attn, L3_ffn]
        for sublayer in every:
            sublayer()
            clear_semaphores()


def layout(inputs):
    import numpy as np

    def a(name):
        return np.asarray(inputs[name])

    def c(x):
        return np.ascontiguousarray(x)

    out = {"L0_attn_X": c(a("L0_attn_X")),
           "c_T": c(np.concatenate([a(f"L{l}_c") for l in range(LAYERS)]).T)}
    for l in range(LAYERS):
        out[f"L{l}_wmod"] = c(a(f"L{l}_wmod"))
    out["ident"] = np.eye(P, dtype=np.float32)
    out["iota8"] = np.tile(np.arange(EXPERTS, dtype=np.float32), (P, 1))
    sel = np.zeros((P, 2 * EXPERTS, P), np.float32)
    for e in range(EXPERTS):
        for k in range(3):
            sel[k * EXPERTS + e, e] = 1.0
        sel[3 * EXPERTS + e, EXPERTS + e] = 1.0
    out["gate_rows"] = sel
    def heads(name):
        return a(name).reshape(P, 8, 2, 64).transpose(1, 0, 2, 3)
    wrap = np.arange(9) % 8
    qk = np.stack([heads("L0_attn_Wq"), heads("L0_attn_Wk")], 3)
    out["L0_qk"] = c(np.concatenate([qk, qk], 4)[wrap])
    out["L0_v"] = c(a("L0_attn_Wv").reshape(P, 8, P).transpose(1, 0, 2)[wrap])
    out["L0_post"] = c(a("L0_attn_Wpost").reshape(8, P, P).transpose(1, 0, 2))
    out["L0_router"] = c(a("L0_ffn_router_w").T)
    out["L0_w1"] = c(a("L0_ffn_w1"))
    out["L0_w2"] = c(a("L0_ffn_w2"))
    out["L1_router"] = c(a("L1_ffn_gate_w").T)
    out["L1_w"] = c(np.stack([a("L1_ffn_w1").transpose(0, 2, 1), a("L1_ffn_w3").transpose(0, 2, 1),
                              a("L1_ffn_w2").transpose(0, 2, 1)], 2))
    out["L1_b"] = c(np.stack([a("L1_ffn_b1"), a("L1_ffn_b3"), a("L1_ffn_b2")], 2))
    out["L1_shared"] = c(np.concatenate([a("L1_ffn_sw1").T.reshape(P, 2, P), a("L1_ffn_sw2").T.reshape(P, 2, P),
                                         a("L1_ffn_sw3").T.reshape(2, P, P).transpose(1, 0, 2)], 1))
    gens = a("L2_ffn_gens")
    out["L2_gens"] = c(np.stack([gens, gens.transpose(0, 2, 1)], 1).reshape(2 * ROTATIONS, P, P).transpose(1, 0, 2))
    table = np.stack([THETA * 2.0 ** np.arange(SQUARINGS + 1), 2.0 ** -np.arange(SQUARINGS + 1)])
    table[0, -1] = 3e38
    out["expm_table"] = c(np.broadcast_to(table.astype(np.float32), (P, 2, SQUARINGS + 1)))
    out["L2_norm"] = c(np.stack([a("L2_ffn_ln_gamma"), a("L2_ffn_ln_beta")], 1))
    out["L2_router"] = c(a("L2_ffn_moe_gate_w"))
    out["L2_router_b"] = c(a("L2_ffn_moe_gate_b"))[None]
    out["L2_w1"] = c(a("L2_ffn_ew1"))
    out["L2_b1"] = c(a("L2_ffn_eb1").reshape(EXPERTS, 2, P).transpose(0, 2, 1))
    out["L2_w2"] = c(a("L2_ffn_ew2"))
    out["L2_b2"] = c(a("L2_ffn_eb2"))[:, :, None]
    out["L2_abel_w"] = c(a("L2_ffn_abel_w"))
    out["L2_abel_b"] = c(a("L2_ffn_abel_b"))[:, None]
    out["L2_mix_w"] = c(a("L2_ffn_gc_w").reshape(2, P).T)
    out["L2_mix_b"] = c(a("L2_ffn_gc_b"))[None]
    out["head_rows"] = np.kron(np.eye(4, dtype=np.float32), np.ones((32, 1), np.float32))
    out["causal"] = np.triu(np.full((P, P), -3e38, np.float32), 1)
    picks = np.zeros((P, HEADS // 4, 4, P), np.float32)
    terms = ([0, 1], [2, 3], [0, 2], [1, 3])
    for h in range(HEADS):
        for kind, places in enumerate(terms):
            for place in places:
                for e in range(HD):
                    picks[h * HD + e, h // 4, kind, 32 * (h % 4) + HD * place + e] = 1.0
    out["picks"] = picks.reshape(P, -1)
    f = np.arange(P)

    def rope(inverse_frequency, minus):
        angle = np.arange(SEQ, dtype=np.float32)[None, :] * inverse_frequency[:, None]
        return c(np.stack([np.cos(angle), np.where(minus[:, None], -np.sin(angle), np.sin(angle))], 1))

    one = np.float32(10000.0) ** (-np.arange(HD // 2, dtype=np.float32) * np.float32(2.0) / np.float32(HD))
    out["L1_rope"] = rope(one[(f % HD) // 2], f % 2 == 0)
    q, k = a("L1_attn_Wq").T, a("L1_attn_Wk").T
    out["L1_attn_w"] = c(np.stack([q, q[:, f ^ 1], k, k[:, f ^ 1], a("L1_attn_Wv").T, a("L1_attn_Wo").T], 1))
    two = np.float32(1.0) / np.float32(10000.0) ** (np.arange(0, P, 2, dtype=np.float32) / np.float32(P))
    out["L2_rope"] = rope(two[f % (P // 2)], f < P // 2)
    swap = (f + P // 2) % P
    q, k = a("L2_attn_wqr"), a("L2_attn_wkr")
    v = np.zeros((P, P), np.float32)
    v[0:32] = a("L2_attn_wv")
    out["L2_attn_w"] = c(np.stack([q, q[:, swap], k, k[:, swap], v, a("L2_attn_wo")], 1))
    qb, kb = a("L2_attn_bqr"), a("L2_attn_bkr")
    out["L2_attn_b"] = c(np.stack([qb, qb[swap], kb, kb[swap], a("L2_attn_bv"), a("L2_attn_bo")], 1))
    out["L2_down"] = c(a("L2_attn_wkv"))
    out["L2_latent_b"] = c(a("L2_attn_bkv"))[:, None]
    names = ("Wq", "Wk", "Wv", "Ww", "Wr")
    out["L3_qkvwr"] = c(np.concatenate([a(f"L3_attn_{n}_w").T for n in names], 1))
    out["L3_qkvwr_b"] = c(np.concatenate([a(f"L3_attn_{n}_b") for n in names]))[None]
    out["L3_wo"] = c(a("L3_attn_Wo_w").T)
    out["L3_bo"] = c(a("L3_attn_Wo_b"))[:, None]
    out["L3_router"] = c(a("L3_ffn_gate_w").T)
    out["L3_router_b"] = c(a("L3_ffn_gate_b"))[None]
    out["L3_w1"] = c(a("L3_ffn_w1").transpose(0, 2, 1))
    out["L3_b1"] = c(a("L3_ffn_b1").reshape(EXPERTS, 4, P).transpose(0, 2, 1))
    out["L3_w2"] = c(a("L3_ffn_w2").transpose(0, 2, 1))
    out["L3_b2"] = c(a("L3_ffn_b2"))[:, :, None]
    return out


def kernel(**inputs):
    import numpy as _np
    import concourse.bacc as _bacc
    from concourse.bass_utils import run_bass_kernel_spmd as _run

    arrays = {f"in_{k}": v for k, v in layout(inputs).items()}
    nc = _bacc.Bacc("TRN2", target_bir_lowering=False, num_devices=1)
    d = {k[3:]: nc.dram_tensor(k, v.shape, mybir.dt.from_np(v.dtype), kind="ExternalInput").ap()
         for k, v in arrays.items()}
    out = nc.dram_tensor("out", (BATCH, SEQ, P), F32, kind="ExternalOutput").ap()
    program(nc, d, out)
    r = _run(nc, [arrays], core_ids=[0])
    return _np.asarray(r.results[0]["out"])
```

```python
from contextlib import ExitStack

import concourse.bass as bass
from concourse import mybir

F32 = mybir.dt.float32
F32R = mybir.dt.float32r
BF16 = mybir.dt.bfloat16
I32 = mybir.dt.int32
U32 = mybir.dt.uint32
ALU = mybir.AluOpType
ACT = mybir.ActivationFunctionType
AX = mybir.AxisListType.X

P = 128
BATCH = 4
SEQ = 1024
TILES = SEQ // P
NT = BATCH * TILES
TOK = BATCH * SEQ
LAYERS = 4
CH = 512
NCH = TOK // CH
EXPERTS = 8
EPS = 1e-5
SHIFT_A, SCALE_A, GATE_A, SHIFT_B, SCALE_B, GATE_B = range(6)


class Memory:
    pass


def bcast(ap, n):
    return ap.unsqueeze(2).broadcast_to((*ap.shape, n))


def load_and_modulation(nc, t, sem, d):
    s_c = sem("mod_inputs_loaded")
    s_silu = sem("mod_silu_ready")
    s_mm = sem("mod_products_ready")
    s_v = sem("mod_vector_steps")
    s_once = sem("resident_loaded")
    with ExitStack() as ctx:
        cT = ctx.enter_context(nc.sbuf_tensor("cT", [P, LAYERS * BATCH], F32))
        cs = ctx.enter_context(nc.sbuf_tensor("c_silu", [P, LAYERS * BATCH], F32))
        wmod = ctx.enter_context(nc.sbuf_tensor("wmod_all", [P, LAYERS, 6 * P], F32))
        sign = ctx.enter_context(nc.sbuf_tensor("gate_sign", [P, LAYERS, 2, BATCH], F32))
        size = ctx.enter_context(nc.sbuf_tensor("gate_size", [P, LAYERS, 2, BATCH], F32))
        mod_ps = t.PS[:, 0, 0:LAYERS * 6 * BATCH]
        gates = t.MOD[:, :, GATE_A:GATE_B + 1:3, :]
        scales = t.MOD[:, :, SCALE_A:SCALE_B + 1:3, :]
        with nc.Block() as block:
            @block.sync
            def _(sp):
                sp.dma_start(cT[:], d["c_T"]).then_inc(s_c, 16)
                for l in range(LAYERS):
                    sp.dma_start(wmod[:, l, :], d[f"L{l}_wmod"]).then_inc(s_c, 16)
                for b in range(BATCH):
                    sp.dma_start(t.X[:, b * TILES:(b + 1) * TILES, :],
                                 d["L0_attn_X"][b].rearrange("(i p) f -> p i f", p=P)).then_inc(s_once, 16)
                sp.dma_start(t.ident[:], d["ident"]).then_inc(s_once, 16)
                sp.wait_ge(s_once, 16 * (BATCH + 1))

            @block.scalar
            def _(act):
                act.wait_ge(s_c, 16 * (1 + LAYERS))
                act.activation(cs[:], cT[:], ACT.Silu).then_inc(s_silu, 1)

            @block.tensor
            def _(pe):
                pe.wait_ge(s_c, 16 * (1 + LAYERS))
                pe.wait_ge(s_silu, 1)
                for l in range(LAYERS):
                    for j in range(6):
                        mm = pe.matmul(mod_ps[:, (l * 6 + j) * BATCH:(l * 6 + j + 1) * BATCH],
                                       wmod[:, l, j * P:(j + 1) * P], cs[:, l * BATCH:(l + 1) * BATCH],
                                       start=True, stop=True)
                mm.then_inc(s_mm, 1)

            @block.vector
            def _(dve):
                dve.wait_ge(s_mm, 1)
                dve.tensor_copy(t.MOD[:], mod_ps.rearrange("p (l j b) -> p l j b", l=LAYERS, j=6)).then_inc(s_v, 1)
                dve.wait_ge(s_v, 1)
                dve.tensor_scalar(scales, scales, 1.0, None, ALU.add).then_inc(s_v, 1)
                dve.tensor_scalar(sign[:], gates, 0.0, 2.0, ALU.is_ge, ALU.mult).then_inc(s_v, 1)
                dve.scalar_tensor_tensor(size[:], gates, -1.0, gates, ALU.mult, ALU.max).then_inc(s_v, 1)
                dve.wait_ge(s_v, 4)
                dve.tensor_scalar(sign[:], sign[:], -1.0, None, ALU.add).then_inc(s_v, 1)
                dve.wait_ge(s_v, 5)
                dve.scalar_tensor_tensor(gates, size[:], 0.25, sign[:], ALU.max, ALU.mult).then_inc(s_v, 1)
                dve.wait_ge(s_v, 6)


def norm_transpose(nc, t, sem, name, layer, shift, scale, load=None):
    add = not t.first
    t.first = False
    s_yt = sem(f"{name}_res_transposed")
    s_add = sem(f"{name}_res_added")
    s_st, s_mv = sem(f"{name}_ln_statistics"), sem(f"{name}_ln_mean_variance")
    s_var, s_v = sem(f"{name}_ln_variance"), sem(f"{name}_ln_vector_steps")
    s_sd = sem(f"{name}_ln_deviation")
    s_xn = sem(f"{name}_ln_normalised")
    s_tr = sem(f"{name}_ln_transposed")
    s_ht = sem(f"{name}_ln_modulated")
    half = TILES // 2
    STEPS = 6
    with ExitStack() as ctx:
        xn = t.YT[:].rearrange("p (i f) -> p i f", f=P)
        st = ctx.enter_context(nc.sbuf_tensor(f"{name}_st", [P, NT, 6], F32))
        mv = ctx.enter_context(nc.sbuf_tensor(f"{name}_mv", [P, NT, 2], F32))
        sc = ctx.enter_context(nc.sbuf_tensor(f"{name}_sc", [P, 5, NT], F32))
        VAR, SD, RS, SQR, TMP = range(5)
        with nc.Block() as block:
            if load is not None:
                @block.sync
                def _(sp):
                    load(sp)

            @block.vector
            def _(dve):
                def statistics(b):
                    if add:
                        for c in (2 * b, 2 * b + 1):
                            dve.wait_ge(s_yt, c + 1)
                            x = t.X[:, c * half:(c + 1) * half, :]
                            dve.tensor_tensor(x, t.PS[:, c % 4, :].rearrange("p (i f) -> p i f", f=P), x,
                                              ALU.add).then_inc(s_add, 1)
                        dve.wait_ge(s_add, 2 * b + 2)
                    for i in range(b * TILES, (b + 1) * TILES):
                        dve.bn_stats(st[:, i, :], t.X[:, i, :]).then_inc(s_st, 1)

                def mean_variance(b):
                    dve.wait_ge(s_st, (b + 1) * TILES)
                    for i in range(b * TILES, (b + 1) * TILES):
                        dve.bn_aggr(mv[:, i, :], st[:, i, :]).then_inc(s_mv, 1)
                    dve.wait_ge(s_mv, (b + 1) * TILES)
                    tl = slice(b * TILES, (b + 1) * TILES)
                    dve.tensor_scalar(sc[:, VAR, tl], mv[:, tl, 1], EPS, None, ALU.add).then_inc(s_var, 1)

                def normalise(b):
                    tl = slice(b * TILES, (b + 1) * TILES)
                    v = b * STEPS

                    def done(instruction):
                        nonlocal v
                        v += 1
                        instruction.then_inc(s_v, 1)
                        dve.wait_ge(s_v, v)
                    dve.wait_ge(s_sd, b + 1)
                    done(dve.reciprocal(sc[:, RS, tl], sc[:, SD, tl]))
                    done(dve.tensor_tensor(sc[:, SQR, tl], sc[:, RS, tl], sc[:, RS, tl], ALU.mult))
                    done(dve.tensor_tensor(sc[:, SQR, tl], sc[:, SQR, tl], sc[:, VAR, tl], ALU.mult))
                    done(dve.tensor_scalar(sc[:, TMP, tl], sc[:, SQR, tl], -0.5, 1.5, ALU.mult, ALU.add))
                    done(dve.tensor_tensor(sc[:, RS, tl], sc[:, RS, tl], sc[:, TMP, tl], ALU.mult))
                    done(dve.tensor_copy(sc[:, SQR, tl], mv[:, tl, 0]))
                    for i in range(b * TILES, (b + 1) * TILES):
                        dve.tensor_scalar(xn[:, i, :], t.X[:, i, :], sc[:, SQR, i:i + 1], sc[:, RS, i:i + 1],
                                          ALU.subtract, ALU.mult).then_inc(s_xn, 1)

                for b in range(BATCH):
                    statistics(b)
                    mean_variance(b)
                    if b:
                        normalise(b - 1)
                normalise(BATCH - 1)

            @block.scalar
            def _(act):
                def modulate(b):
                    for c in (2 * b, 2 * b + 1):
                        act.wait_ge(s_tr, c + 1)
                        act.activation(t.HT[:, c * CH:(c + 1) * CH], t.PS[:, 4 + c % 4, :], ACT.Identity,
                                       bias=t.MOD[:, layer, shift, b:b + 1],
                                       scale=t.MOD[:, layer, scale, b:b + 1]).then_inc(s_ht, 1)
                for b in range(BATCH):
                    act.wait_ge(s_var, b + 1)
                    tl = slice(b * TILES, (b + 1) * TILES)
                    act.activation(sc[:, SD, tl], sc[:, VAR, tl], ACT.Sqrt).then_inc(s_sd, 1)
                    if b > 1:
                        modulate(b - 2)
                modulate(BATCH - 2)
                modulate(BATCH - 1)

            @block.tensor
            def _(pe):
                def turn_back(b):
                    for c in (2 * b, 2 * b + 1):
                        if c >= 4:
                            pe.wait_ge(s_add, c - 3)
                        for i in range(half):
                            mm = pe.transpose(t.PS[:, c % 4, i * P:(i + 1) * P],
                                              t.YT[:, (c * half + i) * P:(c * half + i + 1) * P], t.ident[:])
                        mm.then_inc(s_yt, 1)

                def turn(b):
                    for c in (2 * b, 2 * b + 1):
                        pe.wait_ge(s_xn, (c + 1) * half)
                        if c >= 4:
                            pe.wait_ge(s_ht, c - 3)
                        for i in range(half):
                            mm = pe.transpose(t.PS[:, 4 + c % 4, i * P:(i + 1) * P], xn[:, c * half + i, :], t.ident[:])
                        mm.then_inc(s_tr, 1)

                if add:
                    turn_back(0)
                for b in range(BATCH):
                    if add and b + 1 < BATCH:
                        turn_back(b + 1)
                    if b:
                        turn(b - 1)
                turn(BATCH - 1)


def last_residual(nc, t, sem, out):
    s_tr, s_add, s_out = sem("last_transposed"), sem("last_added"), sem("last_stored")
    half = TILES // 2
    with nc.Block() as block:
        @block.tensor
        def _(pe):
            for c in range(NCH):
                if c >= 4:
                    pe.wait_ge(s_add, c - 3)
                for i in range(half):
                    mm = pe.transpose(t.PS[:, c % 4, i * P:(i + 1) * P],
                                      t.YT[:, (c * half + i) * P:(c * half + i + 1) * P], t.ident[:])
                mm.then_inc(s_tr, 1)

        @block.vector
        def _(dve):
            for c in range(NCH):
                dve.wait_ge(s_tr, c + 1)
                x = t.X[:, c * half:(c + 1) * half, :]
                dve.tensor_tensor(x, t.PS[:, c % 4, :].rearrange("p (i f) -> p i f", f=P), x,
                                  ALU.add).then_inc(s_add, 1)

        @block.sync
        def _(sp):
            for c in range(NCH):
                b, h = c // 2, c % 2 * (SEQ // 2)
                sp.wait_ge(s_add, c + 1)
                sp.dma_start(out[b, h:h + SEQ // 2].rearrange("(i p) f -> p i f", p=P),
                             t.X[:, c * half:(c + 1) * half, :]).then_inc(s_out, 16)
            sp.wait_ge(s_out, 16 * NCH)


GATE_ROWS = 4 * EXPERTS
TOP2_SOFTMAX, SOFTMAX_TOP2, TOP1 = range(3)


def route(nc, t, sem, name, src, router, bias, kind):
    s_lg = sem(f"{name}_logits")
    s_v = sem(f"{name}_route_vector_steps")
    s_e = sem(f"{name}_route_exponentials")
    s_tr = sem(f"{name}_route_transposed")
    s_gt = sem(f"{name}_route_copied")
    s_parts = sem(f"{name}_route_parts_ready")
    shape = [P, NT, EXPERTS]
    with ExitStack() as ctx:
        def sb(n, s, dt=F32):
            return ctx.enter_context(nc.sbuf_tensor(f"{name}_{n}", s, dt))
        lg, rest = sb("lg", shape), sb("rest", shape)
        top, first, second = sb("top", shape), sb("first", shape), sb("second", shape)
        where, wheref = sb("where", shape, U32), sb("wheref", [P, NT, 2])
        w = sb("w", shape)
        ratio, total, share = sb("ratio", [P, NT]), sb("total", [P, NT]), sb("share", [P, NT])
        g = sb("g", [P, NT, 4, EXPERTS], BF16)
        logits_ps = t.PS[:, 0, 0:NT * EXPERTS].rearrange("p (i e) -> p i e", e=EXPERTS)
        gt_ps = [t.PS[:, 1 + b, :].bitcast(BF16) for b in range(BATCH)]
        with nc.Block() as block:
            @block.tensor
            def _(pe):
                for i in range(NT):
                    mm = pe.matmul(logits_ps[:, i, :], src[:, i * P:(i + 1) * P], router, start=True, stop=True)
                mm.then_inc(s_lg, 1)
                pe.wait_ge(s_parts, 1)
                for b in range(BATCH):
                    for i in range(TILES):
                        mm = pe.transpose(gt_ps[b][0:GATE_ROWS, i * P:(i + 1) * P],
                                          g[:, b * TILES + i].rearrange("p k e -> p (k e)"), t.ident_bf[:])
                    mm.then_inc(s_tr, 1)

            @block.scalar
            def _(act):
                if kind == SOFTMAX_TOP2:
                    act.wait_ge(s_v, 3)
                    act.activation(lg[:], lg[:], ACT.Exp).then_inc(s_e, 1)
                if kind == TOP2_SOFTMAX:
                    act.wait_ge(s_v, 3)
                    act.activation(ratio[:], ratio[:], ACT.Exp).then_inc(s_e, 1)
                for b in range(BATCH):
                    act.wait_ge(s_tr, b + 1)
                    act.activation(t.GT[0:GATE_ROWS, b * SEQ:(b + 1) * SEQ], gt_ps[b][0:GATE_ROWS, 0:SEQ],
                                   ACT.Copy).then_inc(s_gt, 1)

            @block.vector
            def _(dve):
                v = 0

                def done(instruction):
                    nonlocal v
                    v += 1
                    instruction.then_inc(s_v, 1)
                    dve.wait_ge(s_v, v)

                dve.wait_ge(s_lg, 1)
                if bias is None:
                    done(dve.tensor_copy(lg[:], logits_ps))
                else:
                    done(dve.tensor_tensor(lg[:], logits_ps, bias.unsqueeze(1).broadcast_to(shape), ALU.add))
                if kind == SOFTMAX_TOP2:
                    done(dve.tensor_reduce(total[:], lg[:], AX, ALU.max))
                    done(dve.tensor_tensor(lg[:], lg[:], bcast(total[:], EXPERTS), ALU.subtract))
                    dve.wait_ge(s_e, 1)
                    done(dve.tensor_reduce(total[:], lg[:], AX, ALU.add))
                    done(dve.reciprocal(share[:], total[:]))
                    done(dve.tensor_tensor(lg[:], lg[:], bcast(share[:], EXPERTS), ALU.mult))
                last = None
                for i in range(NT):
                    last = dve.max(top[:, i], lg[:, i])
                if kind == TOP2_SOFTMAX:
                    done(last)
                    done(dve.tensor_tensor(ratio[:], top[:, :, 1], top[:, :, 0], ALU.subtract))
                else:
                    done(last)
                for i in range(NT):
                    last = dve.max_index(where[:, i], top[:, i], lg[:, i])
                done(last)
                done(dve.tensor_copy(wheref[:], where[:, :, 0:2]))
                places = t.iota8[:].unsqueeze(1).broadcast_to(shape)
                dve.tensor_tensor(first[:], places, bcast(wheref[:, :, 0], EXPERTS), ALU.is_equal)
                done(dve.tensor_tensor(second[:], places, bcast(wheref[:, :, 1], EXPERTS), ALU.is_equal))
                if kind == TOP1:
                    dve.memset(g[:, :, 0:3], 0.0)
                    dve.tensor_copy(g[:, :, 3], first[:]).then_inc(s_parts, 1)
                else:
                    if kind == TOP2_SOFTMAX:
                        dve.wait_ge(s_e, 1)
                        done(dve.tensor_scalar(total[:], ratio[:], 1.0, None, ALU.add))
                        done(dve.reciprocal(share[:], total[:]))
                        done(dve.tensor_tensor(total[:], ratio[:], share[:], ALU.mult))
                        done(dve.tensor_tensor(w[:], first[:], bcast(share[:], EXPERTS), ALU.mult))
                        done(dve.tensor_tensor(rest[:], second[:], bcast(total[:], EXPERTS), ALU.mult))
                        done(dve.tensor_tensor(w[:], w[:], rest[:], ALU.add))
                    done(dve.tensor_tensor(first[:], first[:], second[:], ALU.add))
                    if kind == SOFTMAX_TOP2:
                        done(dve.tensor_tensor(w[:], first[:], lg[:], ALU.mult))
                    dve.tensor_copy(g[:, :, 3], first[:])
                    done(dve.tensor_copy(g[:, :, 0], w[:]))
                    done(dve.tensor_tensor(rest[:], w[:], g[:, :, 0], ALU.subtract))
                    done(dve.tensor_copy(g[:, :, 1], rest[:]))
                    done(dve.tensor_tensor(w[:], rest[:], g[:, :, 1], ALU.subtract))
                    dve.tensor_copy(g[:, :, 2], w[:]).then_inc(s_parts, 1)


def experts(nc, t, sem, name, src, acc, hid, w1_d, w2_d, b1_d, b2_d, act_fn, gate_at):
    parts = hid // (2 * P)
    units = 2 * NCH
    n_w = 2 if b1_d is None else 4
    s_w = [sem(f"{name}_weights_loaded_{k}") for k in range(2)]
    s_free = sem(f"{name}_slots_reloaded")
    s_up = sem(f"{name}_first_products")
    s_relu = sem(f"{name}_relu")
    s_h = sem(f"{name}_hidden_ready")
    s_y = sem(f"{name}_second_products")
    s_gp = sem(f"{name}_gate_rows")
    s_g = sem(f"{name}_gates_ready")
    s_t = sem(f"{name}_gated")
    s_a = sem(f"{name}_added")
    with ExitStack() as ctx:
        def sb(n, s, dt=F32):
            return ctx.enter_context(nc.sbuf_tensor(f"{name}_{n}", s, dt))
        w1 = [sb(f"w1_{k}", [P, hid]) for k in range(2)]
        w2 = [sb(f"w2_{k}", [P, hid // P, P]) for k in range(2)]
        b1 = [sb(f"b1_{k}", [P, hid // P]) for k in range(2)]
        b2 = [sb(f"b2_{k}", [P, 1]) for k in range(2)]
        relu = sb("relu", [P, 2, 2, CH])
        h = sb("h", [P, 2, 2, CH])
        gate = sb("gate", [P, 2, CH])
        gated = sb("gated", [P, 2, CH])
        up_ps = [t.PS[:, 2 * k:2 * k + 2, :] for k in range(2)]
        g_ps = [t.PS[:, 4 + k, :] for k in range(2)]
        y_ps = [t.PS[:, 6 + k, :] for k in range(2)]
        with nc.Block() as block:
            @block.sync
            def _(sp):
                def load(e, k):
                    sp.dma_start(w1[k][:], w1_d[bass.ds(e, 1)].rearrange("a p f -> p (a f)")).then_inc(s_w[k], 16)
                    sp.dma_start(w2[k][:], w2_d[bass.ds(e, 1)].rearrange("a (j p) f -> p (a j) f", p=P)).then_inc(s_w[k], 16)
                    if b1_d is not None:
                        sp.dma_start(b1[k][:], b1_d[bass.ds(e, 1)].rearrange("a p j -> p (a j)")).then_inc(s_w[k], 16)
                        sp.dma_start(b2[k][:], b2_d[bass.ds(e, 1)].rearrange("a p o -> p (a o)")).then_inc(s_w[k], 16)
                for k in range(2):
                    load(k, k)
                with sp.Fori(0, EXPERTS // 2 - 1) as i:
                    for k in range(2):
                        sp.wait_ge(s_y, (2 * i + k + 1) * NCH * parts + 2)
                        sp.sem_inc(s_free, 1)
                        sp.wait_ge(s_t, (2 * i + k + 1) * NCH + 2)
                        load(2 * i + 2 + k, k)

            @block.tensor
            def _(pe):
                def up(i, u, part):
                    k, c, n = u // NCH, u % NCH, u * parts + part
                    if c == 0 and part == 0:
                        pe.wait_ge(s_w[k], 16 * n_w * (i + 1))
                    pe.wait_ge(s_h, i * units * parts + n + 1)
                    for j in range(2):
                        m = 2 * part + j
                        mm = pe.matmul(up_ps[n % 2][:, j, :], w1[k][:, m * P:(m + 1) * P],
                                       src[:, c * CH:(c + 1) * CH], start=True, stop=True)
                    mm.then_inc(s_up, 1)

                def spread(i, u):
                    k, c = u // NCH, u % NCH
                    pe.wait_ge(s_g, i * units + u + 1)
                    pe.matmul(g_ps[u % 2], t.Sel[:, bass.ds(i * 2 + k + gate_at, 1), :].rearrange("p a f -> p (a f)"),
                              t.GT[:, c * CH:(c + 1) * CH], start=True, stop=True).then_inc(s_gp, 1)

                def down(i, u, part):
                    k, n = u // NCH, u * parts + part
                    pe.wait_ge(s_h, i * units * parts + n + 3)
                    if part == 0:
                        pe.wait_ge(s_t, i * units + u + 1)
                    for j in range(2):
                        m = 2 * part + j
                        mm = pe.matmul(y_ps[u % 2], w2[k][:, m, :], h[:, n % 2, j, :],
                                       start=(m == 0), stop=(m == hid // P - 1))
                    mm.then_inc(s_y, 1)

                with pe.Fori(0, EXPERTS // 2) as i:
                    steps = [(u, part) for u in range(units) for part in range(parts)]
                    for n, (u, part) in enumerate(steps):
                        up(i, u, part)
                        if part == 0:
                            spread(i, u)
                        if n:
                            down(i, *steps[n - 1])
                    down(i, *steps[-1])

            @block.scalar
            def _(act):
                act.sem_inc(s_g, 2)
                with act.Fori(0, EXPERTS // 2) as i:
                    for u in range(units):
                        k = u // NCH
                        for part in range(parts):
                            n = u * parts + part
                            act.wait_ge(s_up, i * units * parts + n + 1)
                            if act_fn is None:
                                act.wait_ge(s_h, i * units * parts + n + 1)
                                act.activation(relu[:, n % 2], up_ps[n % 2], ACT.Relu).then_inc(s_relu, 1)
                            else:
                                act.wait_ge(s_y, i * units * parts + n + 1)
                                for j in range(2):
                                    m = 2 * part + j
                                    a = act.activation(h[:, n % 2, j, :], up_ps[n % 2][:, j, :], act_fn,
                                                       bias=b1[k][:, m:m + 1])
                                a.then_inc(s_h, 1)
                            if part == 0:
                                act.wait_ge(s_gp, i * units + u + 1)
                                act.wait_ge(s_t, i * units + u + 1)
                                act.activation(gate[:, u % 2], g_ps[u % 2], ACT.Copy).then_inc(s_g, 1)

            @block.vector
            def _(dve):
                dve.sem_inc(s_t, 2)
                dve.sem_inc(s_y, 2)
                dve.sem_inc(s_h, 2)

                def square(i, u, part):
                    n = u * parts + part
                    dve.wait_ge(s_relu, i * units * parts + n + 1)
                    dve.wait_ge(s_y, i * units * parts + n + 1)
                    dve.scalar_tensor_tensor(h[:, n % 2], up_ps[n % 2], 0.0, relu[:, n % 2], ALU.max,
                                             ALU.mult).then_inc(s_h, 1)

                def weigh(i, u):
                    dve.wait_ge(s_y, i * units * parts + (u + 1) * parts + 2)
                    dve.wait_ge(s_g, i * units + u + 3)
                    dve.wait_ge(s_a, i * units + u + 1)
                    if b2_d is None:
                        dve.tensor_tensor(gated[:, u % 2], y_ps[u % 2], gate[:, u % 2], ALU.mult).then_inc(s_t, 1)
                    else:
                        dve.scalar_tensor_tensor(gated[:, u % 2], y_ps[u % 2], b2[u // NCH][:, 0:1],
                                                 gate[:, u % 2], ALU.add, ALU.mult).then_inc(s_t, 1)

                with dve.Fori(0, EXPERTS // 2) as i:
                    for u in range(units):
                        for part in range(parts):
                            if act_fn is None:
                                square(i, u, part)
                        if u:
                            weigh(i, u - 1)
                    weigh(i, units - 1)

            @block.gpsimd
            def _(pool):
                pool.memset(acc[:], 0.0).then_inc(s_a, 2)
                with pool.Fori(0, EXPERTS // 2) as i:
                    for u in range(units):
                        c = u % NCH
                        pool.wait_ge(s_t, i * units + u + 3)
                        pool.wait_ge(s_a, i * units + u + 2)
                        part = acc[:, c * CH:(c + 1) * CH]
                        pool.tensor_tensor(part, part, gated[:, u % 2], ALU.add).then_inc(s_a, 1)


def gate_in_place(nc, t, sem, name, layer, gate):
    s = sem(f"{name}_gate_applied")
    with nc.Block() as block:
        @block.vector
        def _(dve):
            for b in range(BATCH):
                y = t.YT[:, b * SEQ:(b + 1) * SEQ]
                dve.tensor_scalar(y, y, t.MOD[:, layer, gate, b:b + 1], None, ALU.mult).then_inc(s, 1)
            dve.wait_ge(s, BATCH)


def open_gates(nc, t, sem, name, d, ctx, router, bias=None, norm=None):
    t.GT = ctx.enter_context(nc.sbuf_tensor(f"{name}_GT", [P, TOK], BF16))
    t.Sel = ctx.enter_context(nc.sbuf_tensor(f"{name}_Sel", [P, 2 * EXPERTS, P], BF16))
    router_sb = ctx.enter_context(nc.sbuf_tensor(f"{name}_router", [P, EXPERTS], F32))
    bias_sb = ctx.enter_context(nc.sbuf_tensor(f"{name}_router_b", [P, EXPERTS], F32))
    s = sem(f"{name}_gate_inputs_loaded")
    s_c, s_k = sem(f"{name}_gates_cleared"), sem(f"{name}_gate_constants_ready")
    with nc.sbuf_tensor(f"{name}_sel_f32", [P, 2 * EXPERTS, P], F32) as sel:
        def load(sp):
            sp.dma_start(router_sb[:], router).then_inc(s, 16)
            sp.dma_start(sel[:], d["gate_rows"]).then_inc(s, 16)
            sp.dma_start(t.iota8[:], d["iota8"]).then_inc(s, 16)
            if bias is not None:
                sp.dma_start(bias_sb[:], bias.broadcast_to((P, EXPERTS))).then_inc(s, 16)

        if norm is not None:
            norm(load)
        with nc.Block() as block:
            if norm is None:
                @block.sync
                def _(sp):
                    load(sp)

            @block.gpsimd
            def _(pool):
                pool.memset(t.GT[:], 0.0).then_inc(s_c, 1)
                pool.wait_ge(s_c, 1)

            @block.vector
            def _(dve):
                dve.wait_ge(s, 48 if bias is None else 64)
                dve.tensor_copy(t.ident_bf[:], t.ident[:]).then_inc(s_k, 1)
                dve.tensor_copy(t.Sel[:], sel[:]).then_inc(s_k, 1)
                dve.wait_ge(s_k, 2)
    return router_sb[:], None if bias is None else bias_sb[:]


def ffn0(nc, t, sem, d):
    with ExitStack() as ctx:
        router, _ = open_gates(nc, t, sem, "f0", d, ctx, d["L0_router"],
                               norm=lambda load: norm_transpose(nc, t, sem, "f0", 0, SHIFT_B, SCALE_B, load))
        route(nc, t, sem, "f0", t.HT, router, None, TOP2_SOFTMAX)
        experts(nc, t, sem, "f0", t.HT, t.YT, 2 * P, d["L0_w1"], d["L0_w2"], None, None, None, 0)
        gate_in_place(nc, t, sem, "f0", 0, GATE_B)


def ffn3(nc, t, sem, d):
    with ExitStack() as ctx:
        router, bias = open_gates(nc, t, sem, "f3", d, ctx, d["L3_router"], d["L3_router_b"],
                                  norm=lambda load: norm_transpose(nc, t, sem, "f3", 3, SHIFT_B, SCALE_B, load))
        route(nc, t, sem, "f3", t.HT, router, bias, TOP1)
        experts(nc, t, sem, "f3", t.HT, t.YT, 4 * P, d["L3_w1"], d["L3_w2"], d["L3_b1"], d["L3_b2"],
                ACT.Relu, EXPERTS)
        gate_in_place(nc, t, sem, "f3", 3, GATE_B)


def glu_experts(nc, t, sem, name, src, acc, w_d, b_d):
    units = 2 * NCH
    s_w = [sem(f"{name}_weights_loaded_{k}") for k in range(2)]
    s_gp = sem(f"{name}_gate_rows")
    s_g = sem(f"{name}_gates_ready")
    s_xs = sem(f"{name}_scaled_inputs")
    s_up = sem(f"{name}_first_products")
    s_h = sem(f"{name}_hidden_ready")
    s_x3 = sem(f"{name}_third_ready")
    s_y = sem(f"{name}_second_products")
    s_t = sem(f"{name}_products_taken")
    s_a = sem(f"{name}_added")
    with ExitStack() as ctx:
        def sb(n, s, dt=F32):
            return ctx.enter_context(nc.sbuf_tensor(f"{name}_{n}", s, dt))
        w = [sb(f"w_{k}", [P, 3, P]) for k in range(2)]
        bias = [sb(f"b_{k}", [P, 3]) for k in range(2)]
        gate = sb("gate", [P, 2, 2, CH])
        xs, h, x3, prod = sb("xs", [P, 2, CH]), sb("h", [P, 2, CH]), sb("x3", [P, 2, CH]), sb("prod", [P, 2, CH])
        up_ps = [t.PS[:, 2 * k:2 * k + 2, :] for k in range(2)]
        g_ps = t.PS[:, 4:6, :]
        y_ps = [t.PS[:, 6 + k, :] for k in range(2)]
        with nc.Block() as block:
            @block.sync
            def _(sp):
                def load(e, k):
                    sp.dma_start(w[k][:], w_d[bass.ds(e, 1)].rearrange("a p j f -> p (a j) f")).then_inc(s_w[k], 16)
                    sp.dma_start(bias[k][:], b_d[bass.ds(e, 1)].rearrange("a p j -> p (a j)")).then_inc(s_w[k], 16)
                for k in range(2):
                    load(k, k)
                with sp.Fori(0, EXPERTS // 2 - 1) as i:
                    for k in range(2):
                        sp.wait_ge(s_y, (2 * i + k + 1) * NCH + 2)
                        sp.wait_ge(s_t, (2 * i + k + 1) * NCH + 2)
                        load(2 * i + 2 + k, k)

            @block.tensor
            def _(pe):
                def spread(i, u, k, c):
                    pe.wait_ge(s_g, i * units + u + 1)
                    for m in range(2):
                        mm = pe.matmul(g_ps[:, m, :],
                                       t.Sel[:, bass.ds(i * 2 + k + m * EXPERTS, 1), :].rearrange("p a f -> p (a f)"),
                                       t.GT[:, c * CH:(c + 1) * CH], start=True, stop=True)
                    mm.then_inc(s_gp, 1)

                def up(i, u):
                    k = u // NCH
                    if u % NCH == 0:
                        pe.wait_ge(s_w[k], 32 * (i + 1))
                    pe.wait_ge(s_xs, i * units + u + 1)
                    pe.wait_ge(s_h, i * units + u + 1)
                    pe.wait_ge(s_x3, i * units + u + 1)
                    for m in range(2):
                        mm = pe.matmul(up_ps[u % 2][:, m, :], w[k][:, m, :], xs[:, u % 2, :], start=True, stop=True)
                    mm.then_inc(s_up, 1)

                def down(i, u):
                    pe.wait_ge(s_h, i * units + u + 3)
                    pe.wait_ge(s_t, i * units + u + 1)
                    pe.matmul(y_ps[u % 2], w[u // NCH][:, 2, :], h[:, u % 2, :], start=True, stop=True).then_inc(s_y, 1)

                with pe.Fori(0, EXPERTS // 2) as i:
                    spread(i, 0, 0, 0)
                    for u in range(units):
                        if u + 1 < units:
                            spread(i, u + 1, (u + 1) // NCH, (u + 1) % NCH)
                        up(i, u)
                        if u:
                            down(i, u - 1)
                    down(i, units - 1)

            @block.scalar
            def _(act):
                act.sem_inc(s_g, 1)
                act.sem_inc(s_h, 2)
                with act.Fori(0, EXPERTS // 2) as i:
                    def gates(u):
                        act.wait_ge(s_gp, i * units + u + 1)
                        act.wait_ge(s_x3, i * units + u + 1)
                        act.activation(gate[:, u % 2], g_ps, ACT.Copy).then_inc(s_g, 1)
                    gates(0)
                    for u in range(units):
                        if u + 1 < units:
                            gates(u + 1)
                        act.wait_ge(s_up, i * units + u + 1)
                        act.wait_ge(s_y, i * units + u + 1)
                        act.activation(h[:, u % 2], up_ps[u % 2][:, 0, :], ACT.Silu,
                                       bias=bias[u // NCH][:, 0:1]).then_inc(s_h, 1)

            @block.vector
            def _(dve):
                dve.sem_inc(s_x3, 2)
                dve.sem_inc(s_y, 2)
                dve.sem_inc(s_t, 2)
                with dve.Fori(0, EXPERTS // 2) as i:
                    def scaled(u):
                        c = u % NCH
                        dve.wait_ge(s_g, i * units + u + 2)
                        if u >= 2:
                            dve.wait_ge(s_up, i * units + u - 1)
                        dve.tensor_tensor(xs[:, u % 2], src[:, c * CH:(c + 1) * CH], gate[:, u % 2, 0],
                                          ALU.mult).then_inc(s_xs, 1)

                    def third(u):
                        dve.wait_ge(s_up, i * units + u + 1)
                        dve.wait_ge(s_t, i * units + u + 1)
                        dve.scalar_tensor_tensor(x3[:, u % 2], up_ps[u % 2][:, 1, :], bias[u // NCH][:, 1:2],
                                                 gate[:, u % 2, 1], ALU.add, ALU.mult).then_inc(s_x3, 1)

                    def combine(u):
                        dve.wait_ge(s_y, i * units + u + 3)
                        dve.wait_ge(s_x3, i * units + u + 3)
                        dve.wait_ge(s_a, i * units + u + 1)
                        dve.scalar_tensor_tensor(prod[:, u % 2], y_ps[u % 2], bias[u // NCH][:, 2:3],
                                                 x3[:, u % 2], ALU.add, ALU.mult).then_inc(s_t, 1)

                    scaled(0)
                    for u in range(units):
                        if u + 1 < units:
                            scaled(u + 1)
                        third(u)
                        if u:
                            combine(u - 1)
                    combine(units - 1)

            @block.gpsimd
            def _(pool):
                pool.memset(acc[:], 0.0).then_inc(s_a, 2)
                with pool.Fori(0, EXPERTS // 2) as i:
                    for u in range(units):
                        c = u % NCH
                        pool.wait_ge(s_t, i * units + u + 3)
                        pool.wait_ge(s_a, i * units + u + 2)
                        part = acc[:, c * CH:(c + 1) * CH]
                        pool.tensor_tensor(part, part, prod[:, u % 2], ALU.add).then_inc(s_a, 1)


def shared_expert(nc, t, sem, name, src, acc, d):
    s_w = sem(f"{name}_shared_weights_loaded")
    s_u1, s_u2 = sem(f"{name}_shared_up1"), sem(f"{name}_shared_up2")
    s_si, s_m = sem(f"{name}_shared_silu"), sem(f"{name}_shared_product")
    s_y, s_a = sem(f"{name}_shared_down"), sem(f"{name}_shared_added")
    with ExitStack() as ctx:
        def sb(n, s, dt=F32):
            return ctx.enter_context(nc.sbuf_tensor(f"{name}_{n}", s, dt))
        w = sb("shared_w", [P, 6, P])
        silu, m = sb("shared_silu", [P, 2, 2, CH]), sb("shared_m", [P, 2, 2, CH])
        u1 = [t.PS[:, 2 * k:2 * k + 2, :] for k in range(2)]
        u2 = t.PS[:, 4:6, :]
        y = [t.PS[:, 6 + k, :] for k in range(2)]
        with nc.Block() as block:
            @block.sync
            def _(sp):
                sp.dma_start(w[:], d["L1_shared"]).then_inc(s_w, 16)

            @block.tensor
            def _(pe):
                def down(c):
                    pe.wait_ge(s_m, c + 1)
                    if c >= 2:
                        pe.wait_ge(s_a, c - 1)
                    for j in range(2):
                        mm = pe.matmul(y[c % 2], w[:, 4 + j, :], m[:, c % 2, j, :], start=(j == 0), stop=(j == 1))
                    mm.then_inc(s_y, 1)

                pe.wait_ge(s_w, 16)
                for c in range(NCH):
                    x = src[:, c * CH:(c + 1) * CH]
                    if c >= 2:
                        pe.wait_ge(s_si, c - 1)
                    for j in range(2):
                        mm = pe.matmul(u1[c % 2][:, j, :], w[:, j, :], x, start=True, stop=True)
                    mm.then_inc(s_u1, 1)
                    if c >= 1:
                        down(c - 1)
                    for j in range(2):
                        mm = pe.matmul(u2[:, j, :], w[:, 2 + j, :], x, start=True, stop=True)
                    mm.then_inc(s_u2, 1)
                down(NCH - 1)

            @block.scalar
            def _(act):
                for c in range(NCH):
                    act.wait_ge(s_u1, c + 1)
                    if c >= 2:
                        act.wait_ge(s_m, c - 1)
                    act.activation(silu[:, c % 2], u1[c % 2], ACT.Silu).then_inc(s_si, 1)

            @block.vector
            def _(dve):
                def add(c):
                    dve.wait_ge(s_y, c + 1)
                    part = acc[:, c * CH:(c + 1) * CH]
                    dve.tensor_tensor(part, y[c % 2], part, ALU.add).then_inc(s_a, 1)
                for c in range(NCH):
                    dve.wait_ge(s_u2, c + 1)
                    dve.wait_ge(s_si, c + 1)
                    if c >= 2:
                        dve.wait_ge(s_y, c - 1)
                    dve.tensor_tensor(m[:, c % 2], u2, silu[:, c % 2], ALU.mult).then_inc(s_m, 1)
                    if c:
                        add(c - 1)
                add(NCH - 1)


def ffn1(nc, t, sem, d):
    with ExitStack() as ctx:
        router, _ = open_gates(nc, t, sem, "f1", d, ctx, d["L1_router"],
                               norm=lambda load: norm_transpose(nc, t, sem, "f1", 1, SHIFT_B, SCALE_B, load))
        route(nc, t, sem, "f1", t.HT, router, None, SOFTMAX_TOP2)
        glu_experts(nc, t, sem, "f1", t.HT, t.YT, d["L1_w"], d["L1_b"])
        shared_expert(nc, t, sem, "f1", t.HT, t.YT, d)
        gate_in_place(nc, t, sem, "f1", 1, GATE_B)


ROTATIONS = 3
SQUARINGS = 16
TAYLOR = [1.0, 1.0, 1 / 2, 1 / 6, 1 / 24, 1 / 120, 1 / 720, 1 / 5040, 1 / 40320, 1 / 362880]
THETA = 0.5


def matrix_exponentials(nc, t, sem, d):
    s_in, s_v, s_mm = sem("expm_loaded"), sem("expm_vector_steps"), sem("expm_products")
    s_sq = sem("expm_squarings")
    FIRST = 22
    shape = [P, 2 * ROTATIONS, P]
    with ExitStack() as ctx:
        def sb(n, s, dt=F32):
            return ctx.enter_context(nc.sbuf_tensor(f"expm_{n}", s, dt))
        b1, b2, b3, r = sb("b1", shape), sb("b2", shape), sb("b3", shape), sb("r", shape)
        a, q = sb("a", shape), sb("q", shape)
        diag = sb("diag", [P, 3, P])
        ones = sb("ones", [P, P])
        norm, thr, flag = sb("norm", [P, ROTATIONS]), sb("thr", [P, 1]), sb("flag", [P, ROTATIONS])
        inv = sb("inv", [P, ROTATIONS])
        table = sb("table", [P, 2, SQUARINGS + 1])
        cand = sb("cand", [P, ROTATIONS, SQUARINGS + 1])
        ps = t.PS[:, 0:2, :].rearrange("p b f -> p (b f)")[:, 0:2 * ROTATIONS * P].rearrange("p (m f) -> p m f", f=P)
        with nc.Block() as block:
            @block.sync
            def _(sp):
                sp.dma_start(b1[:], d["L2_gens"]).then_inc(s_in, 16)
                sp.dma_start(table[:], d["expm_table"]).then_inc(s_in, 16)

            @block.tensor
            def _(pe):
                def products(left, right):
                    for m in range(ROTATIONS):
                        pe.matmul(ps[:, 2 * m, :], left[:, 2 * m + 1, :], right[:, 2 * m, :], start=True, stop=True)
                        last = pe.matmul(ps[:, 2 * m + 1, :], left[:, 2 * m, :], right[:, 2 * m + 1, :],
                                         start=True, stop=True)
                    last.then_inc(s_mm, 1)

                pe.wait_ge(s_v, 2)
                for m in range(ROTATIONS):
                    last = pe.matmul(ps[:, m, :], ones[:], a[:, 2 * m, :], start=True, stop=True)
                last.then_inc(s_mm, 1)
                pe.wait_ge(s_v, 7)
                products(b1, b1)
                pe.wait_ge(s_v, 8)
                products(b2, b1)
                pe.wait_ge(s_v, 15)
                products(b3, r)
                pe.wait_ge(s_v, 18)
                products(b3, r)
                with pe.Fori(0, SQUARINGS) as k:
                    pe.wait_ge(s_v, 3 * k + FIRST)
                    products(r, r)
                pe.wait_ge(s_v, 3 * SQUARINGS + FIRST)
                pe.matmul(ps[:, 0, :], r[:, 3, :], r[:, 4, :], start=True, stop=True).then_inc(s_mm, 1)
                pe.wait_ge(s_v, 3 * SQUARINGS + FIRST + 1)
                pe.matmul(ps[:, 1, :], r[:, 1, :], a[:, 0, :], start=True, stop=True).then_inc(s_mm, 1)

            @block.vector
            def _(dve):
                v = 0

                def done(instruction):
                    nonlocal v
                    v += 1
                    instruction.then_inc(s_v, 1)
                    dve.wait_ge(s_v, v)

                dve.wait_ge(s_in, 32)
                done(dve.memset(ones[:], 1.0))
                done(dve.scalar_tensor_tensor(a[:], b1[:], -1.0, b1[:], ALU.mult, ALU.max))
                dve.wait_ge(s_mm, 1)
                done(dve.tensor_reduce(norm[:], ps[:, 0:ROTATIONS, :], AX, ALU.max))
                done(dve.tensor_tensor(cand[:], table[:, 0:1, :].broadcast_to(cand.shape),
                                       bcast(norm[:], SQUARINGS + 1), ALU.is_ge))
                done(dve.tensor_tensor(cand[:], cand[:], table[:, 1:2, :].broadcast_to(cand.shape), ALU.mult))
                done(dve.tensor_reduce(inv[:], cand[:], AX, ALU.max))
                done(dve.tensor_tensor(b1[:].rearrange("p (m k) f -> p m (k f)", k=2),
                                       b1[:].rearrange("p (m k) f -> p m (k f)", k=2), bcast(inv[:], 2 * P), ALU.mult))
                dve.wait_ge(s_mm, 2)
                done(dve.tensor_copy(b2[:], ps))
                dve.wait_ge(s_mm, 3)
                done(dve.tensor_copy(b3[:], ps))
                for j in range(3):
                    done(dve.tensor_scalar(diag[:, j], t.ident[:], TAYLOR[3 * j], None, ALU.mult))

                def bracket(j, out):
                    done(dve.scalar_tensor_tensor(out[:], b1[:], TAYLOR[3 * j + 1],
                                                  diag[:, j:j + 1].broadcast_to(shape), ALU.mult, ALU.add))
                    done(dve.scalar_tensor_tensor(out[:], b2[:], TAYLOR[3 * j + 2], out[:], ALU.mult, ALU.add))

                bracket(2, a)
                done(dve.scalar_tensor_tensor(r[:], b3[:], TAYLOR[9], a[:], ALU.mult, ALU.add))
                bracket(1, q)
                dve.wait_ge(s_mm, 4)
                done(dve.tensor_tensor(r[:], ps, q[:], ALU.add))
                bracket(0, q)
                dve.wait_ge(s_mm, 5)
                done(dve.tensor_tensor(r[:], ps, q[:], ALU.add))
                done(dve.memset(thr[:], THETA))
                assert v == FIRST
                with dve.Fori(0, SQUARINGS) as k:
                    dve.tensor_scalar(flag[:], norm[:], thr[:, 0:1], None, ALU.is_gt).then_inc(s_v, 1)
                    dve.wait_ge(s_v, 3 * k + FIRST + 1)
                    dve.tensor_scalar(thr[:], thr[:], 2.0, None, ALU.mult).then_inc(s_v, 1)
                    dve.wait_ge(s_mm, k + 6)
                    dve.wait_ge(s_v, 3 * k + FIRST + 2)
                    dve.sem_inc(s_sq, 1)
                    dve.copy_predicated(r[:].rearrange("p (m k) f -> p m (k f)", k=2),
                                        bcast(flag[:].bitcast(I32), 2 * P),
                                        ps.rearrange("p (m k) f -> p m (k f)", k=2)).then_inc(s_v, 1)
                    dve.wait_ge(s_v, 3 * k + FIRST + 3)
                v += 3 * SQUARINGS
                dve.wait_ge(s_mm, SQUARINGS + 6)
                done(dve.tensor_copy(a[:, 0], ps[:, 0, :]))
                dve.wait_ge(s_mm, SQUARINGS + 7)
                done(dve.tensor_copy(t.C[:], ps[:, 1, :]))


def norm_features(nc, t, sem, xn, d):
    s_in, s_one = sem("n2_loaded"), sem("n2_ones_ready")
    s_mean, s_c, s_sq = sem("n2_means"), sem("n2_centred"), sem("n2_squares")
    s_var, s_v, s_sd, s_xn = sem("n2_variances"), sem("n2_vector_steps"), sem("n2_deviation"), sem("n2_normalised")
    with ExitStack() as ctx:
        def sb(n, s, dt=F32):
            return ctx.enter_context(nc.sbuf_tensor(f"n2_{n}", s, dt))
        affine, ones = sb("affine", [P, 2]), sb("ones", [P, P])
        sq, var, sd, r, tmp = (sb(n, [P, 2, CH]) for n in ("sq", "var", "sd", "r", "tmp"))
        mean_ps = [t.PS[:, k, :] for k in range(2)]
        var_ps = [t.PS[:, 2 + k, :] for k in range(2)]
        with nc.Block() as block:
            @block.sync
            def _(sp):
                sp.dma_start(affine[:], d["L2_norm"]).then_inc(s_in, 16)

            @block.tensor
            def _(pe):
                def variances(c):
                    pe.wait_ge(s_sq, c + 1)
                    if c >= 2:
                        pe.wait_ge(s_v, 6 * (c - 2) + 1)
                    pe.matmul(var_ps[c % 2], ones[:], sq[:, c % 2], start=True, stop=True).then_inc(s_var, 1)
                pe.wait_ge(s_one, 1)
                for c in range(NCH):
                    if c >= 2:
                        pe.wait_ge(s_c, c - 1)
                    pe.matmul(mean_ps[c % 2], ones[:], t.HT[:, c * CH:(c + 1) * CH],
                              start=True, stop=True).then_inc(s_mean, 1)
                    if c:
                        variances(c - 1)
                variances(NCH - 1)

            @block.scalar
            def _(act):
                def roots(c):
                    act.wait_ge(s_v, 6 * c + 1)
                    act.activation(sd[:, c % 2], var[:, c % 2], ACT.Sqrt).then_inc(s_sd, 1)
                for c in range(NCH):
                    act.wait_ge(s_c, c + 1)
                    if c >= 2:
                        act.wait_ge(s_var, c - 1)
                    act.activation(sq[:, c % 2], xn[:, c * CH:(c + 1) * CH], ACT.Square).then_inc(s_sq, 1)
                    if c:
                        roots(c - 1)
                roots(NCH - 1)

            @block.vector
            def _(dve):
                v = 0

                def done(instruction):
                    nonlocal v
                    v += 1
                    instruction.then_inc(s_v, 1)
                    dve.wait_ge(s_v, v)

                def centre(c):
                    dve.wait_ge(s_mean, c + 1)
                    part = slice(c * CH, (c + 1) * CH)
                    dve.tensor_tensor(xn[:, part], t.HT[:, part], mean_ps[c % 2], ALU.subtract).then_inc(s_c, 1)

                dve.memset(ones[:], 1.0 / P).then_inc(s_one, 1)
                dve.wait_ge(s_in, 16)
                centre(0)
                for c in range(NCH):
                    if c + 1 < NCH:
                        centre(c + 1)
                    k = c % 2
                    part = xn[:, c * CH:(c + 1) * CH]
                    dve.wait_ge(s_var, c + 1)
                    done(dve.tensor_scalar(var[:, k], var_ps[k], EPS, None, ALU.add))
                    dve.wait_ge(s_sd, c + 1)
                    done(dve.reciprocal(r[:, k], sd[:, k]))
                    done(dve.tensor_tensor(tmp[:, k], r[:, k], r[:, k], ALU.mult))
                    done(dve.tensor_tensor(tmp[:, k], tmp[:, k], var[:, k], ALU.mult))
                    done(dve.tensor_scalar(tmp[:, k], tmp[:, k], -0.5, 1.5, ALU.mult, ALU.add))
                    done(dve.tensor_tensor(r[:, k], r[:, k], tmp[:, k], ALU.mult))
                    dve.tensor_tensor(part, part, r[:, k], ALU.mult).then_inc(s_xn, 1)
                    dve.wait_ge(s_xn, 2 * c + 1)
                    dve.tensor_scalar(part, part, affine[:, 0:1], affine[:, 1:2], ALU.mult, ALU.add).then_inc(s_xn, 1)
                    dve.wait_ge(s_xn, 2 * c + 2)


def mix(nc, t, sem, xn, d):
    s_in, s_w = sem("m2_loaded"), sem("m2_mix_weights_ready")
    s_p, s_a, s_m = sem("m2_products"), sem("m2_abel_ready"), sem("m2_moe_ready")
    s_z, s_g, s_v = sem("m2_mix_logits"), sem("m2_mix_gates"), sem("m2_vector_steps")
    with ExitStack() as ctx:
        def sb(n, s, dt=F32):
            return ctx.enter_context(nc.sbuf_tensor(f"m2_{n}", s, dt))
        wa, ba, mw, mb = sb("abel_w", [P, P]), sb("abel_b", [P, 1]), sb("mix_w", [P, 2]), sb("mix_b", [P, 1])
        mwb = sb("mix_wb", [P, 2, P])
        abel, moe, g = sb("abel", [P, 2, CH]), sb("moe", [P, 2, CH]), sb("g", [P, 2, CH])
        with nc.Block() as block:
            @block.sync
            def _(sp):
                sp.dma_start(wa[:], d["L2_abel_w"]).then_inc(s_in, 16)
                sp.dma_start(ba[:], d["L2_abel_b"]).then_inc(s_in, 16)
                sp.dma_start(mw[:], d["L2_mix_w"]).then_inc(s_in, 16)
                sp.dma_start(mb[:], d["L2_mix_b"].broadcast_to((P, 1))).then_inc(s_in, 16)

            @block.tensor
            def _(pe):
                def logits(c):
                    pe.wait_ge(s_a, c + 1)
                    pe.wait_ge(s_m, c + 1)
                    if c >= 2:
                        pe.wait_ge(s_g, c - 1)
                    pe.matmul(t.PS[:, 4 + c % 2, :], mwb[:, 0], abel[:, c % 2], start=True, stop=False)
                    pe.matmul(t.PS[:, 4 + c % 2, :], mwb[:, 1], moe[:, c % 2], start=False, stop=True).then_inc(s_z, 1)
                pe.wait_ge(s_in, 64)
                pe.wait_ge(s_w, 1)
                for c in range(NCH):
                    part = slice(c * CH, (c + 1) * CH)
                    if c >= 2:
                        pe.wait_ge(s_a, c - 1)
                        pe.wait_ge(s_m, c - 1)
                    pe.matmul(t.PS[:, c % 2, :], wa[:], xn[:, part], start=True, stop=True)
                    pe.matmul(t.PS[:, 2 + c % 2, :], t.C[:], t.YT[:, part], start=True, stop=True).then_inc(s_p, 1)
                    if c:
                        logits(c - 1)
                logits(NCH - 1)

            @block.scalar
            def _(act):
                def gates(c):
                    act.wait_ge(s_z, c + 1)
                    if c >= 2:
                        act.wait_ge(s_v, 3 * (c - 1))
                    act.activation(g[:, c % 2], t.PS[:, 4 + c % 2, :], ACT.Sigmoid, bias=mb[:, 0:1]).then_inc(s_g, 1)
                act.wait_ge(s_in, 64)
                for c in range(NCH):
                    act.wait_ge(s_p, c + 1)
                    if c >= 2:
                        act.wait_ge(s_v, 3 * (c - 1))
                    act.activation(abel[:, c % 2], t.PS[:, c % 2, :], ACT.Gelu, bias=ba[:, 0:1]).then_inc(s_a, 1)
                    if c:
                        gates(c - 1)
                gates(NCH - 1)

            @block.vector
            def _(dve):
                dve.wait_ge(s_in, 64)
                dve.tensor_copy(mwb[:], bcast(mw[:], P)).then_inc(s_w, 1)

                def moes(c):
                    dve.wait_ge(s_p, c + 1)
                    dve.tensor_copy(moe[:, c % 2], t.PS[:, 2 + c % 2, :]).then_inc(s_m, 1)
                moes(0)
                for c in range(NCH):
                    k = c % 2
                    part = slice(c * CH, (c + 1) * CH)
                    dve.wait_ge(s_z, c + 1)
                    dve.wait_ge(s_m, c + 1)
                    dve.wait_ge(s_a, c + 1)
                    dve.tensor_tensor(moe[:, k], moe[:, k], abel[:, k], ALU.subtract).then_inc(s_v, 1)
                    if c + 1 < NCH:
                        if c:
                            dve.wait_ge(s_v, 3 * c)
                        moes(c + 1)
                    dve.wait_ge(s_g, c + 1)
                    dve.wait_ge(s_v, 3 * c + 1)
                    dve.tensor_tensor(moe[:, k], moe[:, k], g[:, k], ALU.mult)
                    dve.tensor_tensor(abel[:, k], abel[:, k], t.HT[:, part], ALU.add).then_inc(s_v, 1)
                    dve.wait_ge(s_v, 3 * c + 2)
                    dve.tensor_tensor(t.YT[:, part], moe[:, k], abel[:, k], ALU.add).then_inc(s_v, 1)


def ffn2(nc, t, sem, d):
    with ExitStack() as ctx:
        xn = ctx.enter_context(nc.sbuf_tensor("f2_xn", [P, TOK], F32))
        t.C = ctx.enter_context(nc.sbuf_tensor("expm_C", [P, P], F32))
        norm_transpose(nc, t, sem, "f2", 2, SHIFT_B, SCALE_B)
        matrix_exponentials(nc, t, sem, d)
        norm_features(nc, t, sem, xn, d)
        router, bias = open_gates(nc, t, sem, "f2", d, ctx, d["L2_router"], d["L2_router_b"])
        route(nc, t, sem, "f2", xn, router, bias, TOP2_SOFTMAX)
        experts(nc, t, sem, "f2", xn, t.YT, 2 * P, d["L2_w1"], d["L2_w2"], d["L2_b1"], d["L2_b2"], ACT.Gelu, 0)
        mix(nc, t, sem, xn, d)
        gate_in_place(nc, t, sem, "f2", 2, GATE_B)


HEADS = 16
HD = P // HEADS


def attention3(nc, t, sem, d):
    Q, K, V, W, R = 0, P, 2 * P, 3 * P, 3 * P + HEADS
    COLS = 3 * P + 2 * HEADS
    s_in, s_p, s_qkv = sem("a3_loaded"), sem("a3_projected"), sem("a3_biased")
    s_v, s_act, s_s = sem("a3_vector_steps"), sem("a3_scalar_steps"), sem("a3_scores")
    s_sv, s_o = sem("a3_weighted_values"), sem("a3_heads_out")
    s_tr, s_ot, s_y, s_yt = sem("a3_transposed"), sem("a3_transposes_copied"), sem("a3_output"), sem("a3_gated")
    with ExitStack() as ctx:
        def sb(n, s, dt=F32):
            return ctx.enter_context(nc.sbuf_tensor(f"a3_{n}", s, dt))
        w, bias = sb("w", [P, COLS]), sb("bias", [P, COLS])
        wo, bo = sb("wo", [P, P]), sb("bo", [P, 1])
        qkv = sb("qkv", [P, NT, COLS])
        prod = sb("prod", [P, BATCH, TILES * P])
        sv = sb("sv", [P, BATCH, TILES * P])
        score = sb("score", [P, NT * HEADS])
        o = sb("o", [P, 2, TILES * P])
        n2, nrm, rec = (sb(n, [P, NT, 2 * HEADS]) for n in ("n2", "nrm", "rec"))
        ot = t.HT

        def load(sp):
            sp.dma_start(w[:], d["L3_qkvwr"]).then_inc(s_in, 16)
            sp.dma_start(bias[:], d["L3_qkvwr_b"].broadcast_to((P, COLS))).then_inc(s_in, 16)
            sp.dma_start(wo[:], d["L3_wo"]).then_inc(s_in, 16)
            sp.dma_start(bo[:], d["L3_bo"]).then_inc(s_in, 16)

        norm_transpose(nc, t, sem, "a3", 3, SHIFT_A, SCALE_A, load)
        with nc.Block() as block:
            @block.tensor
            def _(pe):
                pe.wait_ge(s_in, 64)
                for i in range(NT):
                    if i >= 4:
                        pe.wait_ge(s_qkv, i - 3)
                    pe.matmul(t.PS[:, i % 4, 0:COLS], t.HT[:, i * P:(i + 1) * P], w[:], start=True,
                              stop=True).then_inc(s_p, 1)
                for s in range(BATCH):
                    pe.wait_ge(s_o, s + 1)
                    for half in range(2):
                        c = 2 * s + half
                        if c >= 2:
                            pe.wait_ge(s_ot, c - 1)
                        for i in range(4):
                            j = 4 * half + i
                            mm = pe.transpose(t.PS[:, 4 + half, i * P:(i + 1) * P],
                                              o[:, s % 2, j * P:(j + 1) * P], t.ident[:])
                        mm.then_inc(s_tr, 1)
                    for half in range(2):
                        c = 2 * s + half
                        pe.wait_ge(s_ot, c + 1)
                        if c >= 2:
                            pe.wait_ge(s_yt, c - 1)
                        pe.matmul(t.PS[:, 6 + half, :], wo[:], ot[:, c * CH:(c + 1) * CH], start=True,
                                  stop=True).then_inc(s_y, 1)

            @block.scalar
            def _(act):
                act.wait_ge(s_v, 1)
                act.activation(nrm[:], n2[:], ACT.Sqrt).then_inc(s_act, 1)
                act.activation(qkv[:, :, W:COLS], qkv[:, :, W:COLS], ACT.Sigmoid).then_inc(s_act, 1)
                for c in range(NCH):
                    act.wait_ge(s_tr, c + 1)
                    act.activation(ot[:, c * CH:(c + 1) * CH], t.PS[:, 4 + c % 2, :], ACT.Copy).then_inc(s_ot, 1)

            @block.vector
            def _(dve):
                v = 0

                def done(instruction):
                    nonlocal v
                    v += 1
                    instruction.then_inc(s_v, 1)
                    dve.wait_ge(s_v, v)

                def by_head(ap):
                    return ap.rearrange("p i (h e) -> p i h e", e=HD)

                dve.wait_ge(s_in, 64)
                for i in range(NT):
                    dve.wait_ge(s_p, i + 1)
                    dve.tensor_tensor(qkv[:, i], t.PS[:, i % 4, 0:COLS], bias[:], ALU.add).then_inc(s_qkv, 1)
                dve.wait_ge(s_qkv, NT)
                for half, buf in ((0, prod), (1, sv)):
                    tl = slice(half * NT // 2, (half + 1) * NT // 2)
                    sq = buf[:].rearrange("p a b -> p (a b)").rearrange("p (i f) -> p i f", f=2 * P)
                    dve.tensor_tensor(sq, qkv[:, tl, Q:V], qkv[:, tl, Q:V], ALU.mult).then_inc(s_s, 1)
                for half, buf in ((0, prod), (1, sv)):
                    tl = slice(half * NT // 2, (half + 1) * NT // 2)
                    sq = buf[:].rearrange("p a b -> p (a b)").rearrange("p (i f) -> p i f", f=2 * P)
                    dve.wait_ge(s_s, half + 1)
                    last = dve.tensor_reduce(n2[:, tl], by_head(sq), AX, ALU.add)
                done(last)
                dve.wait_ge(s_act, 2)
                done(dve.tensor_scalar(nrm[:], nrm[:], 1e-18, None, ALU.max))
                done(dve.reciprocal(rec[:], nrm[:]))
                done(dve.tensor_tensor(rec[:], rec[:], n2[:], ALU.mult))
                done(dve.tensor_tensor(nrm[:], nrm[:], rec[:], ALU.add))
                done(dve.tensor_scalar(nrm[:], nrm[:], 0.5, 1e-12, ALU.mult, ALU.max))
                done(dve.reciprocal(rec[:], nrm[:]))
                done(dve.tensor_tensor(by_head(qkv[:, :, Q:V]), by_head(qkv[:, :, Q:V]),
                                       rec[:].unsqueeze(3).broadcast_to((P, NT, 2 * HEADS, HD)), ALU.mult))
                done(dve.tensor_tensor(by_head(qkv[:, :, V:W]), by_head(qkv[:, :, V:W]),
                                       qkv[:, :, W:R].unsqueeze(3).broadcast_to((P, NT, HEADS, HD)), ALU.mult))

                def finish(s):
                    dve.wait_ge(s_sv, s + 1)
                    if s >= 2:
                        dve.wait_ge(s_tr, 2 * (s - 1))
                    out = o[:, s % 2]
                    done(dve.tensor_reduce(out, sv[:].rearrange("p s f -> p f s"), AX, ALU.add))
                    tl = slice(s * TILES, (s + 1) * TILES)
                    out4 = out.rearrange("p (i h e) -> p i h e", h=HEADS, e=HD)
                    dve.tensor_tensor(out4, out4, qkv[:, tl, R:COLS].unsqueeze(3).broadcast_to((P, TILES, HEADS, HD)),
                                      ALU.mult).then_inc(s_o, 1)

                def gated(c):
                    dve.wait_ge(s_y, c + 1)
                    dve.tensor_scalar(t.YT[:, c * CH:(c + 1) * CH], t.PS[:, 6 + c % 2, :], bo[:, 0:1],
                                      t.MOD[:, 3, GATE_A, c // 2:c // 2 + 1], ALU.add, ALU.mult).then_inc(s_yt, 1)

                for s in range(BATCH):
                    q = qkv[:, s * TILES:(s + 1) * TILES, Q:K]
                    for s2 in range(BATCH):
                        last = dve.tensor_tensor(prod[:, s2].rearrange("p (i f) -> p i f", f=P), q,
                                                 qkv[:, s2 * TILES:(s2 + 1) * TILES, K:V], ALU.mult)
                    done(last)
                    if s:
                        dve.wait_ge(s_sv, s)
                    dve.tensor_reduce(score[:], prod[:].rearrange("p s (h e) -> p (s h) e", e=HD), AX,
                                      ALU.add).then_inc(s_s, 1)
                    dve.wait_ge(s_s, s + 3)
                    if s:
                        finish(s - 1)
                    dve.sem_inc(s_v, 1)
                    v += 1
                    if s >= 2:
                        gated(2 * (s - 2))
                        gated(2 * (s - 2) + 1)
                finish(BATCH - 1)
                for c in range(2 * (BATCH - 2), NCH):
                    gated(c)

            @block.gpsimd
            def _(pool):
                FIRST, EACH = 9, 3
                for s in range(BATCH):
                    pool.wait_ge(s_s, s + 3)
                    pool.wait_ge(s_v, FIRST + 2 + EACH * s)
                    pool.tensor_tensor(sv[:].rearrange("p s (h e) -> p (s h) e", e=HD),
                                       qkv[:, :, V:W].rearrange("p i (h e) -> p i h e", e=HD),
                                       bcast(score[:], HD), ALU.mult).then_inc(s_sv, 1)


def first_query(c, kt):
    return max(0, (kt - c + 1) // 2)


def causal_attention(nc, t, sem, name, layer, w_d, rows, rope_d, bias_d, down_d, scale):
    J, GROUPS = 4, HEADS // 4
    NS = 8 * J
    KEYS = [7, 8]
    groups = []
    for c in range(2):
        for kt in range(KEYS[c]):
            many = {4: 1, 3: 1, 2: 2, 1: 4}[4 - first_query(c, kt)]
            groups += [(c, kt, tuple(range(j, j + many))) for j in range(0, J, many)]
    NG, NG0 = len(groups), sum(g[0] == 0 for g in groups)
    assert NG % 2 == 0
    KT = sum(KEYS)
    s_in, s_cst, s_cv = sem(f"{name}_loaded"), sem(f"{name}_values_cleared"), sem(f"{name}_constants")
    s_pj, s_pv0 = sem(f"{name}_projected"), sem(f"{name}_values_projected")
    s_a, s_d = sem(f"{name}_batch_scalar_steps"), sem(f"{name}_batch_vector_steps")
    s_vt = sem(f"{name}_values_transposed")
    s_pool = sem(f"{name}_group_staged")
    s_st = sem(f"{name}_stacked")
    s_qa, s_qs = sem(f"{name}_stacks_copied"), sem(f"{name}_q_rows_placed")
    s_S = sem(f"{name}_scores")
    s_mx = sem(f"{name}_maxima")
    s_P = sem(f"{name}_probabilities")
    s_T = sem(f"{name}_blocks_transposed")
    s_ea = sem(f"{name}_blocks_copied")
    s_pv = sem(f"{name}_values_weighted")
    s_at = sem(f"{name}_heads_copied")
    s_att = sem(f"{name}_heads_transposed")
    s_rc, s_o = sem(f"{name}_sums_inverted"), sem(f"{name}_heads_normalised")
    s_ot, s_oc, s_y = sem(f"{name}_rows_transposed"), sem(f"{name}_rows_copied"), sem(f"{name}_output")
    s_yt = sem(f"{name}_gated")
    s_bt = sem(f"{name}_batch_stages")
    s_r, s_g = sem(f"{name}_rotary_products"), sem(f"{name}_gelu")
    biased = bias_d is not None
    with ExitStack() as ctx:
        def sb(n, s, dt=F32):
            return ctx.enter_context(nc.sbuf_tensor(f"{name}_{n}", s, dt))
        w, rope = sb("w", [P, 6, P]), sb("rope", [P, 2, SEQ])
        bias, wd, bd = sb("bias", [P, 6]), sb("wd", [P, 32]), sb("bd", [32, 1])
        high, low = sb("high", [P, 2, SEQ], F32R), sb("low", [P, 2, SEQ], F32R)
        rot = t.YT[:, 3 * SEQ:4 * SEQ].rearrange("p (r f) -> p r f", r=2)
        q_stack = t.YT[:, 3 * SEQ:4 * SEQ].bitcast(F32R)
        picks = sb("picks", [P, GROUPS, 4, P], BF16)
        vb = sb("vb", [P, TILES, P])
        pick = sb("pick", [P, 4, P], F32R)
        mask = sb("mask", [P, P], BF16)
        ident_bf = sb("identb", [P, P], BF16)
        vst = sb("vst", [P, TILES, J, 32])
        qs, ks = sb("qs", [P, J, SEQ], F32R), sb("ks", [P, SEQ], F32R)
        probs = [[sb(f"p{c}_{i}", [P, J, (2 * i + c + 1) * P]) for i in range(4)] for c in range(2)]
        pick_f = probs[1][3][:, 0:2, :].rearrange("p a f -> p (a f)")
        mask_f = probs[1][3][:, 2, 0:P]
        nmax = sb("nmax", [P, NS])
        blk = sb("blk", [P, 2 * J * CH])
        turned = blk[:, 2 * CH:4 * CH].rearrange("p (r f) -> p r f", r=2)
        latent = blk[0:32, 4 * CH:6 * CH]
        oT = blk[:, 0:2 * CH]
        at, rec = sb("at", [P, CH]), sb("rec", [P, 4, J])
        o = sb("o", [P, TILES, P])
        vT = o[:].rearrange("p i f -> p (i f)")
        score_ps = [t.PS[:, 2 * k:2 * k + 2, :].rearrange("p b f -> p (b f)") for k in range(2)]
        blk_ps = [t.PS[:, 4 + k, :] for k in range(2)]
        at_ps, tr_ps = t.PS[:, 6, :], t.PS[:, 7, :]

        def tile_of(c, n):
            return n % 4, 2 * (n % 4) + c, n // 4

        def place(x):
            if x == KT - 1:
                return J * CH + J * CH // 2, x - 3
            if x < KEYS[0]:
                return J * CH * (x % 2), (x - 2 if x > 1 else -3 if x == 0 else -1)
            return J * CH * (x % 2), x - 2

        def half(c, tiles_behind):
            out = []
            for n, (u, kt, heads) in enumerate(groups):
                if u == c:
                    out.append(("T", n))
                    for _ in range(tiles_behind(n - NG0 * c)):
                        out.append(("S", sum(w == "S" for w, _ in out)))
                    if heads[-1] == J - 1:
                        x = kt + (KEYS[0] if c else 0)
                        if kt or c:
                            out.append(("W", x - 1))
                        if c and kt == 0:
                            out.append(("N", 0))
                        if c and kt == 1:
                            out.append(("H", 0))
            return out
        first = half(0, lambda n: 1 if n < 16 else 0)
        second = half(1, lambda n: 0 if n < 10 else (2 if n % 3 == 0 else 1))
        second += [("S", n) for n in range(sum(w == "S" for w, _ in second), 4 * J)]
        second += [("W", KT - 1), ("H", 1)]

        NA = 8 if biased else 6
        def load(sp):
            sp.dma_start(w[:], w_d).then_inc(s_in, 16)
            sp.dma_start(rope[:], rope_d).then_inc(s_in, 16)
            sp.dma_start(pick_f, rows["picks"]).then_inc(s_in, 16)
            sp.dma_start(mask_f, rows["causal"]).then_inc(s_in, 16)
            if biased:
                sp.dma_start(bias[:], bias_d[0]).then_inc(s_in, 16)
                sp.dma_start(wd[:], down_d).then_inc(s_in, 16)
                sp.dma_start(bd[:], bias_d[1]).then_inc(s_in, 16)

        norm_transpose(nc, t, sem, name, layer, SHIFT_A, SCALE_A, load)
        with nc.Block() as block:
            @block.sync
            def _(sp):
                with sp.Fori(0, BATCH * GROUPS) as it:
                    sp.wait_ge(s_qa, it * 2 + 2)
                    for j in range(J):
                        sp.dma_start(qs[32 * j:32 * j + 32, j].bitcast(F32), q_stack[32 * j:32 * j + 32].bitcast(F32)).then_inc(s_qs, 16)
            LOADED = 16 * (7 if biased else 4)

            @block.gpsimd
            def _(pool):
                pool.memset(vst[:], 0.0).then_inc(s_cst, 1)
                pool.wait_ge(s_cst, 1)
                pool.memset(vst[:, :, :, HD:HD + 1], 1.0).then_inc(s_cst, 1)
                pool.wait_ge(s_cst, 2)
                pool.wait_ge(s_cv, 4)
                with pool.Fori(0, BATCH) as b:
                    with pool.Fori(0, GROUPS) as g:
                        it = b * GROUPS + g
                        pool.wait_ge(s_st, it + 1)
                        pool.tensor_copy(pick[:], picks[:, bass.ds(g, 1)].rearrange("p a k f -> p (a k) f")).then_inc(s_pool, 1)
                        pool.wait_ge(s_vt, b + 1)
                        pool.wait_ge(s_pv, it * KT + 3)
                        pool.tensor_copy(vst[:, :, :, 0:HD],
                                         vb[:, :, bass.ds(g * J * HD, J * HD)].rearrange("p i (j e) -> p i j e", e=HD)).then_inc(s_pool, 1)

            @block.tensor
            def _(pe):
                pe.wait_ge(s_in, LOADED)
                pe.wait_ge(s_cst, 2)
                pe.wait_ge(s_cv, 4)
                with pe.Fori(0, BATCH) as b:
                    for c in range(2):
                        x = t.HT[:, bass.ds(b * SEQ + c * CH, CH)]
                        pe.wait_ge(s_P, b * GROUPS * NS + 2)
                        for r in range(2):
                            if c:
                                pe.wait_ge(s_d, b * 8 + 2 * r + 2)
                            for k in range(2):
                                mm = pe.matmul(t.PS[:, 2 * r + k, :], w[:, 2 * r + k, :], x, start=True, stop=True)
                            mm.then_inc(s_pj, 1)
                    for c in range(2):
                        x = t.HT[:, bass.ds(b * SEQ + c * CH, CH)]
                        pe.wait_ge(s_o, b * GROUPS * 2 + 1)
                        if biased:
                            pe.sem_inc(s_bt, 1)
                            pe.matmul(t.PS[0:32, 6 + c, :], wd[:], x, start=True, stop=True).then_inc(s_pv0, 1)
                        else:
                            pe.matmul(t.PS[:, 6 + c, :], w[:, 4, :], x, start=True, stop=True).then_inc(s_pv0, 1)
                    if biased:
                        for c in range(2):
                            pe.wait_ge(s_a, b * NA + 5 + c)
                            pe.matmul(t.PS[:, 6 + c, :], w[0:32, 4, :], latent[:, c * CH:(c + 1) * CH],
                                      start=True, stop=True).then_inc(s_pv0, 1)
                    for c in range(2):
                        pe.wait_ge(s_a, b * NA + NA - 1 + c)
                        for i in range(4):
                            mm = pe.transpose(t.PS[:, 6 + c, i * P:(i + 1) * P],
                                              vT[:, (4 * c + i) * P:(4 * c + i + 1) * P], t.ident[:])
                        mm.then_inc(s_ot, 1)
                    pe.wait_ge(s_d, b * 8 + 8)
                    pe.sem_inc(s_bt, 1)

                    def stacks(it):
                        pe.wait_ge(s_pool, it * 2 + 1)
                        pe.wait_ge(s_P, it * NS + 2)
                        for r in range(2):
                            for c in range(2):
                                pe.matmul(t.PS[:, 2 * r + c, :], pick[:, 2 * r, :], high[:, r, c * CH:(c + 1) * CH],
                                          start=True, stop=False)
                                mm = pe.matmul(t.PS[:, 2 * r + c, :], pick[:, 2 * r + 1, :],
                                               low[:, r, c * CH:(c + 1) * CH], start=False, stop=True)
                        mm.then_inc(s_st, 1)

                    def score(it, c, n):
                        i, q, j = tile_of(c, n)
                        N = 4 * J * c + n
                        width = (q + 1) * P
                        if N == 0:
                            pe.wait_ge(s_qs, it * 64 + 64)
                        pe.wait_ge(s_P, it * NS + N + 1)
                        for k0 in range(0, width, CH):
                            k1 = min(width, k0 + CH)
                            pe.matmul(score_ps[N % 2][:, k0:k1], qs[:, j, q * P:(q + 1) * P], ks[:, k0:k1],
                                      start=True, stop=(k1 < width))
                        pe.matmul(score_ps[N % 2][:, q * P:width], ident_bf[:], mask[:], start=False,
                                  stop=True).then_inc(s_S, 1)

                    def transpose_group(it, n):
                        c, kt, heads = groups[n]
                        if kt == 0:
                            pe.wait_ge(s_P, it * NS + 4 * J * c + 4 * heads[-1] + 6)
                        pe.wait_ge(s_ea, it * NG + n + 1)
                        i0 = first_query(c, kt)
                        for m, j in enumerate(heads):
                            for i in range(i0, 4):
                                at_col = (m * (4 - i0) + i - i0) * P
                                mm = pe.transpose(blk_ps[n % 2][:, at_col:at_col + P],
                                                  probs[c][i][:, j, kt * P:(kt + 1) * P], t.ident[:])
                        mm.then_inc(s_T, 1)

                    def weigh(it, x):
                        c = int(x >= KEYS[0])
                        kt = x - KEYS[0] * c
                        mine = [n for n, g in enumerate(groups) if g[0] == c and g[1] == kt]
                        if kt == 0:
                            pe.wait_ge(s_at, it * 2 + c + 1)
                            if c == 0:
                                pe.wait_ge(s_pool, it * 2 + 2)
                        pe.wait_ge(s_ea, it * NG + mine[-1] + 3)
                        i0 = first_query(c, kt)
                        base, size = place(x)[0], (4 - i0) * P
                        for j in range(J):
                            mm = pe.matmul(at_ps[32 * j:32 * j + 32, i0 * P:], vst[:, kt, j, :],
                                           blk[:, base + j * size:base + (j + 1) * size],
                                           start=(kt == 0), stop=(kt == KEYS[c] - 1), skip_group_check=True)
                        mm.then_inc(s_pv, 1)

                    def heads_back(it, c):
                        pe.wait_ge(s_at, it * 2 + c + 2)
                        pe.wait_ge(s_o, it * 2 + c + 1)
                        for i in range(4):
                            mm = pe.transpose(tr_ps[:, i * P:(i + 1) * P], at[:, i * P:(i + 1) * P], t.ident[:])
                        mm.then_inc(s_att, 1)

                    def step(it, more):
                        for c, order in enumerate((first, second)):
                            for what, n in order:
                                if what == "T":
                                    transpose_group(it, n)
                                elif what == "W":
                                    weigh(it, n)
                                elif what == "H":
                                    heads_back(it, n)
                                elif what == "S" and c == 0:
                                    score(it, 1, n)
                                elif what == "S" and more:
                                    score(it + 1, 0, n)
                                elif what == "N" and more:
                                    stacks(it + 1)

                    stacks(b * GROUPS)
                    for n in range(4 * J):
                        score(b * GROUPS, 0, n)
                    with pe.Fori(0, GROUPS - 1) as g:
                        step(b * GROUPS + g, True)
                    step(b * GROUPS + GROUPS - 1, False)
                    for c in range(2):
                        pe.wait_ge(s_o, (b + 1) * GROUPS * 2 + 1)
                        for i in range(4):
                            mm = pe.transpose(t.PS[:, 6 + c, i * P:(i + 1) * P], o[:, 4 * c + i, :], t.ident[:])
                        mm.then_inc(s_ot, 1)
                    for c in range(2):
                        pe.wait_ge(s_oc, b * 2 + c + 1)
                        pe.matmul(t.PS[:, 6 + c, :], w[:, 5, :], oT[:, c * CH:(c + 1) * CH], start=True,
                                  stop=True).then_inc(s_y, 1)
                    pe.wait_ge(s_yt, b * 2 + 2)

            @block.scalar
            def _(act):
                act.sem_inc(s_ea, 2)
                act.wait_ge(s_in, LOADED)
                with act.Fori(0, BATCH) as b:
                    for c in range(2):
                        part = slice(c * CH, (c + 1) * CH)
                        for r in range(2):
                            if biased:
                                act.wait_ge(s_d, b * 8 + 4 * c + 2 * r + 1)
                                act.activation(rot[:, r], rot[:, r], ACT.Gelu).then_inc(s_g, 1)
                                act.wait_ge(s_g, b * 4 + 2 * c + r + 1)
                            else:
                                act.wait_ge(s_d, b * 8 + 4 * c + 2 * r + 1)
                            act.activation(high[:, r, part], rot[:, r], ACT.Copy, scale=scale if r == 0 else 1.0).then_inc(s_a, 1)
                    if biased:
                        for c in range(2):
                            act.wait_ge(s_pv0, b * 4 + c + 1)
                            act.activation(latent[:, c * CH:(c + 1) * CH], t.PS[0:32, 6 + c, :], ACT.Gelu,
                                           bias=bd[:, 0:1]).then_inc(s_a, 1)
                    for c in range(2):
                        act.wait_ge(s_pv0, b * (4 if biased else 2) + (2 if biased else 0) + c + 1)
                        a = act.activation(vT[:, c * CH:(c + 1) * CH], t.PS[:, 6 + c, :],
                                           ACT.Identity if biased else ACT.Copy,
                                           **({"bias": bias[:, 4:5]} if biased else {}))
                        a.then_inc(s_a, 1)

                    def stacks(it):
                        act.wait_ge(s_st, it + 2)
                        act.wait_ge(s_S, it * NS + 1)
                        act.activation(q_stack, score_ps[0], ACT.Copy).then_inc(s_qa, 1)
                        act.activation(ks[:], score_ps[1], ACT.Copy).then_inc(s_qa, 1)

                    def exponentiate(it, c, n):
                        i, q, j = tile_of(c, n)
                        N = 4 * J * c + n
                        if n == 0:
                            act.wait_ge(s_T, it * NG + (NG if c else NG0))
                        act.wait_ge(s_mx, it * NS + N + 1)
                        act.activation(probs[c][i][:, j, :], score_ps[N % 2][:, 0:(q + 1) * P], ACT.Exp,
                                       bias=nmax[:, N:N + 1]).then_inc(s_P, 1)

                    def copy_group(it, n):
                        c, kt, heads = groups[n]
                        x = kt + KEYS[0] * c
                        base, before = place(x)
                        size = (4 - first_query(c, kt)) * P
                        act.wait_ge(s_T, NG + it * NG + n + 1)
                        act.wait_ge(s_pv, it * KT + before + 4)
                        act.activation(blk[:, base + heads[0] * size:base + (heads[-1] + 1) * size],
                                       blk_ps[n % 2][:, 0:len(heads) * size], ACT.Copy).then_inc(s_ea, 1)

                    def step(it, more):
                        for c, order in enumerate((first, second)):
                            for what, n in order:
                                if what == "T":
                                    copy_group(it, n)
                                elif what == "S" and c == 0:
                                    exponentiate(it, 1, n)
                                elif what == "S" and more:
                                    exponentiate(it + 1, 0, n)
                                elif what == "N" and more:
                                    stacks(it + 1)

                    stacks(b * GROUPS)
                    for n in range(4 * J):
                        exponentiate(b * GROUPS, 0, n)
                    with act.Fori(0, GROUPS - 1) as g:
                        step(b * GROUPS + g, True)
                    step(b * GROUPS + GROUPS - 1, False)
                    for c in range(2):
                        act.wait_ge(s_ot, b * 4 + 2 + c + 1)
                        act.activation(oT[:, c * CH:(c + 1) * CH], t.PS[:, 6 + c, :], ACT.Copy).then_inc(s_oc, 1)

            @block.vector
            def _(dve):
                dve.sem_inc(s_st, 1)
                dve.sem_inc(s_S, 1)
                dve.sem_inc(s_P, 2)
                dve.sem_inc(s_T, NG)
                dve.sem_inc(s_pv, 3)
                dve.sem_inc(s_at, 1)
                dve.sem_inc(s_o, 1)
                dve.wait_ge(s_in, LOADED)
                dve.tensor_copy(picks[:].rearrange("p g k f -> p (g k f)"), pick_f).then_inc(s_cv, 1)
                dve.memset(qs[:].bitcast(F32), 0.0).then_inc(s_cv, 1)
                dve.tensor_copy(mask[:], mask_f).then_inc(s_cv, 1)
                dve.tensor_copy(ident_bf[:], t.ident[:]).then_inc(s_cv, 1)
                dve.wait_ge(s_cv, 4)
                with dve.Fori(0, BATCH) as b:
                    for c in range(2):
                        part = slice(c * CH, (c + 1) * CH)
                        for r in range(2):
                            x_ps, r_ps = t.PS[:, 2 * r, :], t.PS[:, 2 * r + 1, :]
                            dve.wait_ge(s_pj, b * 4 + 2 * c + r + 1)
                            if c:
                                dve.wait_ge(s_a, b * NA + r + 1)
                            if biased:
                                dve.scalar_tensor_tensor(rot[:, r], x_ps, bias[:, 2 * r:2 * r + 1], rope[:, 0, part],
                                                         ALU.add, ALU.mult).then_inc(s_r, 1)
                                dve.scalar_tensor_tensor(turned[:, r], r_ps, bias[:, 2 * r + 1:2 * r + 2], rope[:, 1, part],
                                                         ALU.add, ALU.mult).then_inc(s_r, 1)
                            else:
                                dve.tensor_tensor(rot[:, r], x_ps, rope[:, 0, part], ALU.mult).then_inc(s_r, 1)
                                dve.tensor_tensor(turned[:, r], r_ps, rope[:, 1, part], ALU.mult).then_inc(s_r, 1)
                            dve.wait_ge(s_r, b * 8 + 4 * c + 2 * r + 2)
                            dve.tensor_tensor(rot[:, r], rot[:, r], turned[:, r], ALU.add).then_inc(s_d, 1)
                            dve.wait_ge(s_d, b * 8 + 4 * c + 2 * r + 1)
                            dve.wait_ge(s_a, b * NA + 2 * c + r + 1)
                            dve.scalar_tensor_tensor(low[:, r, part], rot[:, r], scale if r == 0 else 1.0,
                                                     high[:, r, part].bitcast(F32), ALU.mult, ALU.subtract).then_inc(s_d, 1)
                    for c in range(2):
                        dve.wait_ge(s_ot, b * 4 + c + 1)
                        last = dve.tensor_copy(vb[:, 4 * c:4 * c + 4, :], t.PS[:, 6 + c, :].rearrange("p (i f) -> p i f", f=P))
                    last.then_inc(s_vt, 1)

                    def maximum(it, c, n):
                        i, q, j = tile_of(c, n)
                        N = 4 * J * c + n
                        dve.wait_ge(s_S, 1 + it * NS + N + 1)
                        dve.tensor_reduce(nmax[:, N:N + 1], score_ps[N % 2][:, 0:(q + 1) * P], AX, ALU.max,
                                          negate=True).then_inc(s_mx, 1)

                    def heads_out(it, c):
                        dve.wait_ge(s_pv, 3 + it * KT + (KT if c else KEYS[0]))
                        dve.tensor_copy(at[:], at_ps).then_inc(s_at, 1)

                    def normalise(it, g, c):
                        dve.wait_ge(s_att, it * 2 + c + 1)
                        got = tr_ps.rearrange("p (i j e) -> p i j e", j=J, e=32)
                        dve.reciprocal(rec[:], got[:, :, :, HD]).then_inc(s_rc, 1)
                        dve.wait_ge(s_rc, it * 2 + c + 1)
                        mine = o[:].rearrange("p (i c) f -> p i c f", c=2)[:, :, c]
                        dst = mine[:, :, bass.ds(g * J * HD, J * HD)].rearrange("p i (j e) -> p i j e", e=HD)
                        dve.tensor_tensor(dst, got[:, :, :, 0:HD], rec[:].unsqueeze(3).broadcast_to((P, 4, J, HD)),
                                          ALU.mult).then_inc(s_o, 1)

                    def step(it, g, more):
                        for c, order in enumerate((first, second)):
                            for what, n in order:
                                if what == "W" and n == KEYS[0] - 1:
                                    heads_out(it, 0)
                                elif what == "H" and n == 0:
                                    normalise(it, g, 0)
                                elif what == "H":
                                    heads_out(it, 1)
                                    normalise(it, g, 1)
                                elif what == "S" and c == 0:
                                    maximum(it, 1, n)
                                elif what == "S" and more:
                                    maximum(it + 1, 0, n)

                    for n in range(4 * J):
                        maximum(b * GROUPS, 0, n)
                    with dve.Fori(0, GROUPS - 1) as g:
                        step(b * GROUPS + g, g, True)
                    step(b * GROUPS + GROUPS - 1, GROUPS - 1, False)
                    for c in range(2):
                        dve.wait_ge(s_y, b * 2 + c + 1)
                        y = t.YT[:, bass.ds(b * SEQ + c * CH, CH)]
                        dve.tensor_scalar(y, t.PS[:, 6 + c, :], bias[:, 5:6] if biased else 0.0,
                                          t.MOD[:, layer, GATE_A, bass.ds(b, 1)], ALU.add, ALU.mult).then_inc(s_yt, 1)


def attention1(nc, t, sem, d):
    causal_attention(nc, t, sem, "a1", 1, d["L1_attn_w"], d, d["L1_rope"], None, None, HD ** -0.5)


def attention2(nc, t, sem, d):
    causal_attention(nc, t, sem, "a2", 2, d["L2_attn_w"], d, d["L2_rope"], (d["L2_attn_b"], d["L2_latent_b"]),
                     d["L2_down"], HD ** -0.5)


def attention0(nc, t, sem, d):
    WIDE = 64
    PAIRS = HEADS // 2
    NS, NB = 8, 16
    scale = WIDE ** -0.5
    s_wq, s_wv, s_wo = sem("a0_qk_weights_loaded"), sem("a0_v_weights_loaded"), sem("a0_output_weights_loaded")
    s_one = sem("a0_ones_ready")
    s_hb = sem("a0_batch_inputs_copied")
    s_pj, s_hi, s_lo = sem("a0_projected"), sem("a0_high_parts"), sem("a0_low_parts")
    s_vp, s_vd, s_va = sem("a0_values"), sem("a0_values_by_vector"), sem("a0_values_by_scalar")
    s_S, s_mx = sem("a0_scores"), sem("a0_maxima")
    s_P = sem("a0_probabilities")
    s_T = sem("a0_blocks_transposed")
    s_ed, s_ea = sem("a0_blocks_by_vector"), sem("a0_blocks_by_scalar")
    s_pv = sem("a0_values_weighted")
    s_rc = sem("a0_sums_inverted")
    s_dg = sem("a0_diagonals")
    s_rb = sem("a0_inverse_sums_spread")
    s_sp = sem("a0_inverse_sums_copied")
    s_at = sem("a0_heads_normalised")
    s_ge, s_y, s_yt, s_z = sem("a0_gelu"), sem("a0_output"), sem("a0_gated"), sem("a0_input_added")
    with ExitStack() as ctx:
        def sb(n, s, dt=F32):
            return ctx.enter_context(nc.sbuf_tensor(f"a0_{n}", s, dt))
        wqk, wv, wo = sb("wqk", [P, 2, 2, P]), sb("wv", [P, P]), sb("wo", [P, PAIRS, P])
        ones = sb("ones", [P, WIDE])
        hb = sb("hb", [P, SEQ])
        qs, kh, kl = (sb(n, [P, 2, SEQ], F32R) for n in ("qs", "kh", "kl"))
        vst = sb("vst", [P, TILES, P])
        probs = [sb(f"p{c}", [P, 2, 4, SEQ]) for c in range(2)]
        nmax, sums, rec = sb("nmax", [P, 2 * NS]), sb("sums", [P, 2, NS]), sb("rec", [P, 2, NS])
        diag = sb("diag", [P, NS, P])
        spread = sb("spread", [P, CH])
        blk = sb("blk", [P, 4, CH])
        at = sb("at", [P, PAIRS, SEQ])
        score_ps = [t.PS[:, 2 * k:2 * k + 2, :].rearrange("p b f -> p (b f)") for k in range(2)]
        blk_ps = [t.PS[:, 4 + k, :] for k in range(2)]
        at_ps, rec_ps = t.PS[:, 6, :], t.PS[:, 7, :]

        first, second = [], []
        for kt in range(TILES):
            weighed = [("W", kt - 1)] if kt else []
            first += [("B", kt), ("S", kt)] + weighed
            second += [("B", kt)] + ([("P", kt)] + weighed if kt < 4 else
                                     [("S", 2 * kt - 8)] + weighed + [("S", 2 * kt - 7)])
        first.append(("W", TILES - 1))
        second.append(("W", TILES - 1))
        orders = [first, second]

        def load(sp):
            sp.dma_start(wqk[:], d["L0_qk"][0]).then_inc(s_wq, 16)
            sp.dma_start(wv[:], d["L0_v"][0]).then_inc(s_wv, 16)
            sp.dma_start(wo[:], d["L0_post"]).then_inc(s_wo, 16)

        norm_transpose(nc, t, sem, "a0", 0, SHIFT_A, SCALE_A, load)
        with nc.Block() as block:
            @block.sync
            def _(sp):
                with sp.Fori(0, BATCH) as b:
                    with sp.Fori(0, PAIRS) as p:
                        it = b * PAIRS + p
                        sp.wait_ge(s_pj, it * 4 + 4)
                        sp.dma_start(wqk[:].rearrange("p h r f -> p (h r f)"),
                                     d["L0_qk"][bass.ds(p + 1, 1)].rearrange("a p h r f -> p (a h r f)")).then_inc(s_wq, 16)
                        sp.wait_ge(s_vp, it * 2 + 3)
                        sp.dma_start(wv[:], d["L0_v"][bass.ds(p + 1, 1)].rearrange("a p f -> p (a f)")).then_inc(s_wv, 16)
                sp.wait_ge(s_wv, 16 * (BATCH * PAIRS + 1))

            @block.gpsimd
            def _(pool):
                pool.sem_inc(s_rb, 1)
                pool.sem_inc(s_dg, 2)
                pool.memset(ones[:], 1.0).then_inc(s_one, 1)
                with pool.Fori(0, BATCH * PAIRS) as it:
                    for c in range(2):
                        pool.wait_ge(s_rc, it * 2 + c + 2)
                        pool.wait_ge(s_rb, it * 2 + c + 1)
                        pool.tensor_tensor(diag[:], t.ident[:].unsqueeze(1).broadcast_to((P, NS, P)),
                                           bcast(rec[:, c], P), ALU.mult).then_inc(s_dg, 1)

            @block.tensor
            def _(pe):
                def project(J, k, offset):
                    if k == 0:
                        pe.wait_ge(s_wq, 16 * (J + 1))
                    h, r = k // 2, k % 2
                    if k < 2:
                        pe.wait_ge(s_P, J * 2 * NS + 2)
                    else:
                        pe.wait_ge(s_lo, J * 4 + k - 1)
                    for c in range(2):
                        mm = pe.matmul(score_ps[r][:, c * CH:(c + 1) * CH], wqk[:, h, r, :],
                                       t.HT[:, bass.ds(offset + c * CH, CH)], start=True, stop=True)
                    mm.then_inc(s_pj, 1)

                def score(J, c, n):
                    j, i = n // 4, n % 4
                    if c == 0 and n < 2:
                        pe.wait_ge(s_lo, J * 4 + n + 3)
                    pe.wait_ge(s_P, J * 2 * NS + NS * c + n + 1)
                    q = qs[:, j, (4 * c + i) * P:(4 * c + i + 1) * P]
                    for part in (kh, kl):
                        for g in range(2):
                            mm = pe.matmul(score_ps[n % 2][:, g * CH:(g + 1) * CH], q, part[:, j, g * CH:(g + 1) * CH],
                                           start=(part is kh), stop=(part is kl))
                    mm.then_inc(s_S, 1)

                def weigh(it, c, kt):
                    U = 2 * it + c
                    if kt == 0:
                        pe.wait_ge(s_at, U + 1)
                        pe.wait_ge(s_vd, it + 1)
                        pe.wait_ge(s_va, it + 1)
                    pe.wait_ge(s_ed, U * TILES + kt + 2)
                    pe.wait_ge(s_ea, U * TILES + kt + 2)
                    for j in range(2):
                        pe.matmul(at_ps[WIDE * j:WIDE * (j + 1), :], vst[:, kt, WIDE * j:WIDE * (j + 1)],
                                  blk[:, 2 * (kt % 2) + j, :], start=(kt == 0), stop=(kt == TILES - 1),
                                  skip_group_check=True).then_inc(s_pv, 1)

                def blocks(it, c, kt):
                    U = 2 * it + c
                    if kt == 0:
                        pe.wait_ge(s_P, U * NS + NS + 2)
                    for j in range(2):
                        if kt == 0 and c == 0:
                            pe.wait_ge((s_vd, s_va)[j], it + 1)
                        pe.wait_ge((s_ed, s_ea)[j], U * TILES + kt + 1)
                        for i in range(4):
                            mm = pe.transpose(blk_ps[j][:, i * P:(i + 1) * P],
                                              probs[c][:, j, i, kt * P:(kt + 1) * P], t.ident[:])
                        mm.then_inc(s_T, 1)

                pe.wait_ge(s_one, 1)
                for k in range(4):
                    project(0, k, 0)
                for n in range(NS):
                    score(0, 0, n)
                with pe.Fori(0, BATCH) as b:
                    with pe.Fori(0, PAIRS) as p:
                        it = b * PAIRS + p
                        after = ((it + 1) // PAIRS) % BATCH * SEQ
                        pe.wait_ge(s_hb, b + 1)
                        pe.wait_ge(s_wv, 16 * (it + 1))
                        for g in range(2):
                            pe.wait_ge((s_ed, s_ea)[g], it * 2 * TILES + 1)
                            for i in range(4):
                                mm = pe.matmul(blk_ps[g][:, i * P:(i + 1) * P], hb[:, (4 * g + i) * P:(4 * g + i + 1) * P],
                                               wv[:], start=True, stop=True)
                            mm.then_inc(s_vp, 1)
                        for c in range(2):
                            for what, n in orders[c]:
                                if what == "W":
                                    weigh(it, c, n)
                                elif what == "B":
                                    blocks(it, c, n)
                                elif what == "P":
                                    project(it + 1, n, after)
                                elif c == 0:
                                    score(it, 1, n)
                                else:
                                    score(it + 1, 0, n)
                            pe.wait_ge(s_dg, it * 2 + c + 3)
                            for j in range(2):
                                mm = pe.matmul(rec_ps[WIDE * j:WIDE * (j + 1), :], ones[:],
                                               diag[:, 4 * j:4 * j + 4, :].rearrange("p i f -> p (i f)"),
                                               start=True, stop=True, skip_group_check=True)
                            mm.then_inc(s_rb, 1)
                    pe.wait_ge(s_wo, 16)
                    for k in range(PAIRS):
                        pe.wait_ge(s_ge, b * PAIRS + k + 1)
                        for c in range(2):
                            mm = pe.matmul(t.PS[:, 6 + c, :], wo[:, k, :], at[:, k, c * CH:(c + 1) * CH],
                                           start=(k == 0), stop=(k == PAIRS - 1))
                    mm.then_inc(s_y, 1)
                    pe.wait_ge(s_z, b * 2 + 2)

            @block.scalar
            def _(act):
                def split_high(J, k):
                    h, r = k // 2, k % 2
                    act.wait_ge(s_pj, J * 4 + k + 1)
                    dst = (qs, kh)[r][:, h, :]
                    act.activation(dst, score_ps[r], ACT.Copy, scale=scale if r == 0 else 1.0).then_inc(s_hi, 1)

                def exponentiate(J, c, n):
                    j, i = n // 4, n % 4
                    act.wait_ge(s_mx, J * 2 * NS + NS * c + n + 1)
                    act.activation(probs[c][:, j, i, :], score_ps[n % 2], ACT.Exp,
                                   bias=nmax[:, NS * c + n:NS * c + n + 1],
                                   accum_out=sums[:, c, n:n + 1]).then_inc(s_P, 1)

                act.sem_inc(s_P, 2)
                act.sem_inc(s_ea, 1)
                for k in range(4):
                    split_high(0, k)
                for n in range(NS):
                    exponentiate(0, 0, n)
                with act.Fori(0, BATCH) as b:
                    act.wait_ge(s_vp, b * PAIRS * 2 + 1)
                    act.activation(hb[:], t.HT[:, bass.ds(b * SEQ, SEQ)], ACT.Copy).then_inc(s_hb, 1)
                    with act.Fori(0, PAIRS) as p:
                        it = b * PAIRS + p
                        act.wait_ge(s_vp, it * 2 + 3)
                        act.wait_ge(s_pv, it * 2 * NB + 4)
                        act.activation(vst[:, 4:8, :].rearrange("p i f -> p (i f)"), blk_ps[1], ACT.Copy).then_inc(s_va, 1)
                        for c in range(2):
                            U = 2 * it + c
                            for what, n in orders[c]:
                                if what == "B":
                                    m = U * NB + 2 * n + 1
                                    act.wait_ge(s_T, m + 1 + 2 * NB)
                                    act.wait_ge(s_pv, m + 1)
                                    act.activation(blk[:, 2 * (n % 2) + 1, :], blk_ps[1], ACT.Copy).then_inc(s_ea, 1)
                                elif what == "P":
                                    split_high(it + 1, n)
                                elif what == "S" and c == 0:
                                    if n == 0:
                                        act.wait_ge(s_T, it * 2 * NB + 2 * NB)
                                        act.wait_ge(s_rc, it * 2 + 1)
                                    exponentiate(it, 1, n)
                                elif what == "S":
                                    if n == 0:
                                        act.wait_ge(s_T, it * 2 * NB + 3 * NB)
                                        act.wait_ge(s_rc, it * 2 + 2)
                                    exponentiate(it + 1, 0, n)
                    act.wait_ge(s_at, (b + 1) * PAIRS * 2 + 1)
                    for k in range(PAIRS):
                        act.activation(at[:, k, :], at[:, k, :], ACT.Gelu).then_inc(s_ge, 1)

            @block.vector
            def _(dve):
                def split_low(J, k):
                    h, r = k // 2, k % 2
                    dve.wait_ge(s_hi, J * 4 + k + 1)
                    if r == 0:
                        rows = qs[WIDE:, h, :]
                        dve.scalar_tensor_tensor(rows, score_ps[0][WIDE:], scale, rows.bitcast(F32), ALU.mult,
                                                 ALU.subtract).then_inc(s_lo, 1)
                    else:
                        dve.tensor_tensor(kl[:, h, :], score_ps[1], kh[:, h, :].bitcast(F32),
                                          ALU.subtract).then_inc(s_lo, 1)

                def maximum(J, c, n):
                    dve.wait_ge(s_S, J * 2 * NS + NS * c + n + 1)
                    dve.tensor_reduce(nmax[:, NS * c + n:NS * c + n + 1], score_ps[n % 2], AX, ALU.max,
                                      negate=True).then_inc(s_mx, 1)

                def invert_sums(it, c):
                    U = 2 * it + c
                    dve.wait_ge(s_P, U * NS + NS + 2)
                    dve.wait_ge(s_dg, U + 1)
                    dve.reciprocal(rec[:, c], sums[:, c]).then_inc(s_rc, 1)

                def normalise(it, p, c):
                    dve.wait_ge(s_rb, it * 2 + c + 2)
                    dve.wait_ge(s_at, it * 2 + c + 1)
                    dve.tensor_copy(spread[:], rec_ps).then_inc(s_sp, 1)
                    dve.wait_ge(s_sp, it * 2 + c + 1)
                    dve.tensor_tensor(at[:, bass.ds(p, 1), c * CH:(c + 1) * CH].rearrange("p a f -> p (a f)"),
                                      at_ps, spread[:], ALU.mult).then_inc(s_at, 1)

                dve.sem_inc(s_vp, 1)
                dve.sem_inc(s_T, 2 * NB)
                dve.sem_inc(s_ed, 1)
                dve.sem_inc(s_pv, 4)
                dve.sem_inc(s_rc, 1)
                dve.sem_inc(s_at, 1)
                for k in range(4):
                    split_low(0, k)
                for n in range(NS):
                    maximum(0, 0, n)
                with dve.Fori(0, BATCH) as b:
                    with dve.Fori(0, PAIRS) as p:
                        it = b * PAIRS + p
                        dve.wait_ge(s_vp, it * 2 + 2)
                        dve.wait_ge(s_pv, it * 2 * NB + 4)
                        dve.tensor_copy(vst[:, 0:4, :].rearrange("p i f -> p (i f)"), blk_ps[0]).then_inc(s_vd, 1)
                        for c in range(2):
                            U = 2 * it + c
                            for what, n in orders[c]:
                                if what == "B":
                                    m = U * NB + 2 * n
                                    dve.wait_ge(s_T, m + 1 + 2 * NB)
                                    dve.wait_ge(s_pv, m + 1)
                                    dve.tensor_copy(blk[:, 2 * (n % 2), :], blk_ps[0]).then_inc(s_ed, 1)
                                    if n == 0:
                                        if c == 1:
                                            normalise(it, p, 0)
                                        invert_sums(it, c)
                                elif what == "P":
                                    split_low(it + 1, n)
                                elif what == "S" and c == 0:
                                    maximum(it, 1, n)
                                elif what == "S":
                                    maximum(it + 1, 0, n)
                        normalise(it, p, 1)
                    dve.wait_ge(s_y, b + 1)
                    for c in range(2):
                        y = t.YT[:, bass.ds(b * SEQ + c * CH, CH)]
                        dve.tensor_tensor(y, t.PS[:, 6 + c, :], t.HT[:, bass.ds(b * SEQ + c * CH, CH)],
                                          ALU.add).then_inc(s_z, 1)
                    for c in range(2):
                        dve.wait_ge(s_z, b * 2 + c + 1)
                        y = t.YT[:, bass.ds(b * SEQ + c * CH, CH)]
                        dve.tensor_scalar(y, y, t.MOD[:, 0, GATE_A, bass.ds(b, 1)], None, ALU.mult).then_inc(s_yt, 1)


def program(nc, d, out):
    with ExitStack() as ctx:
        def sb(name, shape, dt=F32):
            return ctx.enter_context(nc.sbuf_tensor(name, shape, dt))

        in_use = []

        def sem(name):
            in_use.append(nc.alloc_semaphore(name))
            return in_use[-1]

        def clear_semaphores():
            nc.clear_and_free_semaphores(in_use)
            nc.all_engine_barrier()
            in_use.clear()

        t = Memory()
        t.first = True
        t.X, t.HT, t.YT = sb("X", [P, NT, P]), sb("HT", [P, TOK]), sb("YT", [P, TOK])
        t.MOD, t.iota8 = sb("MOD", [P, LAYERS, 6, BATCH]), sb("iota8", [P, EXPERTS])
        t.ident, t.ident_bf = sb("ident", [P, P]), sb("ident_bf", [P, P], BF16)
        t.PS = ctx.enter_context(nc.psum_tensor("PS", [P, 8, CH], F32))

        load_and_modulation(nc, t, sem, d)
        every = [attention0, ffn0, attention1, ffn1, attention2, ffn2, attention3, ffn3]
        for sublayer in every:
            sublayer(nc, t, sem, d)
            clear_semaphores()
        last_residual(nc, t, sem, out)


def layout(inputs):
    import numpy as np

    def a(name):
        return np.asarray(inputs[name])

    def c(x):
        return np.ascontiguousarray(x)

    out = {"L0_attn_X": c(a("L0_attn_X")),
           "c_T": c(np.concatenate([a(f"L{l}_c") for l in range(LAYERS)]).T)}
    for l in range(LAYERS):
        out[f"L{l}_wmod"] = c(a(f"L{l}_wmod"))
    out["ident"] = np.eye(P, dtype=np.float32)
    out["iota8"] = np.tile(np.arange(EXPERTS, dtype=np.float32), (P, 1))
    sel = np.zeros((P, 2 * EXPERTS, P), np.float32)
    for e in range(EXPERTS):
        for k in range(3):
            sel[k * EXPERTS + e, e] = 1.0
        sel[3 * EXPERTS + e, EXPERTS + e] = 1.0
    out["gate_rows"] = sel
    def heads(name):
        return a(name).reshape(P, 8, 2, 64).transpose(1, 0, 2, 3)
    wrap = np.arange(9) % 8
    qk = np.stack([heads("L0_attn_Wq"), heads("L0_attn_Wk")], 3)
    out["L0_qk"] = c(np.concatenate([qk, qk], 4)[wrap])
    out["L0_v"] = c(a("L0_attn_Wv").reshape(P, 8, P).transpose(1, 0, 2)[wrap])
    out["L0_post"] = c(a("L0_attn_Wpost").reshape(8, P, P).transpose(1, 0, 2))
    out["L0_router"] = c(a("L0_ffn_router_w").T)
    out["L0_w1"] = c(a("L0_ffn_w1"))
    out["L0_w2"] = c(a("L0_ffn_w2"))
    out["L1_router"] = c(a("L1_ffn_gate_w").T)
    out["L1_w"] = c(np.stack([a("L1_ffn_w1").transpose(0, 2, 1), a("L1_ffn_w3").transpose(0, 2, 1),
                              a("L1_ffn_w2").transpose(0, 2, 1)], 2))
    out["L1_b"] = c(np.stack([a("L1_ffn_b1"), a("L1_ffn_b3"), a("L1_ffn_b2")], 2))
    out["L1_shared"] = c(np.concatenate([a("L1_ffn_sw1").T.reshape(P, 2, P), a("L1_ffn_sw2").T.reshape(P, 2, P),
                                         a("L1_ffn_sw3").T.reshape(2, P, P).transpose(1, 0, 2)], 1))
    gens = a("L2_ffn_gens")
    out["L2_gens"] = c(np.stack([gens, gens.transpose(0, 2, 1)], 1).reshape(2 * ROTATIONS, P, P).transpose(1, 0, 2))
    table = np.stack([THETA * 2.0 ** np.arange(SQUARINGS + 1), 2.0 ** -np.arange(SQUARINGS + 1)])
    table[0, -1] = 3e38
    out["expm_table"] = c(np.broadcast_to(table.astype(np.float32), (P, 2, SQUARINGS + 1)))
    out["L2_norm"] = c(np.stack([a("L2_ffn_ln_gamma"), a("L2_ffn_ln_beta")], 1))
    out["L2_router"] = c(a("L2_ffn_moe_gate_w"))
    out["L2_router_b"] = c(a("L2_ffn_moe_gate_b"))[None]
    out["L2_w1"] = c(a("L2_ffn_ew1"))
    out["L2_b1"] = c(a("L2_ffn_eb1").reshape(EXPERTS, 2, P).transpose(0, 2, 1))
    out["L2_w2"] = c(a("L2_ffn_ew2"))
    out["L2_b2"] = c(a("L2_ffn_eb2"))[:, :, None]
    out["L2_abel_w"] = c(a("L2_ffn_abel_w"))
    out["L2_abel_b"] = c(a("L2_ffn_abel_b"))[:, None]
    out["L2_mix_w"] = c(a("L2_ffn_gc_w").reshape(2, P).T)
    out["L2_mix_b"] = c(a("L2_ffn_gc_b"))[None]
    out["causal"] = np.triu(np.full((P, P), -3e38, np.float32), 1)
    picks = np.zeros((P, HEADS // 4, 4, P), np.float32)
    terms = ([0, 1], [2, 3], [0, 2], [1, 3])
    for h in range(HEADS):
        for kind, places in enumerate(terms):
            for place in places:
                for e in range(HD):
                    picks[h * HD + e, h // 4, kind, 32 * (h % 4) + HD * place + e] = 1.0
    out["picks"] = picks.reshape(P, -1)
    f = np.arange(P)

    def rope(inverse_frequency, minus):
        angle = np.arange(SEQ, dtype=np.float32)[None, :] * inverse_frequency[:, None]
        return c(np.stack([np.cos(angle), np.where(minus[:, None], -np.sin(angle), np.sin(angle))], 1))

    one = np.float32(10000.0) ** (-np.arange(HD // 2, dtype=np.float32) * np.float32(2.0) / np.float32(HD))
    out["L1_rope"] = rope(one[(f % HD) // 2], f % 2 == 0)
    q, k = a("L1_attn_Wq").T, a("L1_attn_Wk").T
    out["L1_attn_w"] = c(np.stack([q, q[:, f ^ 1], k, k[:, f ^ 1], a("L1_attn_Wv").T, a("L1_attn_Wo").T], 1))
    two = np.float32(1.0) / np.float32(10000.0) ** (np.arange(0, P, 2, dtype=np.float32) / np.float32(P))
    out["L2_rope"] = rope(two[f % (P // 2)], f < P // 2)
    swap = (f + P // 2) % P
    q, k = a("L2_attn_wqr"), a("L2_attn_wkr")
    v = np.zeros((P, P), np.float32)
    v[0:32] = a("L2_attn_wv")
    out["L2_attn_w"] = c(np.stack([q, q[:, swap], k, k[:, swap], v, a("L2_attn_wo")], 1))
    qb, kb = a("L2_attn_bqr"), a("L2_attn_bkr")
    out["L2_attn_b"] = c(np.stack([qb, qb[swap], kb, kb[swap], a("L2_attn_bv"), a("L2_attn_bo")], 1))
    out["L2_down"] = c(a("L2_attn_wkv"))
    out["L2_latent_b"] = c(a("L2_attn_bkv"))[:, None]
    names = ("Wq", "Wk", "Wv", "Ww", "Wr")
    out["L3_qkvwr"] = c(np.concatenate([a(f"L3_attn_{n}_w").T for n in names], 1))
    out["L3_qkvwr_b"] = c(np.concatenate([a(f"L3_attn_{n}_b") for n in names]))[None]
    out["L3_wo"] = c(a("L3_attn_Wo_w").T)
    out["L3_bo"] = c(a("L3_attn_Wo_b"))[:, None]
    out["L3_router"] = c(a("L3_ffn_gate_w").T)
    out["L3_router_b"] = c(a("L3_ffn_gate_b"))[None]
    out["L3_w1"] = c(a("L3_ffn_w1").transpose(0, 2, 1))
    out["L3_b1"] = c(a("L3_ffn_b1").reshape(EXPERTS, 4, P).transpose(0, 2, 1))
    out["L3_w2"] = c(a("L3_ffn_w2").transpose(0, 2, 1))
    out["L3_b2"] = c(a("L3_ffn_b2"))[:, :, None]
    return out


def kernel(**inputs):
    import numpy as _np
    import concourse.bacc as _bacc
    from concourse.bass_utils import run_bass_kernel_spmd as _run

    arrays = {f"in_{k}": v for k, v in layout(inputs).items()}
    nc = _bacc.Bacc("TRN2", target_bir_lowering=False, num_devices=1)
    d = {k[3:]: nc.dram_tensor(k, v.shape, mybir.dt.from_np(v.dtype), kind="ExternalInput").ap()
         for k, v in arrays.items()}
    out = nc.dram_tensor("out", (BATCH, SEQ, P), F32, kind="ExternalOutput").ap()
    program(nc, d, out)
    r = _run(nc, [arrays], core_ids=[0])
    return _np.asarray(r.results[0]["out"])
```
